# Optimizing a Trainium2 kernel written in Bass

```python
import numpy as np
import jax
import jax.numpy as jnp

def _softmax(x, axis=-1):
    return jax.nn.softmax(x, axis=axis)

def _gelu(x):
    return jax.nn.gelu(x, approximate=True)

def _silu(x):
    return jax.nn.silu(x)

def _sigmoid(x):
    return jax.nn.sigmoid(x)

def _layernorm(x, axis=-1, eps=1e-05):
    m = jnp.mean(x, axis=axis, keepdims=True)
    v = jnp.var(x, axis=axis, keepdims=True)
    return (x - m) / jnp.sqrt(v + eps)

def _scatter_add(tgt, idx, src, axis=0):
    return tgt.at[idx].add(src)

def _segment_sum(src, seg, n):
    return jax.ops.segment_sum(src, seg, n)
kernel_name = 'mk_adj_ffn_d2_adj_r2_28273c'

def setup_inputs(seed: int=0):
    np.random.seed(seed)
    _w = jnp.asarray

    def _rec_inputs():
        import jax
        import jax.numpy as jnp
        _gk = jax.random.key(seed)
        x = -0.0002928 + 1 * jax.random.normal(jax.random.fold_in(_gk, 1), (3327, 256), jnp.float32)
        _w = (1.0 + jnp.arange(3327, dtype=jnp.float32)) ** (-0.5)
        _w = _w / _w.mean()
        _pij = jnp.clip(0.00961827 * _w[:, None] * _w[None, :], 0.0, 1.0)
        _a = jax.random.uniform(jax.random.fold_in(_gk, 2), (3327, 3327)) < _pij
        adj = _a.astype(jnp.int32)
        return (x, adj)
    x, adj = _rec_inputs()

    def _L0_gnn_setup():
        import jax, jax.numpy as jnp
        import numpy as np
        N, D_IN, D_OUT = (4096, 256, 256)
        key = jax.random.key(seed)
        ks = jax.random.split(key, 8)
        scale_in = 1.0 / np.sqrt(D_IN)
        scale_cat = 1.0 / np.sqrt(2 * D_OUT)
        return {'x': jax.random.normal(ks[0], (N, D_IN), dtype=jnp.float32), 'adj': jax.random.randint(ks[1], (N, N), 0, 2, dtype=jnp.int32), 'W_self': jax.random.uniform(ks[2], (D_IN, D_OUT), jnp.float32, -scale_in, scale_in), 'b_self': jax.random.uniform(ks[3], (D_OUT,), jnp.float32, -scale_in, scale_in), 'W_nb': jax.random.uniform(ks[4], (D_IN, D_OUT), jnp.float32, -scale_in, scale_in), 'b_nb': jax.random.uniform(ks[5], (D_OUT,), jnp.float32, -scale_in, scale_in), 'W_comb': jax.random.uniform(ks[6], (2 * D_OUT, D_OUT), jnp.float32, -scale_cat, scale_cat), 'b_comb': jax.random.uniform(ks[7], (D_OUT,), jnp.float32, -scale_cat, scale_cat)}
    _L0_gnn_all = _L0_gnn_setup()
    _L0_gnn_in = {k: v for k, v in _L0_gnn_all.items() if k in ('W_self', 'b_self', 'W_nb', 'b_nb', 'W_comb', 'b_comb')}
    del _L0_gnn_all

    def _L0_ffn_setup():
        import jax, jax.numpy as jnp
        import numpy as np
        TOP_K = 6
        CAP_FACTOR = 2.0
        key = jax.random.key(seed)
        ks = jax.random.split(key, 9)
        B, S, D, F, E, SH = (4, 1024, 256, 128, 64, 2)
        return {'x': jax.random.normal(ks[0], (B, S, D), jnp.float32), 'router_w': jax.random.normal(ks[1], (E, D), jnp.float32) * 0.02, 'bias': jnp.zeros((E,), jnp.float32), 'shared_w_gate': jax.random.normal(ks[2], (SH, F, D), jnp.float32) * 0.02, 'shared_w_up': jax.random.normal(ks[3], (SH, F, D), jnp.float32) * 0.02, 'shared_w_down': jax.random.normal(ks[4], (SH, D, F), jnp.float32) * 0.02, 'w_gate': jax.random.normal(ks[5], (E, F, D), jnp.float32) * 0.02, 'w_up': jax.random.normal(ks[6], (E, F, D), jnp.float32) * 0.02, 'w_down': jax.random.normal(ks[7], (E, D, F), jnp.float32) * 0.02}
    _L0_ffn_all = _L0_ffn_setup()
    _L0_ffn_in = {k: v for k, v in _L0_ffn_all.items() if k in ('router_w', 'bias', 'shared_w_gate', 'shared_w_up', 'shared_w_down', 'w_gate', 'w_up', 'w_down')}
    del _L0_ffn_all

    def _L1_gnn_setup():
        import jax, jax.numpy as jnp
        import numpy as np
        N = 4096
        IN_F = 256
        OUT_F = 256
        ALPHA = 0.2
        NEG_INF = -9000000000000000.0
        key = jax.random.key(seed)
        k1, k2, k3, k4, k5 = jax.random.split(key, 5)
        x = jax.random.normal(k1, (N, IN_F), dtype=jnp.float32)
        adj = jax.random.randint(k2, (N, N), 0, 2, dtype=jnp.int32)
        W = jax.random.normal(k3, (OUT_F, IN_F), dtype=jnp.float32) / np.sqrt(IN_F)
        a1 = jax.random.normal(k4, (OUT_F,), dtype=jnp.float32) / np.sqrt(2 * OUT_F)
        a2 = jax.random.normal(k5, (OUT_F,), dtype=jnp.float32) / np.sqrt(2 * OUT_F)
        return {'x': x, 'adj': adj, 'W': W, 'a1': a1, 'a2': a2}
    _L1_gnn_all = _L1_gnn_setup()
    _L1_gnn_in = {k: v for k, v in _L1_gnn_all.items() if k in ('W', 'a1', 'a2')}
    del _L1_gnn_all

    def _L1_ffn_setup():
        import jax, jax.numpy as jnp
        import numpy as np
        B, S, D = (8, 4096, 256)
        E, DFF = (16, 256)
        CAPACITY = 2
        key = jax.random.key(seed)
        ks = jax.random.split(key, 4)
        x = jax.random.normal(ks[0], (B, S, D), dtype=jnp.float32)
        gate_weight = jax.random.normal(ks[1], (D, E), dtype=jnp.float32) * 0.006
        w1 = jax.random.normal(ks[2], (E, D, DFF), dtype=jnp.float32) * 0.02
        b1 = jnp.zeros((E, DFF), dtype=jnp.float32)
        w2 = jax.random.normal(ks[3], (E, DFF, D), dtype=jnp.float32) * 0.02
        b2 = jnp.zeros((E, D), dtype=jnp.float32)
        return {'x': x, 'gate_weight': gate_weight, 'w1': w1, 'b1': b1, 'w2': w2, 'b2': b2}
    _L1_ffn_all = _L1_ffn_setup()
    _L1_ffn_in = {k: v for k, v in _L1_ffn_all.items() if k in ('gate_weight', 'w1', 'b1', 'w2', 'b2')}
    del _L1_ffn_all
    return {'x': x, 'adj': adj, 'L0_gnn_W_self': _L0_gnn_in['W_self'], 'L0_gnn_b_self': _L0_gnn_in['b_self'], 'L0_gnn_W_nb': _L0_gnn_in['W_nb'], 'L0_gnn_b_nb': _L0_gnn_in['b_nb'], 'L0_gnn_W_comb': _L0_gnn_in['W_comb'], 'L0_gnn_b_comb': _L0_gnn_in['b_comb'], 'L0_ffn_router_w': _L0_ffn_in['router_w'], 'L0_ffn_bias': _L0_ffn_in['bias'], 'L0_ffn_shared_w_gate': _L0_ffn_in['shared_w_gate'], 'L0_ffn_shared_w_up': _L0_ffn_in['shared_w_up'], 'L0_ffn_shared_w_down': _L0_ffn_in['shared_w_down'], 'L0_ffn_w_gate': _L0_ffn_in['w_gate'], 'L0_ffn_w_up': _L0_ffn_in['w_up'], 'L0_ffn_w_down': _L0_ffn_in['w_down'], 'L1_gnn_W': _L1_gnn_in['W'], 'L1_gnn_a1': _L1_gnn_in['a1'], 'L1_gnn_a2': _L1_gnn_in['a2'], 'L1_ffn_gate_weight': _L1_ffn_in['gate_weight'], 'L1_ffn_w1': _L1_ffn_in['w1'], 'L1_ffn_b1': _L1_ffn_in['b1'], 'L1_ffn_w2': _L1_ffn_in['w2'], 'L1_ffn_b2': _L1_ffn_in['b2']}

def reference(x, adj, L0_gnn_W_self, L0_gnn_b_self, L0_gnn_W_nb, L0_gnn_b_nb, L0_gnn_W_comb, L0_gnn_b_comb, L0_ffn_router_w, L0_ffn_bias, L0_ffn_shared_w_gate, L0_ffn_shared_w_up, L0_ffn_shared_w_down, L0_ffn_w_gate, L0_ffn_w_up, L0_ffn_w_down, L1_gnn_W, L1_gnn_a1, L1_gnn_a2, L1_ffn_gate_weight, L1_ffn_w1, L1_ffn_b1, L1_ffn_w2, L1_ffn_b2):
    import jax
    import jax.numpy as jnp

    def _L0_gnn_ref(x, adj, W_self, b_self, W_nb, b_nb, W_comb, b_comb):
        import jax, jax.numpy as jnp
        import numpy as np
        N, D_IN, D_OUT = (4096, 256, 256)
        mask = (adj > 0).astype(x.dtype)
        deg = jnp.sum(mask, axis=1, keepdims=True)
        agg = mask @ x / jnp.maximum(deg, 1.0)
        self_f = x @ W_self + b_self
        nb_f = agg @ W_nb + b_nb
        combined = jnp.concatenate([self_f, nb_f], axis=-1)
        out = combined @ W_comb + b_comb
        return jax.nn.relu(out)

    def _L0_ffn_ref(x, router_w, bias, shared_w_gate, shared_w_up, shared_w_down, w_gate, w_up, w_down):
        import jax, jax.numpy as jnp
        import numpy as np
        TOP_K = 6
        CAP_FACTOR = 2.0
        B, S, D = x.shape
        E = router_w.shape[0]
        K = TOP_K
        N = B * S
        C = max(1, int(N * K * CAP_FACTOR / E))
        router_logits = jnp.einsum('bsd,ed->bse', x, router_w) + bias
        hg = jnp.einsum('bsd,efd->bsef', x, shared_w_gate)
        hu = jnp.einsum('bsd,efd->bsef', x, shared_w_up)
        shared_out = jnp.einsum('bsef,edf->bsd', jax.nn.silu(hg) * hu, shared_w_down)
        shared_out = shared_out / shared_w_gate.shape[0]
        router_probs = jax.nn.softmax(router_logits, axis=-1)
        topk_p, topk_i = jax.lax.top_k(router_probs, K)
        topk_p = topk_p / (jnp.sum(topk_p, axis=-1, keepdims=True) + 1e-09)
        x_flat = x.reshape(N, D)
        flat_e = topk_i.reshape(-1)
        flat_g = topk_p.reshape(-1)
        token_ids = jnp.repeat(jnp.arange(N), K)
        order = jnp.argsort(flat_e)
        se = flat_e[order]
        st = token_ids[order]
        sg = flat_g[order]
        M = se.shape[0]
        pos = jnp.arange(M)
        is_first = jnp.concatenate([jnp.ones((1,), bool), se[1:] != se[:-1]])
        group_starts = jax.lax.cummax(pos * is_first.astype(pos.dtype))
        slot = pos - group_starts
        valid = slot < C
        safe_slot = jnp.where(valid, slot, C)
        expert_in = jnp.zeros((E, C + 1, D), x.dtype).at[se, safe_slot].set(x_flat[st])
        expert_gate = jnp.zeros((E, C + 1), x.dtype).at[se, safe_slot].set(sg)
        expert_tok = jnp.full((E, C + 1), N, jnp.int32).at[se, safe_slot].set(st.astype(jnp.int32))
        expert_mask = jnp.zeros((E, C + 1), bool).at[se, safe_slot].set(valid)
        expert_in = expert_in[:, :C]
        expert_gate = expert_gate[:, :C]
        expert_tok = expert_tok[:, :C]
        expert_mask = expert_mask[:, :C]
        hg = jnp.einsum('ecd,efd->ecf', expert_in, w_gate)
        hu = jnp.einsum('ecd,efd->ecf', expert_in, w_up)
        expert_out = jnp.einsum('ecf,edf->ecd', jax.nn.silu(hg) * hu, w_down)
        fm = expert_mask.reshape(-1)
        dst = jnp.where(fm, expert_tok.reshape(-1), N)
        fg = jnp.where(fm, expert_gate.reshape(-1), jnp.zeros((), x.dtype))
        sparse = jax.ops.segment_sum(fg[:, None] * expert_out.reshape(-1, D), dst, num_segments=N + 1)[:N]
        return shared_out + sparse.reshape(B, S, D)

    def _L1_gnn_ref(x, adj, W, a1, a2):
        import jax, jax.numpy as jnp
        import numpy as np
        N = 4096
        IN_F = 256
        OUT_F = 256
        ALPHA = 0.2
        NEG_INF = -9000000000000000.0
        h = x @ W.T
        src = h @ a1
        dst = h @ a2
        e = jax.nn.leaky_relu(src[:, None] + dst[None, :], negative_slope=ALPHA)
        e = jnp.where(adj == 0, jnp.float32(NEG_INF), e)
        attention = jax.nn.softmax(e, axis=1)
        h_prime = attention @ h
        return h_prime

    def _L1_ffn_ref(x, gate_weight, w1, b1, w2, b2):
        import jax, jax.numpy as jnp
        import numpy as np
        B, S, D = (8, 4096, 256)
        E, DFF = (16, 256)
        CAPACITY = 2
        Bx, Sx, Dx = x.shape
        num_experts = gate_weight.shape[1]
        k = Sx // num_experts * CAPACITY
        logits = jnp.einsum('bsd,de->bse', x, gate_weight)
        affinity = jax.nn.softmax(logits, axis=-1).transpose(0, 2, 1)
        gating, index = jax.lax.top_k(affinity, k)
        x_in = jnp.take_along_axis(x[:, None, :, :], index[..., None], axis=2)
        h = jax.nn.gelu(jnp.einsum('bekd,edh->bekh', x_in, w1) + b1[None, :, None, :])
        x_e = jnp.einsum('bekh,ehd->bekd', h, w2) + b2[None, :, None, :]
        weighted = gating[..., None] * x_e
        out = jnp.zeros_like(x)
        idx_flat = index.reshape(Bx, num_experts * k)
        vals_flat = weighted.reshape(Bx, num_experts * k, Dx)
        out = out.at[jnp.arange(Bx)[:, None], idx_flat].add(vals_flat)
        return out
    x = x + _L0_gnn_ref(_layernorm(x, axis=-1), adj, L0_gnn_W_self, L0_gnn_b_self, L0_gnn_W_nb, L0_gnn_b_nb, L0_gnn_W_comb, L0_gnn_b_comb)
    x = x + _L0_ffn_ref(_layernorm(x, axis=-1)[None], L0_ffn_router_w, L0_ffn_bias, L0_ffn_shared_w_gate, L0_ffn_shared_w_up, L0_ffn_shared_w_down, L0_ffn_w_gate, L0_ffn_w_up, L0_ffn_w_down)[0]
    x = x + _L1_gnn_ref(_layernorm(x, axis=-1), adj, L1_gnn_W, L1_gnn_a1, L1_gnn_a2)
    x = x + _L1_ffn_ref(_layernorm(x, axis=-1)[None], L1_ffn_gate_weight, L1_ffn_w1, L1_ffn_b1, L1_ffn_w2, L1_ffn_b2)[0]
    return x

_drawn_inputs = setup_inputs


def setup_inputs(seed=0):
    import zlib

    import numpy as np

    out = dict(_drawn_inputs(seed))
    spreads = {'L0_ffn_bias': (0.0, 0.8), 'L1_ffn_b1': (0.0, 0.8), 'L1_ffn_b2': (0.0, 2.0)}
    factors = {'L0_gnn_b_self': 4.913,
     'L0_gnn_b_nb': 4.255,
     'L0_ffn_router_w': 8.0,
     'L0_ffn_shared_w_gate': 6.714,
     'L0_ffn_shared_w_up': 6.649,
     'L0_ffn_shared_w_down': 6.658,
     'L0_ffn_w_gate': 8.0,
     'L0_ffn_w_up': 8.0,
     'L0_ffn_w_down': 8.0,
     'L1_ffn_gate_weight': 5.337,
     'L1_ffn_w1': 8.0,
     'L1_ffn_w2': 8.0,
     'L1_gnn_a1': 5.147}
    for name, (base, spread) in spreads.items():
        noise = np.random.default_rng([zlib.crc32(name.encode()), seed]).standard_normal(out[name].shape)
        drawn = base * np.exp(spread * noise) if base else spread * noise
        out[name] = jnp.asarray(drawn.astype(out[name].dtype))
    for name, factor in factors.items():
        out[name] = (out[name] * factor).astype(out[name].dtype)
    return out
```

```python
from contextlib import ExitStack

import concourse.bass as bass
from concourse import mybir

P = 128
N = 3327
D = 256
KC = D // P
T = (N + P - 1) // P
NP = T * P
PAD = N - (T - 1) * P
GT = 2
G = T // GT
GW = GT * P
EPS = 1e-5

E0, K0, SH = 64, 6, 2
CAP0 = max(1, int(N * K0 * 2.0 / E0))
B0 = (CAP0 + P - 1) // P
S0 = B0 * P
ZROW = E0 * S0
SKIP = 65536.0
POS_CHUNKS = [(0, 7), (7, 14), (14, 20), (20, 26)]

E1 = 16
CAP1 = N // E1 * 2
B1 = (CAP1 + P - 1) // P
S1 = B1 * P
XW = D + E1
TOP_BIT = 29

AW = 512
ABLOCKS = [(o, min(AW, NP - o)) for o in range(0, NP, AW)]
ALPHA = 0.2

F32, F16, BF16 = mybir.dt.float32, mybir.dt.float16, mybir.dt.bfloat16
I32, U32, U8 = mybir.dt.int32, mybir.dt.uint32, mybir.dt.uint8
ALU, ACT = mybir.AluOpType, mybir.ActivationFunctionType
AX = mybir.AxisListType.X
MAXR = bass.bass_isa.ReduceOp.max

HI, ONE, LO, XSW = 0, D, D + 2, 2 * D + 2
HW = D + 4


class Chain:

    def __init__(self, eng, sem):
        self.eng, self.sem, self.n, self.loop = eng, sem, 0, None

    def inc(self, ins):
        ins.then_inc(self.sem, 1)
        self.n += 1

    def wait(self):
        if self.loop is None:
            self.eng.wait_ge(self.sem, self.n)
        else:
            i, per = self.loop
            self.eng.wait_ge(self.sem, i * per + self.n)


def pipelined(eng, n, parts, chain=None):
    late = max(off for _, off in parts)
    early = min(off for _, off in parts)

    def step(s, base=None):
        for fn, off in parts:
            k = s - off
            if base is not None:
                fn(base + k, k % 2, False)
            elif 0 <= k < n:
                fn(k, k % 2, k < 2)

    lo, hi = late + 2, n + early
    pairs = max((hi - lo) // 2, 0)
    before = 0
    for s in range(early, lo):
        before = chain.n if chain else 0
        step(s)
    if pairs > 1:
        if chain:
            per, start = chain.n - before, chain.n
        with eng.Fori(0, pairs) as i:
            if chain:
                chain.loop = (i, 2 * per)
            step(lo, base=i * 2)
            step(lo + 1, base=i * 2)
        if chain:
            assert chain.n == start + 2 * per, (chain.n, start, per)
            chain.loop = None
            chain.n = start + 2 * per * pairs
        lo += 2 * pairs
    for s in range(lo, n + late):
        step(s)


def each(eng, n, fn, chain, per):
    start = chain.n
    with eng.Fori(0, n) as i:
        chain.loop = (i, per)
        fn(i)
    assert chain.n == start + per
    chain.loop = None
    chain.n = start + per * n


def cols(k, width):
    return bass.ds(k * width, width)


def bc(ap, shape, axis):
    return ap.unsqueeze(axis).broadcast_to(shape)


def build(nc, d, out, xbuf, ybuf, rbuf):
    top = ExitStack()
    with top:
        def sem(name):
            return top.enter_context(nc.semaphore(name))

        def sems(name, n):
            return [sem(f"{name}{i}") for i in range(n)]

        def stage():
            ctx = ExitStack()
            return ctx, lambda name, shape, dt: ctx.enter_context(nc.sbuf_tensor(name, shape, dt))

        banks = [top.enter_context(nc.psum_tensor(f"bank{i}", [P, 512], F32)) for i in range(8)]

        _ctx, sb = stage()
        top.enter_context(_ctx)
        X = sb("X", [P, T, D], F32)
        ident = sb("ident", [P, P], F32)
        ones = sb("ones", [P, P], F32)
        ones16 = sb("ones16", [P, P], BF16)
        before = sb("before", [P, P], BF16)
        bn = sb("bn", [P, T, 6], F32)
        mean = sb("mean", [P, T], F32)
        rstd = sb("rstd", [P, T], F32)
        stat = sb("stat", [P, 3, T], F32)
        iota64 = sb("iota64", [P, E0], F32)
        slots16 = sb("slots16", [P, S1], F16)
        tokp = sb("tokp", [P, T, 2], F16)
        padm = sb("padm", [P, 1], F32)
        padn = sb("padn", [P, 1], F32)
        tail = sb("tail", [P, B1], F32)
        G6 = sb("G6", [P, T, K0], F32)
        DG = sb("DG", [P, T, K0], U32)
        SC = sb("SC", [P, 64], F32)

        m_ctx, sb = stage()
        M = sb("M", [P, T, NP], U8)

        ctx, sb = stage()
        XS = sb("XS", [P, T, XSW], F16)
        adj = [sb(f"adj{i}", [P, T, P], I32) for i in range(2)]
        mt = [sb(f"mt{i}", [P, T, P], F16) for i in range(2)]
        WselfT = sb("WselfT", [P, KC, D], F32)
        WnbT = sb("WnbT", [P, KC, D], F32)
        Wc = sb("Wc", [P, 2 * KC, D], F32)
        bsn = sb("bsn", [P, 2, KC], F32)
        bcomb = sb("bcomb", [1, D], F32)
        WF = sb("WF", [P, 2 * KC, D], F32)
        BF = sb("BF", [1, D], F32)
        dg = [sb(f"dg{i}", [P, 2], F32) for i in range(2)]
        sa = [sb(f"sa{i}", [P, 2 * KC, P], F32) for i in range(2)]
        saT = [sb(f"saT{i}", [P, 2 * KC, P], F32) for i in range(2)]
        xn0 = [sb(f"xn0{i}", [P, D], F32) for i in range(2)]
        ctx.close()

        ctx, sb = stage()
        XN = sb("XN", [P, T, D], F32)
        zero = sb("zero", [P, 1024], F32)
        LG = sb("LG", [P, T, E0], F32)
        IX8 = sb("IX8", [P, T, 8], U32)
        MX8 = sb("MX8", [P, T, 8], F32)
        DS = sb("DS", [P, T, K0], U32)
        OH = sb("OH", [P, K0, T, E0], BF16)
        in1, sb = stage()
        xg = [sb(f"xg{i}", [P, GT * KC, P], F32) for i in range(2)]
        xT = [sb(f"xT{i}", [P, KC, GW], F32) for i in range(2)]
        sgs = [sb(f"sgs{i}", [P, SH, GW], F32) for i in range(2)]
        acs = [sb(f"acs{i}", [P, SH, GW], F32) for i in range(2)]
        rw = sb("rw", [P, KC, E0], F32)
        rb = sb("rb", [1, E0], F32)
        sgu = sb("sgu", [P, SH, 2, KC, P], F32)
        sdn = sb("sdn", [P, SH, D], F32)
        in1.close()
        in2, sb = stage()
        EXs = sb("EXs", [P, T, E0], F32)
        POS = sb("POS", [P, T, E0], F32)
        TOT = [sb(f"TOT{i}", [P, T, E0], F32) for i in range(2)]
        R6 = [sb(f"R6{i}", [P, T, K0], F32) for i in range(4)]
        in2.close()
        ctx.close()

        ctx, sb = stage()
        ex_in = [sb(f"ex_in{i}", [P, B0, D], F32) for i in range(2)]
        ex_w = [sb(f"ex_w{i}", [P, 6 * P], F32) for i in range(2)]
        ex_T = [sb(f"ex_T{i}", [P, KC, S0], F32) for i in range(2)]
        ex_sg = [sb(f"ex_sg{i}", [P, S0], F32) for i in range(2)]
        ex_ac = [sb(f"ex_ac{i}", [P, S0], F32) for i in range(2)]
        ex_y = [sb(f"ex_y{i}", [P, B0, D], F32) for i in range(2)]
        ctx.close()
        ctx, sb = stage()
        Y6 = [sb(f"Y6{i}", [P, K0, D], F32) for i in range(4)]
        ctx.close()

        ctx, sb = stage()
        H = sb("H", [P, T, HW], F32)
        SD = sb("SD", [P, T, 2], F32)
        dcol = sb("dcol", [P, 3, T], F32)
        HS = sb("HS", [P, D + 2], F32)
        W2 = sb("W2", [P, KC, D + 2], F32)
        in1, sb = stage()
        gxg = [sb(f"gxg{i}", [P, GT * KC, P], F32) for i in range(2)]
        gxT = [sb(f"gxT{i}", [P, KC, GW], F32) for i in range(2)]
        Wn = sb("Wn", [P, KC, D], F32)
        a12 = sb("a12", [P, KC, 2], F32)
        in1.close()
        PB = sb_keep = None
        in1, sb = stage()
        PB = sb("PB", [P, NP], F32)
        QB = sb("QB", [P, NP], F32)
        MM = sb("MM", [P, 6, T], F32)
        in2, sb = stage()
        acc = sb("acc", [P, NP], F32)
        dgn = [sb(f"dgn{i}", [P, 4, P], F32) for i in range(2)]
        in2.close()
        in2, sb = stage()
        at1 = [sb(f"at1{i}", [P, AW], F32) for i in range(2)]
        at2 = [sb(f"at2{i}", [P, AW], F32) for i in range(2)]
        atp = [sb(f"atp{i}", [P, AW], F32) for i in range(2)]
        num = [sb(f"num{i}", [P, D + 2], F32) for i in range(2)]
        in2.close()
        in1.close()
        ctx.close()
        m_ctx.close()

        ctx, sb = stage()
        XR = sb("XR", [P, T, XW], F32)
        AF = sb("AF", [P, T, E1], F32)
        fxg = [sb(f"fxg{i}", [P, GT * KC, P], F32) for i in range(2)]
        fxT = [sb(f"fxT{i}", [P, KC, GW], F32) for i in range(2)]
        gw = sb("gw", [P, KC, E1], F32)
        F1 = sb("F1", [P, T, E1], F32)
        F2 = sb("F2", [P, T, E1], F32)
        F3 = sb("F3", [P, T, E1], F32)
        SL = sb("SL", [P, T, E1], F32)
        S16 = sb("S16", [P, T, E1], BF16)
        thr = sb("thr", [P, E1], I32)
        cand = sb("cand", [P, E1], I32)
        stepi = sb("stepi", [P, E1], I32)
        biti = sb("biti", [P, E1], I32)
        bitf = sb("bitf", [P, E1], F32)
        cnt = sb("cnt", [P, E1], F32)
        oh1 = [sb(f"oh1{i}", [P, S1], F16) for i in range(2)]
        LT = sb("LT", [P, E1, B1, 2], F32)
        LI = sb("LI", [P, E1, B1], F32)
        GI = sb("GI", [P, E1, B1], U32)
        SI = sb("SI", [P, E1, B1], U32)
        in1, sb = stage()
        w12 = [sb(f"w12{i}", [P, 2 * KC, D], F32) for i in range(2)]
        b1c = sb("b1c", [P, E1, KC], F32)
        b2r = sb("b2r", [1, E1, D], F32)
        fx = [sb(f"fx{i}", [P, B1, XW], F32) for i in range(2)]
        fT = [sb(f"fT{i}", [P, KC, S1], F32) for i in range(2)]
        fh = [sb(f"fh{i}", [P, KC, S1], F32) for i in range(2)]
        fy = [sb(f"fy{i}", [P, B1, D], F32) for i in range(2)]
        in1.close()
        ctx.close()

        stage_end = sem("stage_end")
        dve_done, act_done, pool_done = sem("dve_done"), sem("act_done"), sem("pool_done")
        x_in, w0_in, adj_in = sem("x_in"), sem("w0_in"), sems("adj_in", 2)
        consts = sem("consts")
        var_ready, std_ready = sem("var_ready"), sem("std_ready")
        fold_done, fold_copied = sem("fold_done"), sem("fold_copied")
        xs_ready, mask_ready, agg_done, agg_read = sem("xs_ready"), sem("mask_ready"), sem("agg_done"), sem("agg_read")
        sa_ready, saT_done, saT_copied, comb_done, x1_ready = (
            sem("sa_ready"), sem("saT_done"), sem("saT_copied"), sem("comb_done"), sem("x1_ready"))
        zero_ready, zero_out, w1_in = sem("zero_ready"), sem("zero_out"), sem("w1_in")
        xg_ready, xg_kept, xT_done, xT_copied = sem("xg_ready"), sem("xg_kept"), sem("xT_done"), sem("xT_copied")
        lg_done, lg_read, hgu_done, sg_ready, acs_ready, sd_done, sd_read = (
            sem("lg_done"), sem("lg_read"), sem("hgu_done"), sem("sg_ready"), sem("acs_ready"), sem("sd_done"),
            sem("sd_read"))
        exp_in, exp_out = sem("exp_in"), sem("exp_out")
        sel_ready, pos_done, pos_read, rows_ready, rows_out = (
            sem("sel_ready"), sem("pos_done"), sem("pos_read"), sem("rows_ready"), sem("rows_out"))
        exin, exw = sems("exin", 2), sems("exw", 2)
        exT_done, exT_copied, exT_mid, exgu_done, exsg_ready, exac_ready, exy_done, exy_copied = (
            sem("exT_done"), sem("exT_copied"), sem("exT_mid"), sem("exgu_done"), sem("exsg_ready"), sem("exac_ready"),
            sem("exy_done"), sem("exy_copied"))
        exy_out = sems("exy_out", 2)
        y6_in, y6_used = sems("y6_in", 4), sem("y6_used")
        w2_in, va_done, va_copied = sem("w2_in"), sem("va_done"), sem("va_copied")
        gxg_ready, gxT_done, gxT_copied, h_done, h_copied = (
            sem("gxg_ready"), sem("gxT_done"), sem("gxT_copied"), sem("h_done"), sem("h_copied"))
        hs_done, mn_ready, mn_all, acc_ready, accT_done, accT_read = (
            sem("hs_done"), sem("mn_ready"), sem("mn_all"), sem("acc_ready"), sem("accT_done"), sem("accT_read"))
        dgn_ready, pb_done, pb_copied = sem("dgn_ready"), sem("pb_done"), sem("pb_copied")
        at1_ready, at2_ready, ate_ready, atp_ready, atp_used, blk_done, blk_read = (
            sem("at1_ready"), sem("at2_ready"), sem("ate_ready"), sem("atp_ready"), sem("atp_used"),
            sem("blk_done"), sem("blk_read"))
        w3_in, fxg_ready, fxT_done, fxT_copied, fl_done, fl_read = (
            sem("w3_in"), sem("fxg_ready"), sem("fxT_done"), sem("fxT_copied"), sem("fl_done"), sem("fl_read"))
        aff_in, aff_out, xr_ready, xr_out, x3_out = (
            sem("aff_in"), sem("aff_out"), sem("xr_ready"), sem("xr_out"), sem("x3_out"))
        cmp_ready, cnt_done, sel1_ready, sel1_done = (
            sem("cmp_ready"), sem("cnt_done"), sem("sel1_ready"), sem("sel1_done"))
        oh_ready, oh_used, lt_done, lt_read, li_ready = (
            sem("oh_ready"), sem("oh_used"), sem("lt_done"), sem("lt_read"), sem("li_ready"))
        fw_in, fx_in = sems("fw_in", 2), sems("fx_in", 2)
        fT_done, fT_read, fh_done, fh_ready, fy_done, fy_ready = (
            sem("fT_done"), sem("fT_read"), sem("fh_done"), sem("fh_ready"), sem("fy_done"), sem("fy_ready"))
        y_out = sem("y_out")

        block = top.enter_context(nc.Block())

        def end_stage(eng, k):
            eng.drain().then_inc(stage_end, 1)
            eng.wait_ge(stage_end, 5 * k)

        out_rows = out[0:(T - 1) * P, :].rearrange("(t p) d -> p t d", p=P)

        @block.sync
        def _(sp):
            sp.dma_start(X[:, :, :], d["x"]).then_inc(x_in, 16)
            for dst, name in ((WselfT, "W_self_T"), (WnbT, "W_nb_T"), (Wc, "W_comb"), (bsn, "b_self_nb"),
                              (bcomb, "b_comb")):
                sp.dma_start(dst[tuple(slice(None) for _ in dst.shape)], d[name]).then_inc(w0_in, 16)

            def load_adj(k, par, first):
                if not first:
                    sp.wait_ge(mask_ready, k - 1)
                sp.dma_start(adj[par][:, :, :], d["adj"][k, :, :, :]).then_inc(adj_in[par], 16)
            pipelined(sp, T, [(load_adj, 0)])
            end_stage(sp, 1)

            for dst, name in ((rw, "router_w"), (rb, "router_b"), (sgu, "shared_gate_up"), (sdn, "shared_down")):
                sp.dma_start(dst[tuple(slice(None) for _ in dst.shape)], d[name]).then_inc(w1_in, 16)
            sp.wait_ge(zero_ready, 1)
            per = 1024 // D
            with sp.Fori(0, E0 * S0 // (P * per)) as i:
                sp.dma_start(xbuf[bass.ds(i * (P * per), P * per), :].rearrange("(p r) d -> p (r d)", p=P),
                             zero[:, :]).then_inc(zero_out, 16)
            sp.dma_start(ybuf[ZROW:ZROW + 1, :], zero[0:1, 0:D]).then_inc(zero_out, 16)
            sp.wait_ge(zero_out, 16 * (E0 * S0 // (P * per) + 1))
            end_stage(sp, 2)

            def load_expert(k, par, first):
                if not first:
                    sp.wait_ge(exT_done, 3 * k - 3)
                sp.dma_start(ex_in[par][:, :, :],
                             xbuf[bass.ds(k * S0, S0), :].rearrange("(b p) d -> p b d", p=P)).then_inc(exin[par], 16)
                if not first:
                    sp.wait_ge(exy_done, 3 * k - 3)
                sp.dma_start(ex_w[par][:, :], d["experts0"][k, :, :]).then_inc(exw[par], 16)

            def store_expert(k, par, first):
                sp.wait_ge(exy_copied, 3 * k + 3)
                sp.dma_start(ybuf[bass.ds(k * S0, S0), :].rearrange("(b p) d -> p b d", p=P),
                             ex_y[par][:, :, :]).then_inc(exy_out[par], 16)
            pipelined(sp, E0, [(load_expert, -2), (store_expert, 0)])
            for s in exy_out:
                sp.wait_ge(s, 16 * E0 // 2)
            end_stage(sp, 3)
            end_stage(sp, 4)

            sp.dma_start(W2[:, :, 0:D], d["W_T"]).then_inc(w2_in, 16)
            sp.dma_start(Wn[:, :, :], d["W"]).then_inc(w2_in, 16)
            sp.dma_start(a12[:, :, :], d["a12"]).then_inc(w2_in, 16)
            end_stage(sp, 5)
            end_stage(sp, 6)

            sp.dma_start(gw[:, :, :], d["gate_w"]).then_inc(w3_in, 16)
            sp.dma_start(out_rows, X[:, 0:T - 1, :]).then_inc(x3_out, 16)
            sp.dma_start(out[(T - 1) * P:N, :], X[0:PAD, T - 1, :]).then_inc(x3_out, 16)
            sp.dma_start(b1c[:, :, :], d["b1"]).then_inc(w3_in, 16)
            sp.dma_start(b2r[:, :, :], d["b2"]).then_inc(w3_in, 16)
            sp.wait_ge(xr_ready, 1)
            sp.dma_start(rbuf.rearrange("(t p) d -> p t d", p=P), XR[:, :, :]).then_inc(xr_out, 16)
            sp.wait_ge(x3_out, 32)
            sp.wait_ge(xr_out, 16)
            end_stage(sp, 7)

            def load_w1(k, par, first):
                if not first:
                    sp.wait_ge(fy_done, 2 * k - 2)
                sp.dma_start(w12[par][:, :, :], d["experts1"][k, :, :, :]).then_inc(fw_in[par], 16)
            pipelined(sp, E1, [(load_w1, 0)])
            end_stage(sp, 8)

        @block.gpsimd
        def _(pool):
            c = Chain(pool, pool_done)
            c.inc(pool.memset(ident[:, :], 0.0))
            c.inc(pool.memset(before[:, :], 0.0))
            pool.memset(ones[:, :], 1.0).then_inc(consts, 1)
            pool.memset(ones16[:, :], 1.0).then_inc(consts, 1)
            pool.memset(XS[:, :, ONE:LO], 1.0).then_inc(consts, 1)
            pool.iota(iota64[:, :], [[1, E0]], base=0, channel_multiplier=0,
                      allow_small_or_imprecise_dtypes=True).then_inc(consts, 1)
            pool.iota(slots16[:, :], [[1, S1]], base=0, channel_multiplier=0,
                      allow_small_or_imprecise_dtypes=True).then_inc(consts, 1)
            pool.iota(tokp[:, :, 0], [[1, T]], base=0, channel_multiplier=0,
                      allow_small_or_imprecise_dtypes=True).then_inc(consts, 1)
            pool.iota(tokp[:, :, 1], [[0, T]], base=0, channel_multiplier=1,
                      allow_small_or_imprecise_dtypes=True).then_inc(consts, 1)
            c.inc(pool.memset(padm[:, :], 1.0))
            c.inc(pool.memset(padn[:, :], 0.0))
            c.inc(pool.memset(tail[:, :], 0.0))
            c.wait()
            pool.affine_select(out=ident[:, :], in_=ident[:, :], compare_op=ALU.not_equal, fill=1.0, base=0,
                               pattern=[[-1, P]], channel_multiplier=1).then_inc(consts, 1)
            pool.affine_select(out=before[:, :], in_=before[:, :], compare_op=ALU.is_ge, fill=1.0, base=0,
                               pattern=[[-1, P]], channel_multiplier=1).then_inc(consts, 1)
            pool.affine_select(out=padm[:, :], in_=padm[:, :], compare_op=ALU.not_equal, fill=0.0, base=-PAD,
                               pattern=[[0, 1]], channel_multiplier=1).then_inc(consts, 1)
            pool.affine_select(out=padn[:, :], in_=padn[:, :], compare_op=ALU.not_equal, fill=-1.0, base=-PAD,
                               pattern=[[0, 1]], channel_multiplier=1).then_inc(consts, 1)
            pool.affine_select(out=tail[:, :], in_=tail[:, :], compare_op=ALU.is_ge, fill=SKIP, base=CAP1 - 1,
                               pattern=[[-P, B1]], channel_multiplier=-1).then_inc(consts, 1)
            end_stage(pool, 1)

            pool.memset(zero[:, :], 0.0).then_inc(zero_ready, 1)

            def keep_xn(k, par, first):
                pool.wait_ge(xg_ready, k + 1)
                pool.tensor_copy(XN[:, cols(k, GT), :].rearrange("p t d -> p (t d)"),
                                 xg[par][:, :, :].rearrange("p a b -> p (a b)")).then_inc(xg_kept, 1)
            pipelined(pool, G, [(keep_xn, 0)])
            pool.wait_ge(rows_ready, 1)
            pool.wait_ge(xg_kept, G)
            pool.wait_ge(zero_out, 16 * (E0 * S0 // (P * (1024 // D)) + 1))
            for t in range(T):
                for k in range(K0):
                    pool.indirect_dma_start(
                        xbuf[0:E0 * S0, :], bass.IndirectOffsetOnAxis(ap=DS[:, t, k:k + 1], axis=0), XN[:, t, :], None,
                        bounds_check=E0 * S0 - 1, oob_is_err=False).then_inc(rows_out, 16)
            pool.wait_ge(rows_out, 16 * T * K0)
            end_stage(pool, 2)
            end_stage(pool, 3)
            for t in range(T):
                if t >= 4:
                    pool.wait_ge(y6_used, t - 3)
                for k in range(K0):
                    pool.indirect_dma_start(
                        Y6[t % 4][:, k, :], None, ybuf[:, :], bass.IndirectOffsetOnAxis(ap=DG[:, t, k:k + 1], axis=0),
                        bounds_check=ZROW, oob_is_err=False).then_inc(y6_in[t % 4], 16)
            end_stage(pool, 4)
            pool.wait_ge(mn_ready, 1)
            pool.partition_all_reduce(SC[:, 1:2], SC[:, 0:1], P, MAXR).then_inc(mn_all, 1)
            end_stage(pool, 5)
            end_stage(pool, 6)
            end_stage(pool, 7)

            def gather(e):
                if e >= 2:
                    pool.wait_ge(fy_ready, e - 1)
                for b in range(B1):
                    pool.indirect_dma_start(
                        fx[e % 2][:, b, :], None, rbuf[:, :], bass.IndirectOffsetOnAxis(ap=GI[:, e, b:b + 1], axis=0),
                        bounds_check=NP - 1, oob_is_err=False).then_inc(fx_in[e % 2], 16)
            gather(0)
            gather(1)
            for e in range(E1):
                pool.wait_ge(fy_ready, e + 1)
                if e:
                    pool.wait_ge(y_out, 16 * B1 * e)
                for b in range(B1):
                    pool.indirect_dma_start(
                        out[:, :], bass.IndirectOffsetOnAxis(ap=SI[:, e, b:b + 1], axis=0), fy[e % 2][:, b, :], None,
                        bounds_check=N - 1, oob_is_err=False, compute_op=ALU.add).then_inc(y_out, 16)
                if e + 2 < E1:
                    gather(e + 2)
            pool.wait_ge(y_out, 16 * B1 * E1)
            end_stage(pool, 8)

        @block.scalar
        def _(act):
            c = Chain(act, act_done)

            def norm_root(n):
                act.wait_ge(var_ready, n)
                act.activation(stat[:, 1, :], stat[:, 0, :], ACT.Sqrt).then_inc(std_ready, 1)

            norm_root(1)
            act.wait_ge(fold_done, 2)
            act.copy(WF[:, 0:KC, :].rearrange("p c n -> p (c n)"), banks[6][:, :]).then_inc(fold_copied, 1)
            act.copy(WF[:, KC:2 * KC, :].rearrange("p c n -> p (c n)"), banks[7][:, :]).then_inc(fold_copied, 1)

            def copy_saT(k, par, first):
                act.wait_ge(saT_done, k + 1)
                if not first:
                    act.wait_ge(comb_done, k - 1)
                act.copy(saT[par][:, :, :].rearrange("p a b -> p (a b)"), banks[2 + par][:, :]).then_inc(saT_copied, 1)
            pipelined(act, T, [(copy_saT, 0)])
            end_stage(act, 1)

            norm_root(2)

            def copy_xT(k, par, first):
                act.wait_ge(xT_done, k + 1)
                if not first:
                    act.wait_ge(hgu_done, 2 * k - 2)
                act.copy(xT[par][:, :, :].rearrange("p a b -> p (a b)"), banks[par][:, :]).then_inc(xT_copied, 1)

            def silu_shared(k, par, first):
                if not first:
                    act.wait_ge(acs_ready, 2 * k - 2)
                for s in range(SH):
                    act.wait_ge(hgu_done, 2 * k + s + 1)
                    act.activation(sgs[par][:, s, :], banks[3 + s][:, 0:GW], ACT.Silu).then_inc(sg_ready, 1)
            pipelined(act, G, [(copy_xT, 0), (silu_shared, 0)])
            act.wait_ge(exp_in, 1)
            act.activation(EXs[:, :, :], EXs[:, :, :], ACT.Exp).then_inc(exp_out, 1)
            act.activation(R6[0][:, :, :], R6[0][:, :, :], ACT.Exp).then_inc(exp_out, 1)
            end_stage(act, 2)

            def copy_exT(k, par, first):
                if not first:
                    act.wait_ge(exgu_done, 2 * k - 2)
                for j in (0, 2):
                    nb = min(2, B0 - 2 * j)
                    act.wait_ge(exT_done, 3 * k + j + 1)
                    act.copy(ex_T[par][:, :, 2 * j * P:(2 * j + nb) * P],
                             banks[(par + j) % 2][:, 0:KC * nb * P].rearrange("p (c n) -> p c n", c=KC)
                             ).then_inc(exT_copied, 1)

            def silu_expert(k, par, first):
                if not first:
                    act.wait_ge(exac_ready, 2 * k - 2)
                for h in range(2):
                    act.wait_ge(exgu_done, 2 * k + h + 1)
                    act.activation(ex_sg[par][:, cols(h, S0 // 2)], banks[2 + 2 * h][:, 0:S0 // 2],
                                   ACT.Silu).then_inc(exsg_ready, 1)

            def copy_exy(k, par, first):
                if not first:
                    act.wait_ge(exy_out[par], (k - par) * 8)
                for j in range(3):
                    nb = min(2, B0 - 2 * j)
                    act.wait_ge(exy_done, 3 * k + j + 1)
                    act.copy(ex_y[par][:, 2 * j:2 * j + nb, :].rearrange("p b d -> p (b d)"),
                             banks[6 + (par + j) % 2][:, 0:nb * D]).then_inc(exy_copied, 1)
            pipelined(act, E0, [(copy_exT, -1), (silu_expert, 0), (copy_exy, 0)])
            end_stage(act, 3)
            end_stage(act, 4)

            norm_root(3)
            act.wait_ge(va_done, 1)
            act.copy(W2[:, :, D:D + 2], banks[7][:, 0:2 * KC].rearrange("p (c n) -> p c n", c=KC)).then_inc(va_copied, 1)

            def copy_gxT(k, par, first):
                act.wait_ge(gxT_done, k + 1)
                if not first:
                    act.wait_ge(h_done, 2 * k - 2)
                act.copy(gxT[par][:, :, :].rearrange("p a b -> p (a b)"), banks[par][:, :]).then_inc(gxT_copied, 1)
            pipelined(act, G, [(copy_gxT, 0)])
            end_stage(act, 5)

            def copy_pb(k):
                act.wait_ge(pb_done, k + 1)
                o, w = ABLOCKS[k // 2]
                act.copy((PB, QB)[k % 2][:, o:o + w], banks[k % 2][:, 0:w]).then_inc(pb_copied, 1)
            for k in range(2 * len(ABLOCKS)):
                copy_pb(k)
            act.wait_ge(pb_copied, 2 * len(ABLOCKS))
            for bi, (o, w) in enumerate(ABLOCKS):
                base = T * bi

                def attend_sum(k, par, first):
                    if not first or bi:
                        act.wait_ge(at2_ready, k + base - 1)
                    act.activation(at1[par][:, 0:w], PB[:, o:o + w], ACT.Identity,
                                   bias=dcol[:, 0, k:k + 1] if isinstance(k, int) else dcol[:, 0, bass.ds(k, 1)]
                                   ).then_inc(at1_ready, 1)

                def attend_exp(k, par, first):
                    act.wait_ge(at2_ready, k + base + 1)
                    act.activation(at2[par][:, 0:w], at2[par][:, 0:w], ACT.Exp).then_inc(ate_ready, 1)
                pipelined(act, T, [(attend_sum, 0), (attend_exp, 1)])
            end_stage(act, 6)

            norm_root(4)

            def copy_fxT(k, par, first):
                act.wait_ge(fxT_done, k + 1)
                if not first:
                    act.wait_ge(fl_done, k - 1)
                act.copy(fxT[par][:, :, :].rearrange("p a b -> p (a b)"), banks[par][:, :]).then_inc(fxT_copied, 1)
            pipelined(act, G, [(copy_fxT, 0)])
            act.wait_ge(aff_in, 1)
            act.activation(AF[:, :, :], AF[:, :, :], ACT.Exp).then_inc(aff_out, 1)
            end_stage(act, 7)

            act.wait_ge(w3_in, 48)

            def gelu(k, par, first):
                if not first:
                    act.wait_ge(fy_done, 2 * k - 2)
                for h in range(KC):
                    act.wait_ge(fh_done, 2 * k + h + 1)
                    act.activation(fh[par][:, h, :], banks[2 + h][:, :], ACT.Gelu_apprx_tanh,
                                   bias=b1c[:, k, h:h + 1]).then_inc(fh_ready, 1)
            pipelined(act, E1, [(gelu, 0)])
            end_stage(act, 8)

        @block.vector
        def _(dve):
            c = Chain(dve, dve_done)
            norms = [0]

            def layer_norm():
                norms[0] += 1
                each(dve, T, lambda t: c.inc(dve.bn_stats(bn[:, t, :], X[:, t, :])), c, 1)
                c.wait()
                c.inc(dve.tensor_tensor(stat[:, 0, :], bn[:, :, 1], bn[:, :, 4], ALU.add))
                c.inc(dve.tensor_tensor(stat[:, 1, :], bn[:, :, 1], bn[:, :, 4], ALU.subtract))
                c.inc(dve.tensor_tensor(stat[:, 2, :], bn[:, :, 2], bn[:, :, 5], ALU.add))
                c.wait()
                c.inc(dve.tensor_scalar(mean[:, :], stat[:, 0, :], 0.5, None, ALU.mult))
                c.inc(dve.scalar_tensor_tensor(stat[:, 1, :], stat[:, 1, :], 0.25, stat[:, 1, :], ALU.mult, ALU.mult))
                c.wait()
                c.inc(dve.scalar_tensor_tensor(stat[:, 0, :], stat[:, 2, :], 1.0 / D, stat[:, 1, :], ALU.mult, ALU.add))
                c.wait()
                dve.tensor_scalar(stat[:, 0, :], stat[:, 0, :], EPS, None, ALU.add).then_inc(var_ready, 1)
                dve.wait_ge(std_ready, norms[0])
                c.inc(dve.reciprocal(rstd[:, :], stat[:, 1, :]))
                c.wait()

            def normalise(dst, t):
                return dve.tensor_scalar(dst, X[:, t, :], mean[:, bass.ds(t, 1)], rstd[:, bass.ds(t, 1)],
                                         ALU.subtract, ALU.mult)

            def normalise_group(dst, k):
                for u in range(GT - 1):
                    c.inc(normalise(dst[:, cols(u, KC), :].rearrange("p a b -> p (a b)"), k * GT + u))
                return normalise(dst[:, (GT - 1) * KC:GT * KC, :].rearrange("p a b -> p (a b)"), k * GT + GT - 1)

            dve.wait_ge(x_in, 16)
            layer_norm()

            def split(k, par, first):
                c.inc(normalise(xn0[par][:, :], k))
                c.wait()
                c.inc(dve.tensor_copy(XS[:, k, HI:HI + D], xn0[par][:, :]))
                c.wait()
                c.inc(dve.tensor_tensor(XS[:, k, LO:LO + D], xn0[par][:, :], XS[:, k, HI:HI + D], ALU.subtract))
            pipelined(dve, T, [(split, 0)], c)
            c.wait()
            dve.tensor_copy(dg[0][:, :], XS[:, 0, 0:2]).then_inc(xs_ready, 1)
            dve.wait_ge(fold_done, 3)
            dve.wait_ge(w0_in, 80)
            dve.tensor_tensor(BF[:, :], banks[5][0:1, 0:D], bcomb[:, :], ALU.add).then_inc(fold_copied, 1)

            def masks(k, par, first):
                dve.wait_ge(adj_in[par], (k - par) * 8 + 16)
                if not first:
                    dve.wait_ge(agg_done, k - 1)
                c.inc(dve.tensor_scalar(mt[par][:, :, :], adj[par][:, :, :], 0, None, ALU.is_gt))
                c.wait()
                dve.tensor_scalar(M[:, :, cols(k, P)], adj[par][:, :, :], 0, None, ALU.is_gt).then_inc(mask_ready, 1)

            def mean_of_neighbours(k, par, first):
                dve.wait_ge(agg_done, k + 1)
                if not first:
                    dve.wait_ge(saT_done, k - 1)
                c.inc(normalise(sa[par][:, 0:KC, :].rearrange("p a b -> p (a b)"), k))
                c.inc(dve.tensor_scalar(dg[par][:, 0:1], banks[par][:, D:D + 1], 1.0, None, ALU.max))
                c.wait()
                c.inc(dve.reciprocal(dg[par][:, 1:2], dg[par][:, 0:1]))
                c.wait()
                dve.tensor_scalar(sa[par][:, KC:2 * KC, :].rearrange("p a b -> p (a b)"), banks[par][:, 0:D],
                                  dg[par][:, 1:2], None, ALU.mult).then_inc(sa_ready, 1)

            def residual0(k, par, first):
                dve.wait_ge(comb_done, k + 1)
                dve.scalar_tensor_tensor(X[:, k, :], banks[4 + par][:, 0:D], 0.0, X[:, k, :], ALU.max,
                                         ALU.add).then_inc(x1_ready, 1)
            pipelined(dve, T, [(mean_of_neighbours, 1), (residual0, 2), (masks, -1)], c)
            end_stage(dve, 1)

            layer_norm()

            def xn_group(k, par, first):
                if not first:
                    dve.wait_ge(xT_done, k - 1)
                    dve.wait_ge(xg_kept, k - 1)
                normalise_group(xg[par], k).then_inc(xg_ready, 1)

            def read_logits(k, par, first):
                dve.wait_ge(lg_done, k + 1)
                dve.tensor_copy(LG[:, cols(k, GT), :].rearrange("p t e -> p (t e)"),
                                banks[2][:, 0:GT * E0]).then_inc(lg_read, 1)

            def gate_shared(k, par, first):
                if not first:
                    dve.wait_ge(sd_done, k - 1)
                for s in range(SH):
                    dve.wait_ge(sg_ready, 2 * k + s + 1)
                    dve.scalar_tensor_tensor(acs[par][:, s, :], banks[3 + s][:, GW:2 * GW], 1.0 / SH, sgs[par][:, s, :],
                                             ALU.mult, ALU.mult).then_inc(acs_ready, 1)

            def add_shared(k, par, first):
                dve.wait_ge(sd_done, k + 1)
                dve.tensor_tensor(X[:, cols(k, GT), :].rearrange("p t d -> p (t d)"), banks[5 + par][:, :],
                                  X[:, cols(k, GT), :].rearrange("p t d -> p (t d)"), ALU.add).then_inc(sd_read, 1)
            pipelined(dve, G, [(xn_group, -1), (read_logits, 0), (gate_shared, 0), (add_shared, 0)], c)
            dve.wait_ge(lg_read, G)
            dve.wait_ge(xg_kept, G)
            dve.wait_ge(sd_read, G)
            for t in range(T):
                c.inc(dve.max(MX8[:, t, :], LG[:, t, :]))
            c.wait()
            for t in range(T):
                c.inc(dve.max_index(IX8[:, t, :], MX8[:, t, :], LG[:, t, :]))
            c.inc(dve.tensor_tensor(EXs[:, :, :], LG[:, :, :], MX8[:, :, 0:1].broadcast_to([P, T, E0]), ALU.subtract))
            dve.tensor_tensor(R6[0][:, :, :], MX8[:, :, 0:K0], MX8[:, :, 0:1].broadcast_to([P, T, K0]),
                              ALU.subtract).then_inc(exp_in, 1)
            c.wait()
            c.inc(dve.tensor_copy(R6[1][:, :, :], IX8[:, :, 0:K0]))
            c.wait()
            for k in range(K0):
                c.inc(dve.tensor_tensor(OH[:, k, :, :], iota64[:, :].unsqueeze(1).broadcast_to([P, T, E0]),
                                        R6[1][:, :, k:k + 1].broadcast_to([P, T, E0]), ALU.is_equal))
            c.wait()
            SELB = TOT[0][:, :, :].bitcast(BF16)[:, :, 0:E0]
            c.inc(dve.tensor_tensor(SELB, OH[:, 0, :, :], OH[:, 1, :, :], ALU.add))
            for k in range(2, K0):
                c.wait()
                ins = dve.tensor_tensor(SELB, SELB, OH[:, k, :, :], ALU.add)
                if k < K0 - 1:
                    c.inc(ins)
            ins.then_inc(sel_ready, 1)
            dve.wait_ge(exp_out, 2)
            c.inc(dve.tensor_reduce(stat[:, 0, :], EXs[:, :, :], AX, ALU.add))
            c.inc(dve.tensor_reduce(stat[:, 1, :], R6[0][:, :, :], AX, ALU.add))
            c.wait()
            c.inc(dve.scalar_tensor_tensor(stat[:, 0, :], stat[:, 0, :], 1e-9, stat[:, 1, :], ALU.mult, ALU.add))
            c.wait()
            c.inc(dve.reciprocal(stat[:, 1, :], stat[:, 0, :]))
            c.wait()
            c.inc(dve.tensor_tensor(G6[:, :, :], R6[0][:, :, :], bc(stat[:, 1, :], [P, T, K0], 2), ALU.mult))
            dve.wait_ge(pos_done, 1)
            for j, (t0, t1) in enumerate(POS_CHUNKS):
                w = (t1 - t0) * E0
                c.inc(dve.tensor_copy(POS[:, t0:t1, :].rearrange("p t e -> p (t e)"), banks[j][:, 0:w]))
                c.inc(dve.tensor_copy(TOT[0][:, t0:t1, :].rearrange("p t e -> p (t e)"), banks[4 + j][:, 0:w]))
            c.wait()
            cur = 0
            for sh in (1, 2, 4, 8, 16):
                src, dst = TOT[cur], TOT[1 - cur]
                c.inc(dve.tensor_copy(dst[:, 0:sh, :], src[:, 0:sh, :]))
                c.inc(dve.tensor_tensor(dst[:, sh:T, :], src[:, sh:T, :], src[:, 0:T - sh, :], ALU.add))
                c.wait()
                cur = 1 - cur
            c.inc(dve.tensor_tensor(POS[:, 1:T, :], POS[:, 1:T, :], TOT[cur][:, 0:T - 1, :], ALU.add))
            c.wait()
            for k in range(K0):
                c.inc(dve.tensor_tensor(EXs[:, :, :], OH[:, k, :, :], POS[:, :, :], ALU.mult))
                c.wait()
                c.inc(dve.tensor_reduce(R6[2][:, :, k], EXs[:, :, :], AX, ALU.add))
                c.wait()
            c.inc(dve.tensor_scalar(R6[3][:, :, :], R6[2][:, :, :], float(CAP0), None, ALU.is_lt))
            c.inc(dve.scalar_tensor_tensor(R6[2][:, :, :], R6[1][:, :, :], float(S0), R6[2][:, :, :], ALU.mult, ALU.add))
            c.wait()
            c.inc(dve.tensor_scalar(R6[0][:, :, :], R6[3][:, :, :], -SKIP, SKIP, ALU.mult, ALU.add))
            c.inc(dve.tensor_tensor(R6[1][:, :, :], R6[2][:, :, :], R6[3][:, :, :], ALU.mult))
            c.wait()
            dve.tensor_tensor(DS[:, :, :], R6[2][:, :, :], R6[0][:, :, :], ALU.add).then_inc(rows_ready, 1)
            c.inc(dve.tensor_scalar(R6[3][:, :, :], R6[3][:, :, :], -float(ZROW), float(ZROW), ALU.mult, ALU.add))
            c.wait()
            c.inc(dve.tensor_tensor(DG[:, :, :], R6[1][:, :, :], R6[3][:, :, :], ALU.add))
            end_stage(dve, 2)

            def copy_exT1(k, par, first):
                if not first:
                    dve.wait_ge(exgu_done, 2 * k - 2)
                dve.wait_ge(exT_done, 3 * k + 2)
                dve.tensor_copy(ex_T[par][:, :, 2 * P:4 * P],
                                banks[(par + 1) % 2][:, :].rearrange("p (c n) -> p c n", c=KC)).then_inc(exT_mid, 1)

            def gate_expert(k, par, first):
                if not first:
                    dve.wait_ge(exy_done, 3 * k - 3)
                for h in range(2):
                    dve.wait_ge(exsg_ready, 2 * k + h + 1)
                    dve.tensor_tensor(ex_ac[par][:, cols(h, S0 // 2)], banks[3 + 2 * h][:, 0:S0 // 2],
                                      ex_sg[par][:, cols(h, S0 // 2)], ALU.mult).then_inc(exac_ready, 1)
            pipelined(dve, E0, [(copy_exT1, -1), (gate_expert, 0)])
            end_stage(dve, 3)

            for t in range(T):
                dve.wait_ge(y6_in[t % 4], 16 * K0 * (t // 4 + 1))
                for k in range(K0):
                    ins = dve.scalar_tensor_tensor(X[:, t, :], Y6[t % 4][:, k, :], G6[:, t, k:k + 1], X[:, t, :],
                                                   ALU.mult, ALU.add)
                    if k < K0 - 1:
                        c.inc(ins)
                        c.wait()
                ins.then_inc(y6_used, 1)
            dve.wait_ge(y6_used, T)
            end_stage(dve, 4)

            dve.memset(H[:, :, D:HW], 1.0).then_inc(h_copied, 1)
            layer_norm()

            def xn_group1(k, par, first):
                if not first:
                    dve.wait_ge(gxT_done, k - 1)
                normalise_group(gxg[par], k).then_inc(gxg_ready, 1)

            def copy_h(k, par, first):
                for u in range(GT):
                    dve.wait_ge(h_done, 2 * k + u + 1)
                    c.inc(dve.tensor_copy(H[:, k * GT + u, 0:D], banks[2 + u][:, 0:D]))
                    dve.tensor_copy(SD[:, k * GT + u, :], banks[2 + u][:, D:D + 2]).then_inc(h_copied, 1)
            pipelined(dve, G, [(xn_group1, -1), (copy_h, 0)], c)
            dve.wait_ge(h_copied, T + 1)
            c.wait()
            c.inc(dve.tensor_scalar(H[:, T - 1, D:HW], H[:, T - 1, D:HW], padm[:, 0:1], None, ALU.mult))
            c.inc(dve.tensor_copy(dcol[:, 0, :], SD[:, :, 1]))
            c.inc(dve.tensor_scalar(dcol[:, 1, :], SD[:, :, 1], ALPHA, None, ALU.mult))
            c.inc(dve.tensor_scalar(dcol[:, 2, :], SD[:, :, 1], -1.0, None, ALU.mult))
            c.wait()
            dve.tensor_reduce(SC[:, 0:1], dcol[:, 2, :], AX, ALU.max).then_inc(mn_ready, 1)
            dve.wait_ge(mn_all, 1)
            c.inc(dve.tensor_scalar(dcol[:, 2, :], SD[:, :, 1], SC[:, 1:2], 1.0, ALU.add, ALU.add))
            end_stage(dve, 5)

            dve.wait_ge(hs_done, 1)
            c.inc(dve.tensor_copy(HS[:, 0:D + 1], banks[7][:, 0:D + 1]))
            c.inc(dve.tensor_scalar(acc[:, :], M[:, 0, :], dcol[:, 2, 0:1], None, ALU.mult))
            for j in range(1, T):
                c.wait()
                ins = dve.scalar_tensor_tensor(acc[:, :], M[:, j, :], dcol[:, 2, j:j + 1], acc[:, :], ALU.mult, ALU.max)
                if j < T - 1:
                    c.inc(ins)
            ins.then_inc(acc_ready, 1)
            for j, (o, w) in enumerate(ABLOCKS):
                dve.wait_ge(accT_done, j + 1)
                ins = dve.tensor_reduce(MM[:, 0, o // P:(o + w) // P],
                                        banks[j % 2][:, 0:w].rearrange("p (a b) -> p a b", b=P), AX, ALU.max)
                ins.then_inc(accT_read, 1)
            dve.wait_ge(accT_read, len(ABLOCKS))
            c.inc(dve.tensor_scalar(MM[:, 1, :], MM[:, 0, :], SC[:, 1:2], -1.0, ALU.subtract, ALU.add))
            c.wait()
            c.inc(dve.tensor_tensor(MM[:, 1, :], MM[:, 1, :], SD[:, :, 0], ALU.add))
            c.wait()
            c.inc(dve.scalar_tensor_tensor(MM[:, 2, :], MM[:, 1, :], ALPHA, MM[:, 1, :], ALU.mult, ALU.max))
            c.wait()
            c.inc(dve.tensor_tensor(MM[:, 3, :], SD[:, :, 0], MM[:, 2, :], ALU.subtract))
            c.inc(dve.scalar_tensor_tensor(MM[:, 4, :], SD[:, :, 0], ALPHA, MM[:, 2, :], ALU.mult, ALU.subtract))
            c.wait()
            for k in range(2 * len(ABLOCKS)):
                o, w = ABLOCKS[k // 2]
                if k >= 2:
                    dve.wait_ge(pb_done, k - 1)
                for q in range(w // P):
                    ins = dve.tensor_scalar(dgn[k % 2][:, q, :], ident[:, :],
                                            MM[:, 3 + k % 2, o // P + q:o // P + q + 1], None, ALU.mult)
                    if q < w // P - 1:
                        c.inc(ins)
                ins.then_inc(dgn_ready, 1)
            dve.wait_ge(pb_copied, 2 * len(ABLOCKS))

            for bi, (o, w) in enumerate(ABLOCKS):
                base = T * bi

                def attend_max(k, par, first):
                    dve.wait_ge(at1_ready, k + base + 1)
                    if not first or bi:
                        dve.wait_ge(atp_ready, k + base - 1)
                    dve.scalar_tensor_tensor(at2[par][:, 0:w], QB[:, o:o + w],
                                             dcol[:, 1, bass.ds(k, 1)], at1[par][:, 0:w], ALU.add,
                                             ALU.max).then_inc(at2_ready, 1)

                def attend_mask(k, par, first):
                    dve.wait_ge(ate_ready, k + base + 1)
                    if not first or bi:
                        dve.wait_ge(atp_used, k + base - 1)
                    dve.scalar_tensor_tensor(atp[par][:, 0:w], at2[par][:, 0:w], 1.0, M[:, k, o:o + w], ALU.min,
                                             ALU.mult).then_inc(atp_ready, 1)
                pipelined(dve, T, [(attend_max, 0), (attend_mask, 1)])
                dve.wait_ge(blk_done, bi + 1)
                for q in range(w // P):
                    t = o // P + q
                    src = banks[4 * (bi % 2) + q]
                    nb = num[q % 2]
                    c.inc(dve.tensor_scalar(SC[:, 2:3], src[:, D:D + 1], 0.5, None, ALU.is_lt))
                    c.wait()
                    c.inc(dve.tensor_scalar(nb[:, 0:D + 1], HS[:, 0:D + 1], SC[:, 2:3], None, ALU.mult))
                    c.wait()
                    c.inc(dve.tensor_tensor(nb[:, 0:D + 1], src[:, 0:D + 1], nb[:, 0:D + 1], ALU.add))
                    c.wait()
                    c.inc(dve.reciprocal(SC[:, 3:4], nb[:, D:D + 1]))
                    c.wait()
                    c.inc(dve.scalar_tensor_tensor(X[:, t, :], nb[:, 0:D], SC[:, 3:4], X[:, t, :], ALU.mult, ALU.add))
                    c.wait()
                dve.tensor_copy(SC[:, 4:5], SC[:, 3:4]).then_inc(blk_read, 1)
            end_stage(dve, 6)

            layer_norm()

            def xn_group2(k, par, first):
                if not first:
                    dve.wait_ge(fxT_done, k - 1)
                ins = normalise_group(fxg[par], k)
                ins.then_inc(fxg_ready, 1)
                dve.wait_ge(fxg_ready, k + 1)
                c.inc(dve.tensor_copy(XR[:, cols(k, GT), 0:D],
                                      fxg[par][:, :, :].rearrange("p (t c) b -> p t (c b)", t=GT)))

            def read_gates(k, par, first):
                dve.wait_ge(fl_done, k + 1)
                dve.tensor_copy(AF[:, cols(k, GT), :].rearrange("p t e -> p (t e)"),
                                banks[2 + par][:, 0:GT * E1]).then_inc(fl_read, 1)
            pipelined(dve, G, [(xn_group2, -1), (read_gates, 0)], c)
            dve.wait_ge(fl_read, G)
            c.inc(dve.tensor_reduce(stat[:, 0, :], AF[:, :, :], AX, ALU.max))
            c.wait()
            dve.tensor_tensor(AF[:, :, :], AF[:, :, :], bc(stat[:, 0, :], [P, T, E1], 2),
                              ALU.subtract).then_inc(aff_in, 1)
            dve.wait_ge(aff_out, 1)
            c.inc(dve.tensor_reduce(stat[:, 0, :], AF[:, :, :], AX, ALU.add))
            c.wait()
            c.inc(dve.reciprocal(stat[:, 1, :], stat[:, 0, :]))
            c.wait()
            c.inc(dve.tensor_tensor(AF[:, :, :], AF[:, :, :], bc(stat[:, 1, :], [P, T, E1], 2), ALU.mult))
            c.wait()
            c.inc(dve.tensor_scalar(AF[:, T - 1, :], AF[:, T - 1, :], padm[:, 0:1], padn[:, 0:1], ALU.mult, ALU.add))
            c.wait()
            dve.tensor_copy(XR[:, :, D:XW], AF[:, :, :]).then_inc(xr_ready, 1)

            c.inc(dve.memset(thr[:, :], 0))
            c.inc(dve.memset(biti[:, :], 1 << TOP_BIT))
            c.inc(dve.memset(bitf[:, :], float(1 << TOP_BIT)))
            c.wait()

            def one_bit(i):
                c.inc(dve.tensor_tensor(cand[:, :], thr[:, :], biti[:, :], ALU.bitwise_or))
                c.wait()
                c.inc(dve.tensor_tensor(F1[:, :, :], AF[:, :, :], bc(cand[:, :].bitcast(F32), [P, T, E1], 1), ALU.is_ge))
                c.wait()
                dve.tensor_reduce(cnt[:, :], F1[:, :, :].rearrange("p t e -> p e t"), AX, ALU.add).then_inc(cmp_ready, 1)
                dve.wait_ge(cnt_done, i + 1)
                c.inc(dve.scalar_tensor_tensor(stepi[:, :], banks[4][:, 0:E1], float(CAP1), bitf[:, :], ALU.is_ge,
                                               ALU.mult))
                c.inc(dve.tensor_scalar(biti[:, :], biti[:, :], 1, None, ALU.logical_shift_right))
                c.wait()
                c.inc(dve.tensor_scalar(bitf[:, :], bitf[:, :], 0.5, None, ALU.mult))
                c.inc(dve.tensor_tensor(thr[:, :], thr[:, :], stepi[:, :], ALU.bitwise_or))
                c.wait()
            each(dve, TOP_BIT + 1, one_bit, c, 6)

            tb = bc(thr[:, :].bitcast(F32), [P, T, E1], 1)
            c.inc(dve.tensor_tensor(F1[:, :, :], AF[:, :, :], tb, ALU.is_gt))
            c.inc(dve.tensor_tensor(F2[:, :, :], AF[:, :, :], tb, ALU.is_equal))
            c.wait()
            c.inc(dve.tensor_reduce(cnt[:, :], F1[:, :, :].rearrange("p t e -> p e t"), AX, ALU.add))
            c.wait()

            def prefix(src, dst, n):
                dve.tensor_copy(S16[:, :, :], src[:, :, :]).then_inc(sel1_ready, 1)
                dve.wait_ge(sel1_done, n)
                w = T * E1
                c.inc(dve.tensor_copy(dst[:, :, :].rearrange("p t e -> p (t e)"), banks[5][:, 0:w]))
                c.inc(dve.tensor_copy(F3[:, :, :].rearrange("p t e -> p (t e)"), banks[6][:, 0:w]))
                c.wait()

                def add_tile(t):
                    c.inc(dve.tensor_tensor(dst[:, bass.ds(t + 1, 1), :], dst[:, bass.ds(t + 1, 1), :],
                                            F3[:, bass.ds(t, 1), :], ALU.add))
                    c.inc(dve.tensor_tensor(F3[:, bass.ds(t + 1, 1), :], F3[:, bass.ds(t + 1, 1), :],
                                            F3[:, bass.ds(t, 1), :], ALU.add))
                    c.wait()
                each(dve, T - 1, add_tile, c, 2)

            prefix(F2, SL, 1)
            c.inc(dve.tensor_tensor(SL[:, :, :], SL[:, :, :], bc(banks[7][:, 0:E1], [P, T, E1], 1), ALU.add))
            c.wait()
            c.inc(dve.scalar_tensor_tensor(SL[:, :, :], SL[:, :, :], float(CAP1), F2[:, :, :], ALU.is_lt, ALU.mult))
            c.wait()
            c.inc(dve.tensor_tensor(F1[:, :, :], F1[:, :, :], SL[:, :, :], ALU.add))
            c.wait()
            prefix(F1, SL, 2)
            c.inc(dve.scalar_tensor_tensor(SL[:, :, :], SL[:, :, :], 1.0, F1[:, :, :], ALU.add, ALU.mult))
            c.wait()
            c.inc(dve.tensor_scalar(SL[:, :, :], SL[:, :, :], -1.0, None, ALU.add))
            c.wait()

            for e in range(E1):
                def one_hot(t, par, first):
                    if not first or e:
                        dve.wait_ge(oh_used, t + T * e - 1)
                    dve.tensor_scalar(oh1[par][:, :], slots16[:, :], SL[:, t, e:e + 1], None,
                                      ALU.is_equal).then_inc(oh_ready, 1)
                pipelined(dve, T, [(one_hot, 0)])
                dve.wait_ge(lt_done, e + 1)
                for b in range(B1):
                    ins = dve.tensor_copy(LT[:, e, b, :], banks[b][:, 0:2])
                    if b < B1 - 1:
                        c.inc(ins)
                ins.then_inc(lt_read, 1)
            dve.wait_ge(lt_read, E1)
            c.wait()
            c.inc(dve.scalar_tensor_tensor(LI[:, :, :], LT[:, :, :, 0], float(P), LT[:, :, :, 1], ALU.mult, ALU.add))
            c.wait()
            c.inc(dve.tensor_copy(GI[:, :, :], LI[:, :, :]))
            c.inc(dve.tensor_tensor(SI[:, :, :], LI[:, :, :], bc(tail[:, :], [P, E1, B1], 1), ALU.add))
            end_stage(dve, 7)

            def copy_fT(k, par, first):
                if not first:
                    dve.wait_ge(fh_done, 2 * k - 2)
                for j in range(2):
                    dve.wait_ge(fT_done, 2 * k + j + 1)
                    dve.tensor_copy(fT[par][:, :, cols(j, 2 * P)],
                                    banks[j][:, :].rearrange("p (c n) -> p c n", c=KC)).then_inc(fT_read, 1)

            def weigh(k, par, first):
                if not first:
                    dve.wait_ge(y_out, (k - 1) * (16 * B1))
                for b in range(B1):
                    dve.wait_ge(fy_done, 2 * k + b // 2 + 1)
                    ins = dve.tensor_scalar(fy[par][:, b, :], banks[4 + 2 * par + b // 2][:, cols(b % 2, D)],
                                            fx[par][:, b, bass.ds(k + D, 1)], None, ALU.mult)
                    if b < B1 - 1:
                        c.inc(ins)
                ins.then_inc(fy_ready, 1)
            pipelined(dve, E1, [(copy_fT, 0), (weigh, 0)], c)
            end_stage(dve, 8)

        @block.tensor
        def _(pe):
            pe.wait_ge(consts, 12)
            pe.wait_ge(w0_in, 80)
            for which, (wT, bank) in enumerate(((WselfT, banks[6]), (WnbT, banks[7]))):
                for dc in range(KC):
                    for mc in range(KC):
                        mm = pe.matmul(bank[:, cols(dc, D)], wT[:, mc, cols(dc, P)], Wc[:, which * KC + mc, :],
                                       start=(mc == 0), stop=(mc == KC - 1))
                mm.then_inc(fold_done, 1)
            for which in range(2):
                for mc in range(KC):
                    mm = pe.matmul(banks[5][0:1, 0:D], bsn[:, which, mc:mc + 1], Wc[:, which * KC + mc, :],
                                   start=(which + mc == 0), stop=(which + mc == KC))
            mm.then_inc(fold_done, 1)
            pe.wait_ge(fold_copied, 3)
            pe.wait_ge(xs_ready, 1)

            def aggregate(k, par, first, half):
                if half == 0:
                    pe.wait_ge(mask_ready, k + 1)
                    if not first:
                        pe.wait_ge(sa_ready, k - 1)
                for j in range(half * T // 2, (half + 1) * T // 2):
                    halves = ((D + 1, HI), (D, LO)) if j == 0 else ((D, LO), (D + 1, HI))
                    for n, (w, o) in enumerate(halves):
                        mm = pe.matmul(banks[par][:, 0:w], mt[par][:, j, :], XS[:, j, o:o + w],
                                       start=(j == 0 and n == 0), stop=(j == T - 1 and n == 1), skip_group_check=True)
                if half == 1:
                    mm.then_inc(agg_done, 1)

            def turn0(k, par, first):
                pe.wait_ge(sa_ready, k + 1)
                if not first:
                    pe.wait_ge(saT_copied, k - 1)
                for j in range(2 * KC):
                    mm = pe.transpose(banks[2 + par][:, cols(j, P)], sa[par][:, j, :], ident[:, :])
                mm.then_inc(saT_done, 1)

            def combine(k, par, first):
                pe.wait_ge(saT_copied, k + 1)
                if not first:
                    pe.wait_ge(x1_ready, k - 1)
                for j in range(2 * KC):
                    pe.matmul(banks[4 + par][:, 0:D], saT[par][:, j, :], WF[:, j, :], start=(j == 0), stop=False)
                pe.matmul(banks[4 + par][:, 0:D], ones[0:1, :], BF[:, :], start=False, stop=True).then_inc(comb_done, 1)
            pipelined(pe, T, [(lambda k, par, first: aggregate(k, par, first, 0), 0), (turn0, 1),
                              (lambda k, par, first: aggregate(k, par, first, 1), 0), (combine, 1)])
            end_stage(pe, 1)

            pe.wait_ge(w1_in, 64)

            def turn_group(xgb, ready, done, read, k, par, first):
                pe.wait_ge(ready, k + 1)
                if not first:
                    pe.wait_ge(read, k - 1)
                for ch in range(KC):
                    for u in range(GT):
                        mm = pe.transpose(banks[par][:, cols(ch * GT + u, P)], xgb[par][:, u * KC + ch, :], ident[:, :])
                mm.then_inc(done, 1)

            def turn1(k, par, first):
                turn_group(xg, xg_ready, xT_done, xT_copied, k, par, first)

            def shared(k, par, first):
                pe.wait_ge(xT_copied, k + 1)
                if k is not 0 and not (isinstance(k, int) and k < 1):
                    pe.wait_ge(lg_read, k)
                for u in range(GT):
                    for ch in range(KC):
                        pe.matmul(banks[2][:, cols(u, E0)], xT[par][:, ch, cols(u, P)], rw[:, ch, :], start=(ch == 0),
                                  stop=False, skip_group_check=True)
                    mm = pe.matmul(banks[2][:, cols(u, E0)], ones[0:1, :], rb[:, :], start=False, stop=True,
                                   skip_group_check=True)
                mm.then_inc(lg_done, 1)
                for s in range(SH):
                    if not (isinstance(k, int) and k < 1):
                        pe.wait_ge(acs_ready, 2 * k - 1 + s)
                    for gu in range(2):
                        for ch in range(KC):
                            mm = pe.matmul(banks[3 + s][:, cols(gu, GW)], sgu[:, s, gu, ch, :], xT[par][:, ch, :],
                                           start=(ch == 0), stop=(ch == KC - 1), skip_group_check=True)
                    mm.then_inc(hgu_done, 1)

            def shared_down(k, par, first):
                pe.wait_ge(acs_ready, 2 * k + 2)
                if not first:
                    pe.wait_ge(sd_read, k - 1)
                for u in range(GT):
                    for s in range(SH):
                        mm = pe.matmul(banks[5 + par][:, cols(u, D)], acs[par][:, s, cols(u, P)], sdn[:, s, :],
                                       start=(s == 0), stop=(s == SH - 1))
                mm.then_inc(sd_done, 1)
            pipelined(pe, G, [(turn1, -1), (shared, 0), (shared_down, 0)])
            pe.wait_ge(sel_ready, 1)
            pe.wait_ge(sd_read, G)
            pe.wait_ge(lg_read, G)
            sel16 = TOT[0][:, :, :].bitcast(BF16)[:, :, 0:E0]
            for j, (t0, t1) in enumerate(POS_CHUNKS):
                w = (t1 - t0) * E0
                pe.matmul(banks[j][:, 0:w], before[:, :], sel16[:, t0:t1, :], start=True, stop=True)
                mm = pe.matmul(banks[4 + j][:, 0:w], ones16[:, :], sel16[:, t0:t1, :], start=True, stop=True)
            mm.then_inc(pos_done, 1)
            end_stage(pe, 2)

            def turn_expert(k, par, first):
                pe.wait_ge(exin[par], (k - par) * 8 + 16)
                for j in range(3):
                    nb = min(2, B0 - 2 * j)
                    if j == 2:
                        pe.wait_ge(exT_copied, 2 * k + 1)
                    elif not (isinstance(k, int) and k == 0):
                        pe.wait_ge((exT_mid, exT_copied)[j], k if j == 0 else 2 * k)
                    for ch in range(KC):
                        for u in range(nb):
                            mm = pe.transpose(banks[(par + j) % 2][:, cols(ch * nb + u, P)],
                                              ex_in[par][:, 2 * j + u, cols(ch, P)], ident[:, :])
                    mm.then_inc(exT_done, 1)

            def up_expert(k, par, first):
                pe.wait_ge(exw[par], (k - par) * 8 + 16)
                pe.wait_ge(exT_copied, 2 * k + 2)
                pe.wait_ge(exT_mid, k + 1)
                for h in range(2):
                    if not (isinstance(k, int) and k < 1):
                        pe.wait_ge(exac_ready, 2 * k - 1 + h)
                    for gu in range(2):
                        for ch in range(KC):
                            mm = pe.matmul(banks[2 + 2 * h + gu][:, 0:S0 // 2], ex_w[par][:, cols(gu * KC + ch, P)],
                                           ex_T[par][:, ch, cols(h, S0 // 2)], start=(ch == 0), stop=(ch == KC - 1))
                    mm.then_inc(exgu_done, 1)

            def down_expert(k, par, first):
                pe.wait_ge(exac_ready, 2 * k + 2)
                for j in range(3):
                    if not (isinstance(k, int) and k == 0 and j < 2):
                        pe.wait_ge(exy_copied, 3 * k + j - 1)
                    for u in range(min(2, B0 - 2 * j)):
                        mm = pe.matmul(banks[6 + (par + j) % 2][:, cols(u, D)],
                                       ex_ac[par][:, cols(2 * j + u, P)], ex_w[par][:, 4 * P:6 * P],
                                       start=True, stop=True)
                    mm.then_inc(exy_done, 1)
            pipelined(pe, E0, [(up_expert, 0), (turn_expert, -1), (down_expert, 0)])
            end_stage(pe, 3)
            end_stage(pe, 4)

            pe.wait_ge(w2_in, 48)
            for dc in range(KC):
                for oc in range(KC):
                    mm = pe.matmul(banks[7][:, cols(dc, 2)], Wn[:, oc, cols(dc, P)], a12[:, oc, :],
                                   start=(oc == 0), stop=(oc == KC - 1))
            mm.then_inc(va_done, 1)
            pe.wait_ge(va_copied, 1)

            def turn2(k, par, first):
                turn_group(gxg, gxg_ready, gxT_done, gxT_copied, k, par, first)

            def features(k, par, first):
                pe.wait_ge(gxT_copied, k + 1)
                for u in range(GT):
                    if not (isinstance(k, int) and k < 1):
                        pe.wait_ge(h_copied, 2 * k + u)
                    for ch in range(KC):
                        mm = pe.matmul(banks[2 + u][:, 0:D + 2], gxT[par][:, ch, cols(u, P)], W2[:, ch, :],
                                       start=(ch == 0), stop=(ch == KC - 1))
                    mm.then_inc(h_done, 1)
            pipelined(pe, G, [(turn2, -1), (features, 0)])
            end_stage(pe, 5)

            for j in range(T):
                mm = pe.matmul(banks[7][:, 0:D + 2], ones[:, :], H[:, j, 0:D + 2], start=(j == 0), stop=(j == T - 1))
            mm.then_inc(hs_done, 1)
            pe.wait_ge(acc_ready, 1)
            for j, (o, w) in enumerate(ABLOCKS):
                if j >= 2:
                    pe.wait_ge(accT_read, j - 1)
                for q in range(w // P):
                    mm = pe.transpose(banks[j % 2][:, cols(q, P)], acc[:, o + q * P:o + (q + 1) * P], ident[:, :])
                mm.then_inc(accT_done, 1)
            pe.wait_ge(accT_read, len(ABLOCKS))
            for k in range(2 * len(ABLOCKS)):
                o, w = ABLOCKS[k // 2]
                pe.wait_ge(dgn_ready, k + 1)
                if k >= 2:
                    pe.wait_ge(pb_copied, k - 1)
                for q in range(w // P):
                    mm = pe.matmul(banks[k % 2][:, cols(q, P)], ones[:, :], dgn[k % 2][:, q, :], start=True, stop=True)
                mm.then_inc(pb_done, 1)
            pe.wait_ge(pb_copied, 2 * len(ABLOCKS))
            for bi, (o, w) in enumerate(ABLOCKS):
                if bi >= 2:
                    pe.wait_ge(blk_read, bi - 1)

                def attend(k, par, first):
                    pe.wait_ge(atp_ready, k + T * bi + 1)
                    for q in range(w // P):
                        mm = pe.matmul(banks[4 * (bi % 2) + q][:, 0:D + 1], atp[par][:, cols(q, P)], H[:, k, 0:D + 1],
                                       start=(isinstance(k, int) and k == 0), stop=(isinstance(k, int) and k == T - 1),
                                       skip_group_check=True)
                    mm.then_inc(atp_used, 1)
                pipelined(pe, T, [(attend, 0)])
                pe.wait_ge(atp_used, T * (bi + 1))
                pe.drain().then_inc(blk_done, 1)
            end_stage(pe, 6)

            pe.wait_ge(w3_in, 48)

            def turn3(k, par, first):
                turn_group(fxg, fxg_ready, fxT_done, fxT_copied, k, par, first)

            def gates(k, par, first):
                pe.wait_ge(fxT_copied, k + 1)
                if not first:
                    pe.wait_ge(fl_read, k - 1)
                for u in range(GT):
                    for ch in range(KC):
                        mm = pe.matmul(banks[2 + par][:, cols(u, E1)], fxT[par][:, ch, cols(u, P)], gw[:, ch, :],
                                       start=(ch == 0), stop=(ch == KC - 1), skip_group_check=True)
                mm.then_inc(fl_done, 1)
            pipelined(pe, G, [(turn3, -1), (gates, 0)])
            with pe.Fori(0, TOP_BIT + 1) as i:
                pe.wait_ge(cmp_ready, i + 1)
                pe.matmul(banks[4][:, 0:E1], ones[:, :], cnt[:, :], start=True, stop=True).then_inc(cnt_done, 1)
            w = T * E1
            for n in range(2):
                pe.wait_ge(sel1_ready, n + 1)
                pe.matmul(banks[5][:, 0:w], before[:, :], S16[:, :, :].rearrange("p t e -> p (t e)"),
                          start=True, stop=True)
                mm = pe.matmul(banks[6][:, 0:w], ones16[:, :], S16[:, :, :].rearrange("p t e -> p (t e)"),
                               start=True, stop=True)
                if n == 0:
                    mm = pe.matmul(banks[7][:, 0:E1], ones[:, :], cnt[:, :], start=True, stop=True)
                mm.then_inc(sel1_done, 1)
            for e in range(E1):
                if e:
                    pe.wait_ge(lt_read, e)

                def place(t, par, first):
                    pe.wait_ge(oh_ready, t + T * e + 1)
                    for b in range(B1):
                        mm = pe.matmul(banks[b][:, 0:2], oh1[par][:, cols(b, P)], tokp[:, t, :],
                                       start=(isinstance(t, int) and t == 0), stop=(isinstance(t, int) and t == T - 1),
                                       skip_group_check=True)
                    mm.then_inc(oh_used, 1)
                pipelined(pe, T, [(place, 0)])
                pe.drain().then_inc(lt_done, 1)
            end_stage(pe, 7)

            pe.wait_ge(w3_in, 48)

            def turn_rows(k, par, first):
                pe.wait_ge(fx_in[par], (k - par) * (8 * B1) + 16 * B1)
                for j in range(2):
                    if not (isinstance(k, int) and k < 1):
                        pe.wait_ge(fT_read, 2 * k + j - 1)
                    for ch in range(KC):
                        for u in range(2):
                            mm = pe.transpose(banks[j][:, cols(ch * 2 + u, P)], fx[par][:, 2 * j + u, cols(ch, P)],
                                              ident[:, :])
                    mm.then_inc(fT_done, 1)

            def hidden(k, par, first):
                pe.wait_ge(fw_in[par], (k - par) * 8 + 16)
                pe.wait_ge(fT_read, 2 * k + 2)
                for h in range(KC):
                    if not (isinstance(k, int) and k < 1):
                        pe.wait_ge(fh_ready, 2 * k - 1 + h)
                    for ch in range(KC):
                        mm = pe.matmul(banks[2 + h][:, :], w12[par][:, ch, cols(h, P)], fT[par][:, ch, :],
                                       start=(ch == 0), stop=(ch == KC - 1))
                    mm.then_inc(fh_done, 1)

            def outputs(k, par, first):
                pe.wait_ge(fh_ready, 2 * k + 2)
                if not first:
                    pe.wait_ge(fy_ready, k - 1)
                for b in range(B1):
                    for h in range(KC):
                        pe.matmul(banks[4 + 2 * par + b // 2][:, cols(b % 2, D)], fh[par][:, h, cols(b, P)],
                                  w12[par][:, KC + h, :], start=(h == 0), stop=False, skip_group_check=True)
                    mm = pe.matmul(banks[4 + 2 * par + b // 2][:, cols(b % 2, D)], ones[0:1, :], b2r[:, k, :],
                                   start=False, stop=True, skip_group_check=True)
                    if b % 2:
                        mm.then_inc(fy_done, 1)
            pipelined(pe, E1, [(turn_rows, 0), (hidden, 0), (outputs, 0)])
            end_stage(pe, 8)


def kernel(**inputs):
    import numpy as np
    import concourse.bacc as bacc
    from concourse.bass_utils import run_bass_kernel_spmd

    def arr(name):
        return np.asarray(inputs[name])

    def kmaj(w):
        return w.reshape(-1, P, w.shape[1]).transpose(1, 0, 2)

    g0, f0, g1, f1 = "L0_gnn_", "L0_ffn_", "L1_gnn_", "L1_ffn_"
    x = np.pad(arr("x"), ((0, NP - N), (0, 0)))
    adj = np.pad(arr("adj"), ((0, NP - N), (0, NP - N)))
    gate, up, down = (arr(f0 + n).transpose(0, 2, 1) for n in ("w_gate", "w_up", "w_down"))
    sgate, sup, sdown = (arr(f0 + n).transpose(0, 2, 1) for n in ("shared_w_gate", "shared_w_up", "shared_w_down"))

    def two(w):
        return w.reshape(w.shape[0], -1, P, w.shape[2]).transpose(0, 2, 1, 3)

    arrays = {
        "x": x.reshape(T, P, D).transpose(1, 0, 2),
        "adj": adj.reshape(T, P, T, P).transpose(0, 3, 2, 1),
        "W_self_T": kmaj(arr(g0 + "W_self").T),
        "W_nb_T": kmaj(arr(g0 + "W_nb").T),
        "W_comb": kmaj(arr(g0 + "W_comb")),
        "b_self_nb": np.stack([arr(g0 + "b_self"), arr(g0 + "b_nb")]).reshape(2, KC, P).transpose(2, 0, 1),
        "b_comb": arr(g0 + "b_comb").reshape(1, D),
        "router_w": kmaj(arr(f0 + "router_w").T),
        "router_b": arr(f0 + "bias").reshape(1, E0),
        "shared_gate_up": np.stack([two(sgate), two(sup)], 1).transpose(2, 0, 1, 3, 4),
        "shared_down": sdown.transpose(1, 0, 2),
        "experts0": np.concatenate([two(gate).reshape(E0, P, D), two(up).reshape(E0, P, D), down], 2),
        "W_T": kmaj(arr(g1 + "W").T),
        "W": kmaj(arr(g1 + "W")),
        "a12": kmaj(np.stack([arr(g1 + "a1"), arr(g1 + "a2")], 1)),
        "gate_w": kmaj(arr(f1 + "gate_weight")),
        "experts1": np.concatenate([two(arr(f1 + "w1")), two(arr(f1 + "w2"))], 2),
        "b1": arr(f1 + "b1").reshape(E1, KC, P).transpose(2, 0, 1),
        "b2": arr(f1 + "b2").reshape(1, E1, D),
    }
    nc = bacc.Bacc("TRN2", target_bir_lowering=False, num_devices=1)
    feeds, aps = {}, {}
    for name, a in arrays.items():
        a = np.ascontiguousarray(a)
        feeds[f"in_{name}"] = a
        aps[name] = nc.dram_tensor(f"in_{name}", a.shape, mybir.dt.from_np(a.dtype), kind="ExternalInput").ap()
    out = nc.dram_tensor("out", (N, D), F32, kind="ExternalOutput").ap()
    xbuf = nc.dram_tensor("xbuf", (E0 * S0, D), F32, kind="Internal").ap()
    ybuf = nc.dram_tensor("ybuf", (E0 * S0 + 1, D), F32, kind="Internal").ap()
    rbuf = nc.dram_tensor("rbuf", (NP, XW), F32, kind="Internal").ap()
    build(nc, aps, out, xbuf, ybuf, rbuf)
    return run_bass_kernel_spmd(nc, [feeds], core_ids=[0]).results[0]["out"]
```

```python
from contextlib import ExitStack

import concourse.bass as bass
from concourse import mybir

P = 128
N = 3327
D = 256
KC = D // P
T = (N + P - 1) // P
NP = T * P
PAD = N - (T - 1) * P
GT = 2
G = T // GT
GW = GT * P
EPS = 1e-5

E0, K0, SH = 64, 6, 2
CAP0 = max(1, int(N * K0 * 2.0 / E0))
B0 = (CAP0 + P - 1) // P
S0 = B0 * P
ZROW = E0 * S0
SKIP = 65536.0

E1 = 16
CAP1 = N // E1 * 2
B1 = (CAP1 + P - 1) // P
S1 = B1 * P
XW = D + E1
TOP_BIT = 29

HT = T // 2

AW = 512
ABLOCKS = [(o, min(AW, NP - o)) for o in range(0, NP, AW)]
ALPHA = 0.2

F32, F16, BF16 = mybir.dt.float32, mybir.dt.float16, mybir.dt.bfloat16
I32, U32, U8 = mybir.dt.int32, mybir.dt.uint32, mybir.dt.uint8
ALU, ACT = mybir.AluOpType, mybir.ActivationFunctionType
AX = mybir.AxisListType.X
MAXR = bass.bass_isa.ReduceOp.max

HI, ONE, LO, XSW = 0, D, D + 2, 2 * D + 2
HW = D + 4


class Chain:

    def __init__(self, eng, sem):
        self.eng, self.sem, self.n, self.loop = eng, sem, 0, None

    def inc(self, ins):
        ins.then_inc(self.sem, 1)
        self.n += 1

    def wait(self):
        if self.loop is None:
            self.eng.wait_ge(self.sem, self.n)
        else:
            i, per = self.loop
            self.eng.wait_ge(self.sem, i * per + self.n)


def pipelined(eng, n, parts, chain=None):
    late = max(off for _, off in parts)
    early = min(off for _, off in parts)

    def step(s, base=None):
        for fn, off in parts:
            k = s - off
            if base is not None:
                fn(base + k, k % 2, False)
            elif 0 <= k < n:
                fn(k, k % 2, k < 2)

    lo, hi = late + 2, n + early
    pairs = max((hi - lo) // 2, 0)
    before = 0
    for s in range(early, lo):
        before = chain.n if chain else 0
        step(s)
    if pairs > 1:
        if chain:
            per, start = chain.n - before, chain.n
        with eng.Fori(0, pairs) as i:
            if chain:
                chain.loop = (i, 2 * per)
            step(lo, base=i * 2)
            step(lo + 1, base=i * 2)
        if chain:
            assert chain.n == start + 2 * per, (chain.n, start, per)
            chain.loop = None
            chain.n = start + 2 * per * pairs
        lo += 2 * pairs
    for s in range(lo, n + late):
        step(s)


def each(eng, n, fn, chain, per):
    start = chain.n
    with eng.Fori(0, n) as i:
        chain.loop = (i, per)
        fn(i)
    assert chain.n == start + per
    chain.loop = None
    chain.n = start + per * n


def cols(k, width):
    return bass.ds(k * width, width)


def bc(ap, shape, axis):
    return ap.unsqueeze(axis).broadcast_to(shape)


def build(nc, d, out, ids, nbuf, ybuf, rbuf):
    top = ExitStack()
    with top:
        def sem(name):
            return top.enter_context(nc.semaphore(name))

        def sems(name, n):
            return [sem(f"{name}{i}") for i in range(n)]

        def stage():
            ctx = ExitStack()
            return ctx, lambda name, shape, dt: ctx.enter_context(nc.sbuf_tensor(name, shape, dt))

        banks = [top.enter_context(nc.psum_tensor(f"bank{i}", [P, 512], F32)) for i in range(8)]

        _ctx, sb = stage()
        top.enter_context(_ctx)
        X = sb("X", [P, T, D], F32)
        ident = sb("ident", [P, P], F32)
        ones = sb("ones", [P, P], F32)
        ones16 = sb("ones16", [P, P], BF16)
        before = sb("before", [P, P], BF16)
        notbefore = sb("notbefore", [P, P], BF16)
        bn = sb("bn", [P, T, 6], F32)
        mean = sb("mean", [P, T], F32)
        rstd = sb("rstd", [P, T], F32)
        stat = sb("stat", [P, 3, T], F32)
        iota64 = sb("iota64", [P, E0], F32)
        slots16 = sb("slots16", [P, S1], F16)
        tokp = sb("tokp", [P, T, 2], F16)
        padm = sb("padm", [P, 1], F32)
        padn = sb("padn", [P, 1], F32)
        tail = sb("tail", [P, B1], F32)
        tokens = sb("tokens", [P, T], U32)
        LG = sb("LG", [P, T, E0], F32)
        MX8 = sb("MX8", [P, T, 8], F32)
        VAL = sb("VAL", [P, T, K0], F32)
        DS = sb("DS", [P, T, K0], U32)
        G6 = sb("G6", [P, T, K0], F32)
        DG = sb("DG", [P, T, K0], U32)
        SC = sb("SC", [P, 64], F32)

        m_ctx, sb = stage()
        M = sb("M", [P, T, NP], U8)

        ctx, sb = stage()
        XS = sb("XS", [P, T, XSW], F16)
        adj = [sb(f"adj{i}", [P, HT, P], I32) for i in range(2)]
        mt = [sb(f"mt{i}", [P, T, P], F16) for i in range(2)]
        bsn = sb("bsn", [P, 2, KC], F32)
        bcomb = sb("bcomb", [1, D], F32)
        WF = sb("WF", [P, 2 * KC, D], F32)
        BF = sb("BF", [1, D], F32)
        dg = [sb(f"dg{i}", [P, 2], F32) for i in range(2)]
        sa = [sb(f"sa{i}", [P, 2 * KC, P], F32) for i in range(2)]
        saT = [sb(f"saT{i}", [P, 2 * KC, P], F32) for i in range(2)]
        WselfT, WnbT = (buf[:, :, :].rearrange("p (c x) b -> p c (x b)", c=KC) for buf in sa)
        Wc = [buf[:, :, :].rearrange("p (c x) b -> p c (x b)", c=KC) for buf in saT]
        xn0 = [sb(f"xn0{i}", [P, D], F32) for i in range(2)]
        bnb = [sb(f"bnb{i}", [P, 6], F32) for i in range(2)]
        mv = [sb(f"mv{i}", [P, 2], F32) for i in range(2)]
        sd = [sb(f"sd{i}", [P, 2], F32) for i in range(2)]
        xnb = [sb(f"xnb{i}", [P, KC, P], F32) for i in range(2)]
        xTb = [sb(f"xTb{i}", [P, KC, P], F32) for i in range(2)]
        lgb = [sb(f"lgb{i}", [P, E0], F32) for i in range(2)]
        mx8b = [sb(f"mx8b{i}", [P, 8], F32) for i in range(2)]
        ix8b = [sb(f"ix8b{i}", [P, 8], U32) for i in range(2)]
        OH = [sb(f"OH{i}", [P, K0, E0], BF16) for i in range(2)]
        OHP = sb("OHP", [P, K0, E0], F32)
        r6 = sb("r6", [P, 4, K0], F32)
        rw = sb("rw", [P, KC, E0], F32)
        rb = sb("rb", [1, E0], F32)
        zero = sb("zero", [P, 320], U32)
        ctx.close()

        ctx, sb = stage()
        EI = sb("EI", [P, E0, B0], U32)
        EXs = sb("EXs", [P, T, E0], F32)
        EX6 = sb("EX6", [P, T, K0], F32)
        zrow = sb("zrow", [1, D], F32)
        ex_in = [sb(f"ex_in{i}", [P, B0, D], F32) for i in range(2)]
        ex_w = [sb(f"ex_w{i}", [P, 2 * KC, P], F32) for i in range(2)]
        ex_wd = [sb(f"ex_wd{i}", [P, D], F32) for i in range(2)]
        ex_T = [sb(f"ex_T{i}", [P, KC, S0], F32) for i in range(2)]
        ex_sg = [sb(f"ex_sg{i}", [P, S0], F32) for i in range(2)]
        ex_ac = [sb(f"ex_ac{i}", [P, S0], F32) for i in range(2)]
        ex_y = [sb(f"ex_y{i}", [P, B0, D], F32) for i in range(2)]
        ctx.close()
        ctx, sb = stage()
        Y6 = [sb(f"Y6{i}", [P, K0, D], F32) for i in range(4)]
        xg = [sb(f"xg{i}", [P, GT * KC, P], F32) for i in range(2)]
        xT = [sb(f"xT{i}", [P, KC, GW], F32) for i in range(2)]
        sgs = [sb(f"sgs{i}", [P, SH, GW], F32) for i in range(2)]
        acs = [sb(f"acs{i}", [P, SH, GW], F32) for i in range(2)]
        sgu = sb("sgu", [P, SH, 2, KC, P], F32)
        sdn = sb("sdn", [P, SH, D], F32)
        ctx.close()

        ctx, sb = stage()
        H = sb("H", [P, T, HW], F32)
        SD = sb("SD", [P, T, 2], F32)
        dcol = sb("dcol", [P, 3, T], F32)
        HS = sb("HS", [P, D + 2], F32)
        W2 = sb("W2", [P, KC, D + 2], F32)
        in1, sb = stage()
        gxg = [sb(f"gxg{i}", [P, GT * KC, P], F32) for i in range(2)]
        gxT = [sb(f"gxT{i}", [P, KC, GW], F32) for i in range(2)]
        Wn = sb("Wn", [P, KC, D], F32)
        a12 = sb("a12", [P, KC, 2], F32)
        in1.close()
        PB = sb_keep = None
        in1, sb = stage()
        PB = sb("PB", [P, NP], F32)
        QB = sb("QB", [P, NP], F32)
        MM = sb("MM", [P, 6, T], F32)
        in2, sb = stage()
        acc = sb("acc", [P, NP], F32)
        dgn = [sb(f"dgn{i}", [P, 4, P], F32) for i in range(2)]
        in2.close()
        in2, sb = stage()
        at1 = [sb(f"at1{i}", [P, AW], F32) for i in range(2)]
        at2 = [sb(f"at2{i}", [P, AW], F32) for i in range(2)]
        atp = [sb(f"atp{i}", [P, AW], F32) for i in range(2)]
        num = [sb(f"num{i}", [P, D + 2], F32) for i in range(2)]
        in2.close()
        in1.close()
        ctx.close()
        m_ctx.close()

        ctx, sb = stage()
        XR = sb("XR", [P, T, XW], F32)
        AF = sb("AF", [P, T, E1], F32)
        fxg = [sb(f"fxg{i}", [P, GT * KC, P], F32) for i in range(2)]
        fxT = [sb(f"fxT{i}", [P, KC, GW], F32) for i in range(2)]
        gw = sb("gw", [P, KC, E1], F32)
        F1 = sb("F1", [P, T, E1], F32)
        F2 = sb("F2", [P, T, E1], F32)
        F3 = sb("F3", [P, T, E1], F32)
        SL = sb("SL", [P, T, E1], F32)
        S16 = sb("S16", [P, T, E1], BF16)
        thr = sb("thr", [P, E1], I32)
        cand = sb("cand", [P, E1], I32)
        stepi = sb("stepi", [P, E1], I32)
        biti = sb("biti", [P, E1], I32)
        bitf = sb("bitf", [P, E1], F32)
        cnt = sb("cnt", [P, E1], F32)
        oh1 = [sb(f"oh1{i}", [P, S1], F16) for i in range(2)]
        LT = sb("LT", [P, E1, B1, 2], F32)
        LI = sb("LI", [P, E1, B1], F32)
        GI = sb("GI", [P, E1, B1], U32)
        SI = sb("SI", [P, E1, B1], U32)
        in1, sb = stage()
        w12 = [sb(f"w12{i}", [P, 2 * KC, D], F32) for i in range(2)]
        b1c = sb("b1c", [P, E1, KC], F32)
        b2r = sb("b2r", [1, E1, D], F32)
        fx = [sb(f"fx{i}", [P, B1, XW], F32) for i in range(2)]
        fT = [sb(f"fT{i}", [P, KC, S1], F32) for i in range(2)]
        fh = [sb(f"fh{i}", [P, KC, S1], F32) for i in range(2)]
        fy = [sb(f"fy{i}", [P, B1, D], F32) for i in range(2)]
        in1.close()
        ctx.close()

        stage_end = sem("stage_end")
        dve_done, act_done, pool_done = sem("dve_done"), sem("act_done"), sem("pool_done")
        x_in, w0_in, adj_in = sem("x_in"), sem("w0_in"), sems("adj_in", 2)
        consts = sem("consts")
        var_ready, std_ready = sem("var_ready"), sem("std_ready")
        fold_done, fold_copied = sem("fold_done"), sem("fold_copied")
        xs_ready, mask_ready, agg_done, agg_read = sem("xs_ready"), sem("mask_ready"), sem("agg_done"), sem("agg_read")
        sa_ready, saT_done, saT_copied, comb_done, x1_ready = (
            sem("sa_ready"), sem("saT_done"), sem("saT_copied"), sem("comb_done"), sem("x1_ready"))
        m_kept, vr_ready, sd_ready, xn_ready, xn_out = (
            sem("m_kept"), sem("vr_ready"), sem("sd_ready"), sem("xn_ready"), sems("xn_out", 2))
        x1T_done, x1T_copied, lg_done, lg_copied, oh_made, pos_done, pos_read, rows_ready = (
            sem("x1T_done"), sem("x1T_copied"), sem("lg_done"), sem("lg_copied"), sem("oh_made"), sem("pos_done"),
            sem("pos_read"), sem("rows_ready"))
        zero_ready, zero_out, ids_out, ids_in, zrow_ready = (
            sem("zero_ready"), sem("zero_out"), sem("ids_out"), sem("ids_in"), sem("zrow_ready"))
        exp_in, exp_out = sem("exp_in"), sem("exp_out")
        w1_in, xg_in, xT_done, xT_copied = sem("w1_in"), sems("xg_in", 2), sem("xT_done"), sem("xT_copied")
        hgu_done, sg_ready, acs_ready, sd_done, sd_read = (
            sem("hgu_done"), sem("sg_ready"), sem("acs_ready"), sem("sd_done"), sem("sd_read"))
        exin, exw, exwd = sems("exin", 2), sems("exw", 2), sems("exwd", 2)
        exT_done, exT_copied, exT_mid, exgu_done, exsg_ready, exac_ready, exy_done, exy_copied = (
            sem("exT_done"), sem("exT_copied"), sem("exT_mid"), sem("exgu_done"), sem("exsg_ready"), sem("exac_ready"),
            sem("exy_done"), sem("exy_copied"))
        exy_out = sems("exy_out", 2)
        y6_in, y6_used = sems("y6_in", 4), sem("y6_used")
        w2_in, va_done, va_copied = sem("w2_in"), sem("va_done"), sem("va_copied")
        gxg_ready, gxT_done, gxT_copied, h_done, h_copied = (
            sem("gxg_ready"), sem("gxT_done"), sem("gxT_copied"), sem("h_done"), sem("h_copied"))
        hs_done, mn_ready, mn_all, acc_ready, accT_done, accT_read = (
            sem("hs_done"), sem("mn_ready"), sem("mn_all"), sem("acc_ready"), sem("accT_done"), sem("accT_read"))
        dgn_ready, pb_done, pb_copied = sem("dgn_ready"), sem("pb_done"), sem("pb_copied")
        at1_ready, at2_ready, ate_ready, atp_ready, atp_used, blk_done, blk_read = (
            sem("at1_ready"), sem("at2_ready"), sem("ate_ready"), sem("atp_ready"), sem("atp_used"),
            sem("blk_done"), sem("blk_read"))
        w3_in, fxg_ready, fxT_done, fxT_copied, fl_done, fl_read = (
            sem("w3_in"), sem("fxg_ready"), sem("fxT_done"), sem("fxT_copied"), sem("fl_done"), sem("fl_read"))
        aff_in, aff_out, xr_ready, xr_out, x3_out = (
            sem("aff_in"), sem("aff_out"), sem("xr_ready"), sem("xr_out"), sem("x3_out"))
        cmp_ready, cnt_done, sel1_ready, sel1_done = (
            sem("cmp_ready"), sem("cnt_done"), sem("sel1_ready"), sem("sel1_done"))
        oh_ready, oh_used, lt_done, lt_read, li_ready = (
            sem("oh_ready"), sem("oh_used"), sem("lt_done"), sem("lt_read"), sem("li_ready"))
        fw_in, fx_in = sems("fw_in", 2), sems("fx_in", 2)
        fT_done, fT_read, fh_done, fh_ready, fy_done, fy_ready = (
            sem("fT_done"), sem("fT_read"), sem("fh_done"), sem("fh_ready"), sem("fy_done"), sem("fy_ready"))
        y_out = sem("y_out")

        block = top.enter_context(nc.Block())

        def end_stage(eng, k):
            eng.drain().then_inc(stage_end, 1)
            eng.wait_ge(stage_end, 5 * k)

        out_rows = out[0:(T - 1) * P, :].rearrange("(t p) d -> p t d", p=P)

        @block.sync
        def _(sp):
            sp.dma_start(X[:, :, :], d["x"]).then_inc(x_in, 16)
            for dst, name in ((WselfT, "W_self_T"), (WnbT, "W_nb_T"), (bsn, "b_self_nb"),
                              (bcomb, "b_comb"), (rw, "router_w"), (rb, "router_b")):
                sp.dma_start(dst[tuple(slice(None) for _ in dst.shape)], d[name]).then_inc(w0_in, 16)
            for half in range(2):
                sp.dma_start(Wc[half], d["W_comb"][:, half * KC:(half + 1) * KC, :]).then_inc(w0_in, 16)

            def load_adj(k, par, first):
                for h in range(2):
                    if not (isinstance(k, int) and k < 1):
                        sp.wait_ge(mask_ready, 2 * k - 1 + h)
                    sp.dma_start(adj[h][:, :, :], d["adj"][k, :, h * HT:(h + 1) * HT, :]).then_inc(adj_in[h], 16)

            def store_xn(k, par, first):
                sp.wait_ge(xn_ready, k + 1)
                sp.dma_start(nbuf[cols(k, P), :], xnb[par][:, :, :].rearrange("p a b -> p (a b)")
                             ).then_inc(xn_out[par], 16)
            sp.wait_ge(zero_ready, 1)
            sp.dma_start(ids.rearrange("(p n) o -> p (n o)", p=P), zero[:, :]).then_inc(zero_out, 16)
            pipelined(sp, T, [(load_adj, -2), (store_xn, 2)])
            for s in xn_out:
                sp.wait_ge(s, 16 * T // 2)
            end_stage(sp, 1)

            sp.dma_start(EI[:, :, :], ids.rearrange("(e p b) o -> p e (b o)", p=P, b=B0)).then_inc(ids_in, 16)
            sp.wait_ge(zrow_ready, 1)
            sp.dma_start(ybuf[ZROW:ZROW + 1, :], zrow[:, :]).then_inc(zero_out, 16)

            def load_up(k, par, first):
                if not first:
                    sp.wait_ge(exgu_done, 2 * k - 2)
                sp.dma_start(ex_w[par][:, :, :], d["gate_up0"][k, :, :, :]).then_inc(exw[par], 16)

            def load_down(k, par, first):
                if not first:
                    sp.wait_ge(exy_done, 3 * k - 3)
                sp.dma_start(ex_wd[par][:, :], d["down0"][k, :, :]).then_inc(exwd[par], 16)

            def store_expert(k, par, first):
                sp.wait_ge(exy_copied, 3 * k + 3)
                sp.dma_start(ybuf[bass.ds(k * S0, S0), :].rearrange("(p b) d -> p (b d)", p=P),
                             ex_y[par][:, :, :].rearrange("p b d -> p (b d)")).then_inc(exy_out[par], 16)
            pipelined(sp, E0, [(load_up, -1), (store_expert, 1), (load_down, -1)])
            for s in exy_out:
                sp.wait_ge(s, 16 * E0 // 2)
            sp.wait_ge(zero_out, 32)
            end_stage(sp, 2)

            for dst, name in ((sgu, "shared_gate_up"), (sdn, "shared_down")):
                sp.dma_start(dst[tuple(slice(None) for _ in dst.shape)], d[name]).then_inc(w1_in, 16)

            def load_xn(k, par, first):
                if not first:
                    sp.wait_ge(xT_done, k - 1)
                sp.dma_start(xg[par][:, :, :].rearrange("p (t c) b -> p t (c b)", t=GT),
                             nbuf[cols(k, GW), :].rearrange("(t p) d -> p t d", p=P)).then_inc(xg_in[par], 16)
            pipelined(sp, G, [(load_xn, 0)])
            end_stage(sp, 3)

            sp.dma_start(W2[:, :, 0:D], d["W_T"]).then_inc(w2_in, 16)
            sp.dma_start(Wn[:, :, :], d["W"]).then_inc(w2_in, 16)
            sp.dma_start(a12[:, :, :], d["a12"]).then_inc(w2_in, 16)
            end_stage(sp, 4)
            end_stage(sp, 5)

            sp.dma_start(gw[:, :, :], d["gate_w"]).then_inc(w3_in, 16)
            sp.dma_start(out_rows, X[:, 0:T - 1, :]).then_inc(x3_out, 16)
            sp.dma_start(out[(T - 1) * P:N, :], X[0:PAD, T - 1, :]).then_inc(x3_out, 16)
            sp.dma_start(b1c[:, :, :], d["b1"]).then_inc(w3_in, 16)
            sp.dma_start(b2r[:, :, :], d["b2"]).then_inc(w3_in, 16)
            sp.wait_ge(xr_ready, 1)
            sp.dma_start(rbuf.rearrange("(t p) d -> p t d", p=P), XR[:, :, :]).then_inc(xr_out, 16)
            sp.wait_ge(x3_out, 32)
            sp.wait_ge(xr_out, 16)
            end_stage(sp, 6)

            def load_w1(k, par, first):
                if not first:
                    sp.wait_ge(fy_done, 2 * k - 2)
                sp.dma_start(w12[par][:, :, :], d["experts1"][k, :, :, :]).then_inc(fw_in[par], 16)
            pipelined(sp, E1, [(load_w1, 0)])
            end_stage(sp, 7)

        @block.gpsimd
        def _(pool):
            c = Chain(pool, pool_done)
            c.inc(pool.memset(ident[:, :], 0.0))
            pool.memset(zero[:, :], 0).then_inc(zero_ready, 1)
            c.inc(pool.memset(before[:, :], 0.0))
            c.inc(pool.memset(notbefore[:, :], 1.0))
            pool.memset(ones[:, :], 1.0).then_inc(consts, 1)
            pool.memset(ones16[:, :], 1.0).then_inc(consts, 1)
            pool.memset(XS[:, :, ONE:LO], 1.0).then_inc(consts, 1)
            pool.iota(iota64[:, :], [[1, E0]], base=0, channel_multiplier=0,
                      allow_small_or_imprecise_dtypes=True).then_inc(consts, 1)
            pool.iota(slots16[:, :], [[1, S1]], base=0, channel_multiplier=0,
                      allow_small_or_imprecise_dtypes=True).then_inc(consts, 1)
            pool.iota(tokens[:, :], [[P, T]], base=0, channel_multiplier=1).then_inc(consts, 1)
            pool.iota(tokp[:, :, 0], [[1, T]], base=0, channel_multiplier=0,
                      allow_small_or_imprecise_dtypes=True).then_inc(consts, 1)
            pool.iota(tokp[:, :, 1], [[0, T]], base=0, channel_multiplier=1,
                      allow_small_or_imprecise_dtypes=True).then_inc(consts, 1)
            c.inc(pool.memset(padm[:, :], 1.0))
            c.inc(pool.memset(padn[:, :], 0.0))
            c.inc(pool.memset(tail[:, :], 0.0))
            c.wait()
            pool.affine_select(out=ident[:, :], in_=ident[:, :], compare_op=ALU.not_equal, fill=1.0, base=0,
                               pattern=[[-1, P]], channel_multiplier=1).then_inc(consts, 1)
            pool.affine_select(out=before[:, :], in_=before[:, :], compare_op=ALU.is_ge, fill=1.0, base=0,
                               pattern=[[-1, P]], channel_multiplier=1).then_inc(consts, 1)
            pool.affine_select(out=notbefore[:, :], in_=notbefore[:, :], compare_op=ALU.is_ge, fill=0.0, base=0,
                               pattern=[[-1, P]], channel_multiplier=1).then_inc(consts, 1)
            pool.affine_select(out=padm[:, :], in_=padm[:, :], compare_op=ALU.not_equal, fill=0.0, base=-PAD,
                               pattern=[[0, 1]], channel_multiplier=1).then_inc(consts, 1)
            pool.affine_select(out=padn[:, :], in_=padn[:, :], compare_op=ALU.not_equal, fill=-1.0, base=-PAD,
                               pattern=[[0, 1]], channel_multiplier=1).then_inc(consts, 1)
            pool.affine_select(out=tail[:, :], in_=tail[:, :], compare_op=ALU.is_ge, fill=SKIP, base=CAP1 - 1,
                               pattern=[[-P, B1]], channel_multiplier=-1).then_inc(consts, 1)
            pool.wait_ge(consts, 14)
            pool.wait_ge(zero_out, 16)
            for t in range(T):
                pool.wait_ge(rows_ready, t + 1)
                for k in range(K0):
                    pool.indirect_dma_start(
                        ids[:, :], bass.IndirectOffsetOnAxis(ap=DS[:, t, k:k + 1], axis=0), tokens[:, t:t + 1], None,
                        bounds_check=E0 * S0 - 1, oob_is_err=False).then_inc(ids_out, 16)
            pool.wait_ge(ids_out, 16 * T * K0)
            end_stage(pool, 1)
            pool.memset(zrow[:, :], 0.0).then_inc(zrow_ready, 1)
            pool.wait_ge(ids_in, 16)
            for e in range(E0):
                if e >= 2:
                    pool.wait_ge(exT_done, 3 * e - 3)
                for b in range(B0):
                    pool.indirect_dma_start(
                        ex_in[e % 2][:, b, :], None, nbuf[:, :], bass.IndirectOffsetOnAxis(ap=EI[:, e, b:b + 1], axis=0),
                        bounds_check=NP - 1, oob_is_err=False).then_inc(exin[e % 2], 16)
            end_stage(pool, 2)
            for t in range(T):
                if t >= 4:
                    pool.wait_ge(y6_used, t - 3)
                for k in range(K0):
                    pool.indirect_dma_start(
                        Y6[t % 4][:, k, :], None, ybuf[:, :], bass.IndirectOffsetOnAxis(ap=DG[:, t, k:k + 1], axis=0),
                        bounds_check=ZROW, oob_is_err=False).then_inc(y6_in[t % 4], 16)
            end_stage(pool, 3)
            pool.wait_ge(mn_ready, 1)
            pool.partition_all_reduce(SC[:, 1:2], SC[:, 0:1], P, MAXR).then_inc(mn_all, 1)
            end_stage(pool, 4)
            end_stage(pool, 5)
            end_stage(pool, 6)

            def gather(e):
                if e >= 2:
                    pool.wait_ge(fy_ready, e - 1)
                for b in range(B1):
                    pool.indirect_dma_start(
                        fx[e % 2][:, b, :], None, rbuf[:, :], bass.IndirectOffsetOnAxis(ap=GI[:, e, b:b + 1], axis=0),
                        bounds_check=NP - 1, oob_is_err=False).then_inc(fx_in[e % 2], 16)
            gather(0)
            gather(1)
            for e in range(E1):
                pool.wait_ge(fy_ready, e + 1)
                if e:
                    pool.wait_ge(y_out, 16 * B1 * e)
                for b in range(B1):
                    pool.indirect_dma_start(
                        out[:, :], bass.IndirectOffsetOnAxis(ap=SI[:, e, b:b + 1], axis=0), fy[e % 2][:, b, :], None,
                        bounds_check=N - 1, oob_is_err=False, compute_op=ALU.add).then_inc(y_out, 16)
                if e + 2 < E1:
                    gather(e + 2)
            pool.wait_ge(y_out, 16 * B1 * E1)
            end_stage(pool, 7)

        @block.scalar
        def _(act):
            c = Chain(act, act_done)

            def norm_root(n):
                act.wait_ge(var_ready, n)
                act.activation(stat[:, 1, :], stat[:, 0, :], ACT.Sqrt).then_inc(std_ready, 1)

            norm_root(1)
            act.wait_ge(fold_done, 2)
            act.copy(WF[:, 0:KC, :].rearrange("p c n -> p (c n)"), banks[6][:, :]).then_inc(fold_copied, 1)
            act.copy(WF[:, KC:2 * KC, :].rearrange("p c n -> p (c n)"), banks[7][:, :]).then_inc(fold_copied, 1)

            def copy_saT(k, par, first):
                act.wait_ge(saT_done, k + 1)
                if not first:
                    act.wait_ge(comb_done, k - 1)
                act.copy(saT[par][:, :, :].rearrange("p a b -> p (a b)"), banks[2][:, :]).then_inc(saT_copied, 1)

            def keep_mask(k, par, first):
                act.wait_ge(mask_ready, 2 * k + 2)
                act.copy(M[:, :, cols(k, P)], mt[par][:, :, :]).then_inc(m_kept, 1)

            def root(k, par, first):
                act.wait_ge(vr_ready, k + 1)
                act.activation(sd[par][:, 0:1], mv[par][:, 1:2], ACT.Sqrt).then_inc(sd_ready, 1)

            def copy_x1T(k, par, first):
                act.wait_ge(x1T_done, k + 1)
                if not first:
                    act.wait_ge(lg_done, k - 1)
                act.copy(xTb[par][:, :, :].rearrange("p a b -> p (a b)"), banks[4][:, 0:D]).then_inc(x1T_copied, 1)

            def copy_logits(k, par, first):
                act.wait_ge(lg_done, k + 1)
                if not first:
                    act.wait_ge(oh_made, k - 1)
                act.copy(lgb[par][:, :], banks[5][:, 0:E0]).then_inc(lg_copied, 1)
                act.wait_ge(lg_copied, 2 * k + 1)
                act.copy(LG[:, k, :], lgb[par][:, :]).then_inc(lg_copied, 1)
            pipelined(act, T, [(root, 2), (keep_mask, -1), (copy_saT, 1), (copy_logits, 3), (copy_x1T, 2)])
            end_stage(act, 1)

            act.wait_ge(exp_in, 2)
            act.activation(EXs[:, :, :], EXs[:, :, :], ACT.Exp).then_inc(exp_out, 1)
            act.activation(EX6[:, :, :], EX6[:, :, :], ACT.Exp).then_inc(exp_out, 1)

            def copy_exT(k, par, first):
                if not first:
                    act.wait_ge(exgu_done, 2 * k - 2)
                for j in (0, 2):
                    nb = min(2, B0 - 2 * j)
                    act.wait_ge(exT_done, 3 * k + j + 1)
                    act.copy(ex_T[par][:, :, 2 * j * P:(2 * j + nb) * P],
                             banks[(par + j) % 2][:, 0:KC * nb * P].rearrange("p (c n) -> p c n", c=KC)
                             ).then_inc(exT_copied, 1)

            def silu_expert(k, par, first):
                if not first:
                    act.wait_ge(exac_ready, 2 * k - 2)
                for h in range(2):
                    act.wait_ge(exgu_done, 2 * k + h + 1)
                    act.activation(ex_sg[par][:, cols(h, S0 // 2)], banks[2 + 2 * h][:, 0:S0 // 2],
                                   ACT.Silu).then_inc(exsg_ready, 1)

            def copy_exy(k, par, first):
                if not first:
                    act.wait_ge(exy_out[par], (k - par) * 8)
                for j in range(3):
                    nb = min(2, B0 - 2 * j)
                    act.wait_ge(exy_done, 3 * k + j + 1)
                    act.copy(ex_y[par][:, 2 * j:2 * j + nb, :].rearrange("p b d -> p (b d)"),
                             banks[6 + (par + j) % 2][:, 0:nb * D]).then_inc(exy_copied, 1)
            pipelined(act, E0, [(silu_expert, 0), (copy_exy, 1), (copy_exT, -1)])
            end_stage(act, 2)

            def copy_xT(k, par, first):
                act.wait_ge(xT_done, k + 1)
                if not first:
                    act.wait_ge(hgu_done, 2 * k - 2)
                act.copy(xT[par][:, :, :].rearrange("p a b -> p (a b)"), banks[par][:, :]).then_inc(xT_copied, 1)

            def silu_shared(k, par, first):
                if not first:
                    act.wait_ge(acs_ready, 2 * k - 2)
                for s in range(SH):
                    act.wait_ge(hgu_done, 2 * k + s + 1)
                    act.activation(sgs[par][:, s, :], banks[3 + s][:, 0:GW], ACT.Silu).then_inc(sg_ready, 1)
            pipelined(act, G, [(copy_xT, 0), (silu_shared, 0)])
            end_stage(act, 3)

            norm_root(2)
            act.wait_ge(va_done, 1)
            act.copy(W2[:, :, D:D + 2], banks[7][:, 0:2 * KC].rearrange("p (c n) -> p c n", c=KC)).then_inc(va_copied, 1)

            def copy_gxT(k, par, first):
                act.wait_ge(gxT_done, k + 1)
                if not first:
                    act.wait_ge(h_done, 2 * k - 2)
                act.copy(gxT[par][:, :, :].rearrange("p a b -> p (a b)"), banks[par][:, :]).then_inc(gxT_copied, 1)
            pipelined(act, G, [(copy_gxT, 0)])
            end_stage(act, 4)

            def copy_pb(k):
                act.wait_ge(pb_done, k + 1)
                o, w = ABLOCKS[k // 2]
                act.copy((PB, QB)[k % 2][:, o:o + w], banks[k % 2][:, 0:w]).then_inc(pb_copied, 1)
            for k in range(2 * len(ABLOCKS)):
                copy_pb(k)
            act.wait_ge(pb_copied, 2 * len(ABLOCKS))
            for bi, (o, w) in enumerate(ABLOCKS):
                base = T * bi

                def attend_sum(k, par, first):
                    if not first or bi:
                        act.wait_ge(at2_ready, k + base - 1)
                    act.activation(at1[par][:, 0:w], PB[:, o:o + w], ACT.Identity,
                                   bias=dcol[:, 0, k:k + 1] if isinstance(k, int) else dcol[:, 0, bass.ds(k, 1)]
                                   ).then_inc(at1_ready, 1)

                def attend_exp(k, par, first):
                    act.wait_ge(at2_ready, k + base + 1)
                    act.activation(at2[par][:, 0:w], at2[par][:, 0:w], ACT.Exp).then_inc(ate_ready, 1)
                pipelined(act, T, [(attend_sum, 0), (attend_exp, 1)])
            end_stage(act, 5)

            norm_root(3)

            def copy_fxT(k, par, first):
                act.wait_ge(fxT_done, k + 1)
                if not first:
                    act.wait_ge(fl_done, k - 1)
                act.copy(fxT[par][:, :, :].rearrange("p a b -> p (a b)"), banks[par][:, :]).then_inc(fxT_copied, 1)
            pipelined(act, G, [(copy_fxT, 0)])
            act.wait_ge(aff_in, 1)
            act.activation(AF[:, :, :], AF[:, :, :], ACT.Exp).then_inc(aff_out, 1)
            end_stage(act, 6)

            act.wait_ge(w3_in, 48)

            def gelu(k, par, first):
                if not first:
                    act.wait_ge(fy_done, 2 * k - 2)
                for h in range(KC):
                    act.wait_ge(fh_done, 2 * k + h + 1)
                    act.activation(fh[par][:, h, :], banks[2 + h][:, :], ACT.Gelu_apprx_tanh,
                                   bias=b1c[:, k, h:h + 1]).then_inc(fh_ready, 1)
            pipelined(act, E1, [(gelu, 0)])
            end_stage(act, 7)

        @block.vector
        def _(dve):
            c = Chain(dve, dve_done)
            norms = [0]

            def layer_norm():
                norms[0] += 1
                each(dve, T, lambda t: c.inc(dve.bn_stats(bn[:, t, :], X[:, t, :])), c, 1)
                c.wait()
                c.inc(dve.tensor_tensor(stat[:, 0, :], bn[:, :, 1], bn[:, :, 4], ALU.add))
                c.inc(dve.tensor_tensor(stat[:, 1, :], bn[:, :, 1], bn[:, :, 4], ALU.subtract))
                c.inc(dve.tensor_tensor(stat[:, 2, :], bn[:, :, 2], bn[:, :, 5], ALU.add))
                c.wait()
                c.inc(dve.tensor_scalar(mean[:, :], stat[:, 0, :], 0.5, None, ALU.mult))
                c.inc(dve.scalar_tensor_tensor(stat[:, 1, :], stat[:, 1, :], 0.25, stat[:, 1, :], ALU.mult, ALU.mult))
                c.wait()
                c.inc(dve.scalar_tensor_tensor(stat[:, 0, :], stat[:, 2, :], 1.0 / D, stat[:, 1, :], ALU.mult, ALU.add))
                c.wait()
                dve.tensor_scalar(stat[:, 0, :], stat[:, 0, :], EPS, None, ALU.add).then_inc(var_ready, 1)
                dve.wait_ge(std_ready, norms[0])
                c.inc(dve.reciprocal(rstd[:, :], stat[:, 1, :]))
                c.wait()

            def normalise(dst, t):
                return dve.tensor_scalar(dst, X[:, t, :], mean[:, bass.ds(t, 1)], rstd[:, bass.ds(t, 1)],
                                         ALU.subtract, ALU.mult)

            def normalise_group(dst, k):
                for u in range(GT - 1):
                    c.inc(normalise(dst[:, cols(u, KC), :].rearrange("p a b -> p (a b)"), k * GT + u))
                return normalise(dst[:, (GT - 1) * KC:GT * KC, :].rearrange("p a b -> p (a b)"), k * GT + GT - 1)

            def stand_alone():
                dve.memset(SC[0:1, 8:9], 0.0)

            dve.wait_ge(x_in, 16)
            layer_norm()

            def split(k, par, first):
                c.inc(normalise(xn0[par][:, :], k))
                c.wait()
                c.inc(dve.tensor_copy(XS[:, k, HI:HI + D], xn0[par][:, :]))
                c.wait()
                c.inc(dve.tensor_tensor(XS[:, k, LO:LO + D], xn0[par][:, :], XS[:, k, HI:HI + D], ALU.subtract))
            pipelined(dve, T, [(split, 0)], c)
            c.wait()
            dve.tensor_copy(dg[0][:, :], XS[:, 0, 0:2]).then_inc(xs_ready, 1)
            dve.wait_ge(fold_done, 3)
            dve.wait_ge(w0_in, 128)
            dve.tensor_tensor(BF[:, :], banks[5][0:1, 0:D], bcomb[:, :], ALU.add).then_inc(fold_copied, 1)

            def masks(k, par, first):
                if not first:
                    dve.wait_ge(agg_done, k - 1)
                    dve.wait_ge(m_kept, k - 1)
                for h in range(2):
                    dve.wait_ge(adj_in[h], 16 * k + 16)
                    dve.tensor_scalar(mt[par][:, h * HT:(h + 1) * HT, :], adj[h][:, :, :], 0, None,
                                      ALU.is_gt).then_inc(mask_ready, 1)

            def mean_of_neighbours(k, par, first):
                dve.wait_ge(agg_done, k + 1)
                if not first:
                    dve.wait_ge(saT_done, k - 1)
                c.inc(normalise(sa[par][:, 0:KC, :].rearrange("p a b -> p (a b)"), k))
                c.inc(dve.tensor_scalar(dg[par][:, 0:1], banks[par][:, D:D + 1], 1.0, None, ALU.max))
                c.wait()
                c.inc(dve.reciprocal(dg[par][:, 1:2], dg[par][:, 0:1]))
                c.wait()
                dve.tensor_scalar(sa[par][:, KC:2 * KC, :].rearrange("p a b -> p (a b)"), banks[par][:, 0:D],
                                  dg[par][:, 1:2], None, ALU.mult).then_inc(sa_ready, 1)

            def residual0(k, par, first):
                dve.wait_ge(comb_done, k + 1)
                dve.scalar_tensor_tensor(X[:, k, :], banks[3][:, 0:D], 0.0, X[:, k, :], ALU.max,
                                         ALU.add).then_inc(x1_ready, 1)
                dve.wait_ge(x1_ready, k + 1)
                stand_alone()
                c.inc(dve.bn_stats(bnb[par][:, :], X[:, k, :]))
                c.wait()
                stand_alone()
                c.inc(dve.bn_aggr(mv[par][:, :], bnb[par][:, :]))
                c.wait()
                dve.tensor_scalar(mv[par][:, 1:2], mv[par][:, 1:2], EPS, None, ALU.add).then_inc(vr_ready, 1)

            def norm1(k, par, first):
                dve.wait_ge(sd_ready, k + 1)
                c.inc(dve.reciprocal(sd[par][:, 1:2], sd[par][:, 0:1]))
                c.wait()
                if not first:
                    dve.wait_ge(x1T_done, k - 1)
                    dve.wait_ge(xn_out[par], (k - par) * 8)
                dve.tensor_scalar(xnb[par][:, :, :].rearrange("p a b -> p (a b)"), X[:, k, :], mv[par][:, 0:1],
                                  sd[par][:, 1:2], ALU.subtract, ALU.mult).then_inc(xn_ready, 1)

            def choose(k, par, first):
                dve.wait_ge(lg_copied, 2 * k + 1)
                stand_alone()
                c.inc(dve.max(mx8b[par][:, :], lgb[par][:, :]))
                c.wait()
                stand_alone()
                c.inc(dve.max_index(ix8b[par][:, :], mx8b[par][:, :], lgb[par][:, :]))
                c.inc(dve.tensor_copy(MX8[:, k, :], mx8b[par][:, :]))
                c.wait()
                if not first:
                    dve.wait_ge(pos_done, k)
                dve.tensor_tensor(OH[par][:, :, :], iota64[:, :].unsqueeze(1).broadcast_to([P, K0, E0]),
                                  ix8b[par][:, 0:K0].unsqueeze(2).broadcast_to([P, K0, E0]),
                                  ALU.is_equal).then_inc(oh_made, 1)

            def assign(k, par, first):
                dve.wait_ge(pos_done, k + 1)
                dve.tensor_tensor(OHP[:, :, :], OH[par][:, :, :],
                                  banks[6][:, 0:E0].unsqueeze(1).broadcast_to([P, K0, E0]), ALU.mult).then_inc(pos_read, 1)
                dve.wait_ge(pos_read, k + 1)
                c.inc(dve.tensor_reduce(r6[:, 0, :], OHP[:, :, :], AX, ALU.add))
                c.wait()
                c.inc(dve.tensor_scalar(VAL[:, k, :], r6[:, 0, :], float(CAP0), None, ALU.is_lt))
                c.inc(dve.scalar_tensor_tensor(r6[:, 1, :], ix8b[par][:, 0:K0], float(S0), r6[:, 0, :], ALU.mult, ALU.add))
                c.wait()
                c.inc(dve.tensor_scalar(r6[:, 2, :], VAL[:, k, :], -SKIP, SKIP, ALU.mult, ALU.add))
                c.inc(dve.scalar_tensor_tensor(r6[:, 3, :], r6[:, 1, :], -float(ZROW), VAL[:, k, :], ALU.add, ALU.mult))
                c.wait()
                dve.tensor_tensor(DS[:, k, :], r6[:, 1, :], r6[:, 2, :], ALU.add).then_inc(rows_ready, 1)
                c.inc(dve.tensor_scalar(DG[:, k, :], r6[:, 3, :], float(ZROW), None, ALU.add))
            pipelined(dve, T, [(mean_of_neighbours, 1), (residual0, 2), (masks, -1), (norm1, 2), (choose, 4),
                               (assign, 5)], c)
            end_stage(dve, 1)

            dve.tensor_tensor(EXs[:, :, :], LG[:, :, :], MX8[:, :, 0:1].broadcast_to([P, T, E0]),
                              ALU.subtract).then_inc(exp_in, 1)
            dve.tensor_tensor(EX6[:, :, :], MX8[:, :, 0:K0], MX8[:, :, 0:1].broadcast_to([P, T, K0]),
                              ALU.subtract).then_inc(exp_in, 1)
            dve.wait_ge(exp_out, 2)
            c.inc(dve.tensor_reduce(stat[:, 0, :], EXs[:, :, :], AX, ALU.add))
            c.inc(dve.tensor_reduce(stat[:, 1, :], EX6[:, :, :], AX, ALU.add))
            c.wait()
            c.inc(dve.scalar_tensor_tensor(stat[:, 0, :], stat[:, 0, :], 1e-9, stat[:, 1, :], ALU.mult, ALU.add))
            c.wait()
            c.inc(dve.reciprocal(stat[:, 1, :], stat[:, 0, :]))
            c.wait()
            c.inc(dve.tensor_tensor(G6[:, :, :], EX6[:, :, :], bc(stat[:, 1, :], [P, T, K0], 2), ALU.mult))

            def copy_exT1(k, par, first):
                if not first:
                    dve.wait_ge(exgu_done, 2 * k - 2)
                dve.wait_ge(exT_done, 3 * k + 2)
                dve.tensor_copy(ex_T[par][:, :, 2 * P:4 * P],
                                banks[(par + 1) % 2][:, :].rearrange("p (c n) -> p c n", c=KC)).then_inc(exT_mid, 1)

            def gate_expert(k, par, first):
                if not first:
                    dve.wait_ge(exy_done, 3 * k - 3)
                for h in range(2):
                    dve.wait_ge(exsg_ready, 2 * k + h + 1)
                    dve.tensor_tensor(ex_ac[par][:, cols(h, S0 // 2)], banks[3 + 2 * h][:, 0:S0 // 2],
                                      ex_sg[par][:, cols(h, S0 // 2)], ALU.mult).then_inc(exac_ready, 1)
            pipelined(dve, E0, [(gate_expert, 0), (copy_exT1, -1)])
            end_stage(dve, 2)

            def gate_shared(k, par, first):
                if not first:
                    dve.wait_ge(sd_done, k - 1)
                for s in range(SH):
                    dve.wait_ge(sg_ready, 2 * k + s + 1)
                    dve.scalar_tensor_tensor(acs[par][:, s, :], banks[3 + s][:, GW:2 * GW], 1.0 / SH, sgs[par][:, s, :],
                                             ALU.mult, ALU.mult).then_inc(acs_ready, 1)

            def add_shared(k, par, first):
                dve.wait_ge(sd_done, k + 1)
                dve.tensor_tensor(X[:, cols(k, GT), :].rearrange("p t d -> p (t d)"), banks[5 + par][:, :],
                                  X[:, cols(k, GT), :].rearrange("p t d -> p (t d)"), ALU.add).then_inc(sd_read, 1)
                dve.wait_ge(sd_read, k + 1)

            def add_choices(k, par, first):
                for u in range(GT):
                    dve.wait_ge(y6_in[2 * par + u], (k - par) * (8 * K0) + 16 * K0)
                for j in range(K0):
                    for u in range(GT):
                        t = k * GT + u
                        ins = dve.scalar_tensor_tensor(X[:, t, :], Y6[2 * par + u][:, j, :],
                                                       G6[:, bass.ds(t, 1), j], X[:, t, :], ALU.mult, ALU.add)
                        if j < K0 - 1:
                            c.inc(ins)
                        else:
                            ins.then_inc(y6_used, 1)
                    if j < K0 - 1:
                        c.wait()
            pipelined(dve, G, [(gate_shared, 0), (add_shared, 1), (add_choices, 1)], c)
            dve.wait_ge(y6_used, T)
            end_stage(dve, 3)

            dve.memset(H[:, :, D:HW], 1.0).then_inc(h_copied, 1)
            layer_norm()

            def xn_group1(k, par, first):
                if not first:
                    dve.wait_ge(gxT_done, k - 1)
                normalise_group(gxg[par], k).then_inc(gxg_ready, 1)

            def copy_h(k, par, first):
                for u in range(GT):
                    dve.wait_ge(h_done, 2 * k + u + 1)
                    c.inc(dve.tensor_copy(H[:, k * GT + u, 0:D], banks[2 + u][:, 0:D]))
                    dve.tensor_copy(SD[:, k * GT + u, :], banks[2 + u][:, D:D + 2]).then_inc(h_copied, 1)
            pipelined(dve, G, [(xn_group1, -1), (copy_h, 0)], c)
            dve.wait_ge(h_copied, T + 1)
            c.wait()
            c.inc(dve.tensor_scalar(H[:, T - 1, D:HW], H[:, T - 1, D:HW], padm[:, 0:1], None, ALU.mult))
            c.inc(dve.tensor_copy(dcol[:, 0, :], SD[:, :, 1]))
            c.inc(dve.tensor_scalar(dcol[:, 1, :], SD[:, :, 1], ALPHA, None, ALU.mult))
            c.inc(dve.tensor_scalar(dcol[:, 2, :], SD[:, :, 1], -1.0, None, ALU.mult))
            c.wait()
            dve.tensor_reduce(SC[:, 0:1], dcol[:, 2, :], AX, ALU.max).then_inc(mn_ready, 1)
            dve.wait_ge(mn_all, 1)
            c.inc(dve.tensor_scalar(dcol[:, 2, :], SD[:, :, 1], SC[:, 1:2], 1.0, ALU.add, ALU.add))
            end_stage(dve, 4)

            dve.wait_ge(hs_done, 1)
            c.inc(dve.tensor_copy(HS[:, 0:D + 1], banks[7][:, 0:D + 1]))
            c.inc(dve.tensor_scalar(acc[:, :], M[:, 0, :], dcol[:, 2, 0:1], None, ALU.mult))
            for j in range(1, T):
                c.wait()
                ins = dve.scalar_tensor_tensor(acc[:, :], M[:, j, :], dcol[:, 2, j:j + 1], acc[:, :], ALU.mult, ALU.max)
                if j < T - 1:
                    c.inc(ins)
            ins.then_inc(acc_ready, 1)
            for j, (o, w) in enumerate(ABLOCKS):
                dve.wait_ge(accT_done, j + 1)
                ins = dve.tensor_reduce(MM[:, 0, o // P:(o + w) // P],
                                        banks[j % 2][:, 0:w].rearrange("p (a b) -> p a b", b=P), AX, ALU.max)
                ins.then_inc(accT_read, 1)
            dve.wait_ge(accT_read, len(ABLOCKS))
            c.inc(dve.tensor_scalar(MM[:, 1, :], MM[:, 0, :], SC[:, 1:2], -1.0, ALU.subtract, ALU.add))
            c.wait()
            c.inc(dve.tensor_tensor(MM[:, 1, :], MM[:, 1, :], SD[:, :, 0], ALU.add))
            c.wait()
            c.inc(dve.scalar_tensor_tensor(MM[:, 2, :], MM[:, 1, :], ALPHA, MM[:, 1, :], ALU.mult, ALU.max))
            c.wait()
            c.inc(dve.tensor_tensor(MM[:, 3, :], SD[:, :, 0], MM[:, 2, :], ALU.subtract))
            c.inc(dve.scalar_tensor_tensor(MM[:, 4, :], SD[:, :, 0], ALPHA, MM[:, 2, :], ALU.mult, ALU.subtract))
            c.wait()
            for k in range(2 * len(ABLOCKS)):
                o, w = ABLOCKS[k // 2]
                if k >= 2:
                    dve.wait_ge(pb_done, k - 1)
                for q in range(w // P):
                    ins = dve.tensor_scalar(dgn[k % 2][:, q, :], ident[:, :],
                                            MM[:, 3 + k % 2, o // P + q:o // P + q + 1], None, ALU.mult)
                    if q < w // P - 1:
                        c.inc(ins)
                ins.then_inc(dgn_ready, 1)
            dve.wait_ge(pb_copied, 2 * len(ABLOCKS))

            for bi, (o, w) in enumerate(ABLOCKS):
                base = T * bi

                def attend_max(k, par, first):
                    dve.wait_ge(at1_ready, k + base + 1)
                    if not first or bi:
                        dve.wait_ge(atp_ready, k + base - 1)
                    dve.scalar_tensor_tensor(at2[par][:, 0:w], QB[:, o:o + w],
                                             dcol[:, 1, bass.ds(k, 1)], at1[par][:, 0:w], ALU.add,
                                             ALU.max).then_inc(at2_ready, 1)

                def attend_mask(k, par, first):
                    dve.wait_ge(ate_ready, k + base + 1)
                    if not first or bi:
                        dve.wait_ge(atp_used, k + base - 1)
                    dve.scalar_tensor_tensor(atp[par][:, 0:w], at2[par][:, 0:w], 1.0, M[:, k, o:o + w], ALU.min,
                                             ALU.mult).then_inc(atp_ready, 1)
                pipelined(dve, T, [(attend_max, 0), (attend_mask, 1)])
                dve.wait_ge(blk_done, bi + 1)
                for q in range(w // P):
                    t = o // P + q
                    src = banks[4 * (bi % 2) + q]
                    nb = num[q % 2]
                    c.inc(dve.tensor_scalar(SC[:, 2:3], src[:, D:D + 1], 0.5, None, ALU.is_lt))
                    c.wait()
                    c.inc(dve.tensor_scalar(nb[:, 0:D + 1], HS[:, 0:D + 1], SC[:, 2:3], None, ALU.mult))
                    c.wait()
                    c.inc(dve.tensor_tensor(nb[:, 0:D + 1], src[:, 0:D + 1], nb[:, 0:D + 1], ALU.add))
                    c.wait()
                    c.inc(dve.reciprocal(SC[:, 3:4], nb[:, D:D + 1]))
                    c.wait()
                    c.inc(dve.scalar_tensor_tensor(X[:, t, :], nb[:, 0:D], SC[:, 3:4], X[:, t, :], ALU.mult, ALU.add))
                    c.wait()
                dve.tensor_copy(SC[:, 4:5], SC[:, 3:4]).then_inc(blk_read, 1)
            end_stage(dve, 5)

            layer_norm()

            def xn_group2(k, par, first):
                if not first:
                    dve.wait_ge(fxT_done, k - 1)
                ins = normalise_group(fxg[par], k)
                ins.then_inc(fxg_ready, 1)
                dve.wait_ge(fxg_ready, k + 1)
                c.inc(dve.tensor_copy(XR[:, cols(k, GT), 0:D],
                                      fxg[par][:, :, :].rearrange("p (t c) b -> p t (c b)", t=GT)))

            def read_gates(k, par, first):
                dve.wait_ge(fl_done, k + 1)
                dve.tensor_copy(AF[:, cols(k, GT), :].rearrange("p t e -> p (t e)"),
                                banks[2 + par][:, 0:GT * E1]).then_inc(fl_read, 1)
            pipelined(dve, G, [(xn_group2, -1), (read_gates, 0)], c)
            dve.wait_ge(fl_read, G)
            c.inc(dve.tensor_reduce(stat[:, 0, :], AF[:, :, :], AX, ALU.max))
            c.wait()
            dve.tensor_tensor(AF[:, :, :], AF[:, :, :], bc(stat[:, 0, :], [P, T, E1], 2),
                              ALU.subtract).then_inc(aff_in, 1)
            dve.wait_ge(aff_out, 1)
            c.inc(dve.tensor_reduce(stat[:, 0, :], AF[:, :, :], AX, ALU.add))
            c.wait()
            c.inc(dve.reciprocal(stat[:, 1, :], stat[:, 0, :]))
            c.wait()
            c.inc(dve.tensor_tensor(AF[:, :, :], AF[:, :, :], bc(stat[:, 1, :], [P, T, E1], 2), ALU.mult))
            c.wait()
            c.inc(dve.tensor_scalar(AF[:, T - 1, :], AF[:, T - 1, :], padm[:, 0:1], padn[:, 0:1], ALU.mult, ALU.add))
            c.wait()
            dve.tensor_copy(XR[:, :, D:XW], AF[:, :, :]).then_inc(xr_ready, 1)

            c.inc(dve.memset(thr[:, :], 0))
            c.inc(dve.memset(biti[:, :], 1 << TOP_BIT))
            c.inc(dve.memset(bitf[:, :], float(1 << TOP_BIT)))
            c.wait()

            def one_bit(i):
                c.inc(dve.tensor_tensor(cand[:, :], thr[:, :], biti[:, :], ALU.bitwise_or))
                c.wait()
                c.inc(dve.tensor_tensor(F1[:, :, :], AF[:, :, :], bc(cand[:, :].bitcast(F32), [P, T, E1], 1), ALU.is_ge))
                c.wait()
                dve.tensor_reduce(cnt[:, :], F1[:, :, :].rearrange("p t e -> p e t"), AX, ALU.add).then_inc(cmp_ready, 1)
                dve.wait_ge(cnt_done, i + 1)
                c.inc(dve.scalar_tensor_tensor(stepi[:, :], banks[4][:, 0:E1], float(CAP1), bitf[:, :], ALU.is_ge,
                                               ALU.mult))
                c.inc(dve.tensor_scalar(biti[:, :], biti[:, :], 1, None, ALU.logical_shift_right))
                c.wait()
                c.inc(dve.tensor_scalar(bitf[:, :], bitf[:, :], 0.5, None, ALU.mult))
                c.inc(dve.tensor_tensor(thr[:, :], thr[:, :], stepi[:, :], ALU.bitwise_or))
                c.wait()
            each(dve, TOP_BIT + 1, one_bit, c, 6)

            tb = bc(thr[:, :].bitcast(F32), [P, T, E1], 1)
            c.inc(dve.tensor_tensor(F1[:, :, :], AF[:, :, :], tb, ALU.is_gt))
            c.inc(dve.tensor_tensor(F2[:, :, :], AF[:, :, :], tb, ALU.is_equal))
            c.wait()
            c.inc(dve.tensor_reduce(cnt[:, :], F1[:, :, :].rearrange("p t e -> p e t"), AX, ALU.add))
            c.wait()

            def prefix(src, dst, n):
                dve.tensor_copy(S16[:, :, :], src[:, :, :]).then_inc(sel1_ready, 1)
                dve.wait_ge(sel1_done, n)
                w = T * E1
                c.inc(dve.tensor_copy(dst[:, :, :].rearrange("p t e -> p (t e)"), banks[5][:, 0:w]))
                c.inc(dve.tensor_copy(F3[:, :, :].rearrange("p t e -> p (t e)"), banks[6][:, 0:w]))
                c.wait()

                def add_tile(t):
                    c.inc(dve.tensor_tensor(dst[:, bass.ds(t + 1, 1), :], dst[:, bass.ds(t + 1, 1), :],
                                            F3[:, bass.ds(t, 1), :], ALU.add))
                    c.inc(dve.tensor_tensor(F3[:, bass.ds(t + 1, 1), :], F3[:, bass.ds(t + 1, 1), :],
                                            F3[:, bass.ds(t, 1), :], ALU.add))
                    c.wait()
                each(dve, T - 1, add_tile, c, 2)

            prefix(F2, SL, 1)
            c.inc(dve.tensor_tensor(SL[:, :, :], SL[:, :, :], bc(banks[7][:, 0:E1], [P, T, E1], 1), ALU.add))
            c.wait()
            c.inc(dve.scalar_tensor_tensor(SL[:, :, :], SL[:, :, :], float(CAP1), F2[:, :, :], ALU.is_lt, ALU.mult))
            c.wait()
            c.inc(dve.tensor_tensor(F1[:, :, :], F1[:, :, :], SL[:, :, :], ALU.add))
            c.wait()
            prefix(F1, SL, 2)
            c.inc(dve.scalar_tensor_tensor(SL[:, :, :], SL[:, :, :], 1.0, F1[:, :, :], ALU.add, ALU.mult))
            c.wait()
            c.inc(dve.tensor_scalar(SL[:, :, :], SL[:, :, :], -1.0, None, ALU.add))
            c.wait()

            for e in range(E1):
                def one_hot(t, par, first):
                    if not first or e:
                        dve.wait_ge(oh_used, t + T * e - 1)
                    dve.tensor_scalar(oh1[par][:, :], slots16[:, :], SL[:, t, e:e + 1], None,
                                      ALU.is_equal).then_inc(oh_ready, 1)
                pipelined(dve, T, [(one_hot, 0)])
                dve.wait_ge(lt_done, e + 1)
                for b in range(B1):
                    ins = dve.tensor_copy(LT[:, e, b, :], banks[b][:, 0:2])
                    if b < B1 - 1:
                        c.inc(ins)
                ins.then_inc(lt_read, 1)
            dve.wait_ge(lt_read, E1)
            c.wait()
            c.inc(dve.scalar_tensor_tensor(LI[:, :, :], LT[:, :, :, 0], float(P), LT[:, :, :, 1], ALU.mult, ALU.add))
            c.wait()
            c.inc(dve.tensor_copy(GI[:, :, :], LI[:, :, :]))
            c.inc(dve.tensor_tensor(SI[:, :, :], LI[:, :, :], bc(tail[:, :], [P, E1, B1], 1), ALU.add))
            end_stage(dve, 6)

            def copy_fT(k, par, first):
                if not first:
                    dve.wait_ge(fh_done, 2 * k - 2)
                for j in range(2):
                    dve.wait_ge(fT_done, 2 * k + j + 1)
                    dve.tensor_copy(fT[par][:, :, cols(j, 2 * P)],
                                    banks[j][:, :].rearrange("p (c n) -> p c n", c=KC)).then_inc(fT_read, 1)

            def weigh(k, par, first):
                if not first:
                    dve.wait_ge(y_out, (k - 1) * (16 * B1))
                for b in range(B1):
                    dve.wait_ge(fy_done, 2 * k + b // 2 + 1)
                    ins = dve.tensor_scalar(fy[par][:, b, :], banks[4 + 2 * par + b // 2][:, cols(b % 2, D)],
                                            fx[par][:, b, bass.ds(k + D, 1)], None, ALU.mult)
                    if b < B1 - 1:
                        c.inc(ins)
                ins.then_inc(fy_ready, 1)
            pipelined(dve, E1, [(copy_fT, 0), (weigh, 0)], c)
            end_stage(dve, 7)

        @block.tensor
        def _(pe):
            pe.wait_ge(consts, 14)
            pe.wait_ge(w0_in, 128)
            for which, (wT, bank) in enumerate(((WselfT, banks[6]), (WnbT, banks[7]))):
                for dc in range(KC):
                    for mc in range(KC):
                        mm = pe.matmul(bank[:, cols(dc, D)], wT[:, mc, cols(dc, P)], Wc[which][:, mc, :],
                                       start=(mc == 0), stop=(mc == KC - 1))
                mm.then_inc(fold_done, 1)
            for which in range(2):
                for mc in range(KC):
                    mm = pe.matmul(banks[5][0:1, 0:D], bsn[:, which, mc:mc + 1], Wc[which][:, mc, :],
                                   start=(which + mc == 0), stop=(which + mc == KC))
            mm.then_inc(fold_done, 1)
            pe.wait_ge(fold_copied, 3)
            pe.wait_ge(xs_ready, 1)

            def aggregate(k, par, first, half):
                if half == 0:
                    if not first:
                        pe.wait_ge(sa_ready, k - 1)
                pe.wait_ge(mask_ready, 2 * k + 1 + half)
                for j in range(half * HT, (half + 1) * HT):
                    halves = ((D + 1, HI), (D, LO)) if j == 0 else ((D, LO), (D + 1, HI))
                    for n, (w, o) in enumerate(halves):
                        mm = pe.matmul(banks[par][:, 0:w], mt[par][:, j, :], XS[:, j, o:o + w],
                                       start=(j == 0 and n == 0), stop=(j == T - 1 and n == 1), skip_group_check=True)
                if half == 1:
                    mm.then_inc(agg_done, 1)

            def turn0(k, par, first):
                pe.wait_ge(sa_ready, k + 1)
                if not (isinstance(k, int) and k < 1):
                    pe.wait_ge(saT_copied, k)
                for j in range(2 * KC):
                    mm = pe.transpose(banks[2][:, cols(j, P)], sa[par][:, j, :], ident[:, :])
                mm.then_inc(saT_done, 1)

            def combine(k, par, first):
                pe.wait_ge(saT_copied, k + 1)
                if not (isinstance(k, int) and k < 1):
                    pe.wait_ge(x1_ready, k)
                for j in range(2 * KC):
                    pe.matmul(banks[3][:, 0:D], saT[par][:, j, :], WF[:, j, :], start=(j == 0), stop=False)
                pe.matmul(banks[3][:, 0:D], ones[0:1, :], BF[:, :], start=False, stop=True).then_inc(comb_done, 1)

            def turn1(k, par, first):
                pe.wait_ge(xn_ready, k + 1)
                if not (isinstance(k, int) and k < 1):
                    pe.wait_ge(x1T_copied, k)
                for ch in range(KC):
                    mm = pe.transpose(banks[4][:, cols(ch, P)], xnb[par][:, ch, :], ident[:, :])
                mm.then_inc(x1T_done, 1)

            def logits(k, par, first):
                pe.wait_ge(x1T_copied, k + 1)
                if not (isinstance(k, int) and k < 1):
                    pe.wait_ge(lg_copied, 2 * k - 1)
                for ch in range(KC):
                    pe.matmul(banks[5][:, 0:E0], xTb[par][:, ch, :], rw[:, ch, :], start=(ch == 0), stop=False)
                pe.matmul(banks[5][:, 0:E0], ones[0:1, :], rb[:, :], start=False, stop=True).then_inc(lg_done, 1)

            def count(k, par, first):
                pe.wait_ge(oh_made, k + 1)
                start = isinstance(k, int) and k == 0
                if not start:
                    pe.wait_ge(pos_read, k)
                    for j in range(K0):
                        pe.matmul(banks[6][:, 0:E0], notbefore[:, :], OH[1 - par][:, j, :], start=False, stop=False,
                                  skip_group_check=True)
                for j in range(K0):
                    mm = pe.matmul(banks[6][:, 0:E0], before[:, :], OH[par][:, j, :], start=(start and j == 0),
                                   stop=(j == K0 - 1), skip_group_check=True)
                mm.then_inc(pos_done, 1)
            pipelined(pe, T, [(lambda k, par, first: aggregate(k, par, first, 0), 0), (turn0, 1), (logits, 3),
                              (lambda k, par, first: aggregate(k, par, first, 1), 0), (combine, 1), (count, 4),
                              (turn1, 2)])
            end_stage(pe, 1)

            def turn_tiles(src, bank):
                for ch in range(KC):
                    for u in range(GT):
                        mm = pe.transpose(banks[bank][:, cols(ch * GT + u, P)], src[:, u * KC + ch, :], ident[:, :])
                return mm

            def turn_group(src, ready, done, read, k, par, first):
                pe.wait_ge(ready, k + 1)
                if not first:
                    pe.wait_ge(read, k - 1)
                turn_tiles(src[par], par).then_inc(done, 1)

            def turn_expert(k, par, first):
                pe.wait_ge(exin[par], (k - par) * (8 * B0) + 16 * B0)
                for j in range(3):
                    nb = min(2, B0 - 2 * j)
                    if j == 2:
                        pe.wait_ge(exT_copied, 2 * k + 1)
                    elif not (isinstance(k, int) and k == 0):
                        pe.wait_ge((exT_mid, exT_copied)[j], k if j == 0 else 2 * k)
                    for ch in range(KC):
                        for u in range(nb):
                            mm = pe.transpose(banks[(par + j) % 2][:, cols(ch * nb + u, P)],
                                              ex_in[par][:, 2 * j + u, cols(ch, P)], ident[:, :])
                    mm.then_inc(exT_done, 1)

            def up_expert(k, par, first):
                pe.wait_ge(exw[par], (k - par) * 8 + 16)
                pe.wait_ge(exT_copied, 2 * k + 2)
                pe.wait_ge(exT_mid, k + 1)
                for h in range(2):
                    if not (isinstance(k, int) and k < 1):
                        pe.wait_ge(exac_ready, 2 * k - 1 + h)
                    for gu in range(2):
                        for ch in range(KC):
                            mm = pe.matmul(banks[2 + 2 * h + gu][:, 0:S0 // 2], ex_w[par][:, gu * KC + ch, :],
                                           ex_T[par][:, ch, cols(h, S0 // 2)], start=(ch == 0), stop=(ch == KC - 1))
                    mm.then_inc(exgu_done, 1)

            def down_expert(k, par, first):
                pe.wait_ge(exwd[par], (k - par) * 8 + 16)
                pe.wait_ge(exac_ready, 2 * k + 2)
                for j in range(3):
                    if not (isinstance(k, int) and k == 0 and j < 2):
                        pe.wait_ge(exy_copied, 3 * k + j - 1)
                    for u in range(min(2, B0 - 2 * j)):
                        mm = pe.matmul(banks[6 + (par + j) % 2][:, cols(u, D)],
                                       ex_ac[par][:, cols(2 * j + u, P)], ex_wd[par][:, :],
                                       start=True, stop=True)
                    mm.then_inc(exy_done, 1)
            pipelined(pe, E0, [(up_expert, 0), (down_expert, 1), (turn_expert, -1)])
            end_stage(pe, 2)

            pe.wait_ge(w1_in, 32)

            def turn_shared(k, par, first):
                pe.wait_ge(xg_in[par], (k - par) * 8 + 16)
                if not first:
                    pe.wait_ge(xT_copied, k - 1)
                turn_tiles(xg[par], par).then_inc(xT_done, 1)

            def shared(k, par, first):
                pe.wait_ge(xT_copied, k + 1)
                for s in range(SH):
                    if not (isinstance(k, int) and k < 1):
                        pe.wait_ge(acs_ready, 2 * k - 1 + s)
                    for gu in range(2):
                        for ch in range(KC):
                            mm = pe.matmul(banks[3 + s][:, cols(gu, GW)], sgu[:, s, gu, ch, :], xT[par][:, ch, :],
                                           start=(ch == 0), stop=(ch == KC - 1), skip_group_check=True)
                    mm.then_inc(hgu_done, 1)

            def shared_down(k, par, first):
                pe.wait_ge(acs_ready, 2 * k + 2)
                if not first:
                    pe.wait_ge(sd_read, k - 1)
                for u in range(GT):
                    for s in range(SH):
                        mm = pe.matmul(banks[5 + par][:, cols(u, D)], acs[par][:, s, cols(u, P)], sdn[:, s, :],
                                       start=(s == 0), stop=(s == SH - 1))
                mm.then_inc(sd_done, 1)
            pipelined(pe, G, [(turn_shared, 0), (shared, 0), (shared_down, 0)])
            end_stage(pe, 3)

            pe.wait_ge(w2_in, 48)
            for dc in range(KC):
                for oc in range(KC):
                    mm = pe.matmul(banks[7][:, cols(dc, 2)], Wn[:, oc, cols(dc, P)], a12[:, oc, :],
                                   start=(oc == 0), stop=(oc == KC - 1))
            mm.then_inc(va_done, 1)
            pe.wait_ge(va_copied, 1)

            def turn2(k, par, first):
                turn_group(gxg, gxg_ready, gxT_done, gxT_copied, k, par, first)

            def features(k, par, first):
                pe.wait_ge(gxT_copied, k + 1)
                for u in range(GT):
                    if not (isinstance(k, int) and k < 1):
                        pe.wait_ge(h_copied, 2 * k + u)
                    for ch in range(KC):
                        mm = pe.matmul(banks[2 + u][:, 0:D + 2], gxT[par][:, ch, cols(u, P)], W2[:, ch, :],
                                       start=(ch == 0), stop=(ch == KC - 1))
                    mm.then_inc(h_done, 1)
            pipelined(pe, G, [(turn2, -1), (features, 0)])
            end_stage(pe, 4)

            for j in range(T):
                mm = pe.matmul(banks[7][:, 0:D + 2], ones[:, :], H[:, j, 0:D + 2], start=(j == 0), stop=(j == T - 1))
            mm.then_inc(hs_done, 1)
            pe.wait_ge(acc_ready, 1)
            for j, (o, w) in enumerate(ABLOCKS):
                if j >= 2:
                    pe.wait_ge(accT_read, j - 1)
                for q in range(w // P):
                    mm = pe.transpose(banks[j % 2][:, cols(q, P)], acc[:, o + q * P:o + (q + 1) * P], ident[:, :])
                mm.then_inc(accT_done, 1)
            pe.wait_ge(accT_read, len(ABLOCKS))
            for k in range(2 * len(ABLOCKS)):
                o, w = ABLOCKS[k // 2]
                pe.wait_ge(dgn_ready, k + 1)
                if k >= 2:
                    pe.wait_ge(pb_copied, k - 1)
                for q in range(w // P):
                    mm = pe.matmul(banks[k % 2][:, cols(q, P)], ones[:, :], dgn[k % 2][:, q, :], start=True, stop=True)
                mm.then_inc(pb_done, 1)
            pe.wait_ge(pb_copied, 2 * len(ABLOCKS))
            for bi, (o, w) in enumerate(ABLOCKS):
                if bi >= 2:
                    pe.wait_ge(blk_read, bi - 1)

                def attend(k, par, first):
                    pe.wait_ge(atp_ready, k + T * bi + 1)
                    for q in range(w // P):
                        mm = pe.matmul(banks[4 * (bi % 2) + q][:, 0:D + 1], atp[par][:, cols(q, P)], H[:, k, 0:D + 1],
                                       start=(isinstance(k, int) and k == 0), stop=(isinstance(k, int) and k == T - 1),
                                       skip_group_check=True)
                    mm.then_inc(atp_used, 1)
                pipelined(pe, T, [(attend, 0)])
                pe.wait_ge(atp_used, T * (bi + 1))
                pe.drain().then_inc(blk_done, 1)
            end_stage(pe, 5)

            pe.wait_ge(w3_in, 48)

            def turn3(k, par, first):
                turn_group(fxg, fxg_ready, fxT_done, fxT_copied, k, par, first)

            def gates(k, par, first):
                pe.wait_ge(fxT_copied, k + 1)
                if not first:
                    pe.wait_ge(fl_read, k - 1)
                for u in range(GT):
                    for ch in range(KC):
                        mm = pe.matmul(banks[2 + par][:, cols(u, E1)], fxT[par][:, ch, cols(u, P)], gw[:, ch, :],
                                       start=(ch == 0), stop=(ch == KC - 1), skip_group_check=True)
                mm.then_inc(fl_done, 1)
            pipelined(pe, G, [(turn3, -1), (gates, 0)])
            with pe.Fori(0, TOP_BIT + 1) as i:
                pe.wait_ge(cmp_ready, i + 1)
                pe.matmul(banks[4][:, 0:E1], ones[:, :], cnt[:, :], start=True, stop=True).then_inc(cnt_done, 1)
            w = T * E1
            for n in range(2):
                pe.wait_ge(sel1_ready, n + 1)
                pe.matmul(banks[5][:, 0:w], before[:, :], S16[:, :, :].rearrange("p t e -> p (t e)"),
                          start=True, stop=True)
                mm = pe.matmul(banks[6][:, 0:w], ones16[:, :], S16[:, :, :].rearrange("p t e -> p (t e)"),
                               start=True, stop=True)
                if n == 0:
                    mm = pe.matmul(banks[7][:, 0:E1], ones[:, :], cnt[:, :], start=True, stop=True)
                mm.then_inc(sel1_done, 1)
            for e in range(E1):
                if e:
                    pe.wait_ge(lt_read, e)

                def place(t, par, first):
                    pe.wait_ge(oh_ready, t + T * e + 1)
                    for b in range(B1):
                        mm = pe.matmul(banks[b][:, 0:2], oh1[par][:, cols(b, P)], tokp[:, t, :],
                                       start=(isinstance(t, int) and t == 0), stop=(isinstance(t, int) and t == T - 1),
                                       skip_group_check=True)
                    mm.then_inc(oh_used, 1)
                pipelined(pe, T, [(place, 0)])
                pe.drain().then_inc(lt_done, 1)
            end_stage(pe, 6)

            pe.wait_ge(w3_in, 48)

            def turn_rows(k, par, first):
                pe.wait_ge(fx_in[par], (k - par) * (8 * B1) + 16 * B1)
                for j in range(2):
                    if not (isinstance(k, int) and k < 1):
                        pe.wait_ge(fT_read, 2 * k + j - 1)
                    for ch in range(KC):
                        for u in range(2):
                            mm = pe.transpose(banks[j][:, cols(ch * 2 + u, P)], fx[par][:, 2 * j + u, cols(ch, P)],
                                              ident[:, :])
                    mm.then_inc(fT_done, 1)

            def hidden(k, par, first):
                pe.wait_ge(fw_in[par], (k - par) * 8 + 16)
                pe.wait_ge(fT_read, 2 * k + 2)
                for h in range(KC):
                    if not (isinstance(k, int) and k < 1):
                        pe.wait_ge(fh_ready, 2 * k - 1 + h)
                    for ch in range(KC):
                        mm = pe.matmul(banks[2 + h][:, :], w12[par][:, ch, cols(h, P)], fT[par][:, ch, :],
                                       start=(ch == 0), stop=(ch == KC - 1))
                    mm.then_inc(fh_done, 1)

            def outputs(k, par, first):
                pe.wait_ge(fh_ready, 2 * k + 2)
                if not first:
                    pe.wait_ge(fy_ready, k - 1)
                for b in range(B1):
                    for h in range(KC):
                        pe.matmul(banks[4 + 2 * par + b // 2][:, cols(b % 2, D)], fh[par][:, h, cols(b, P)],
                                  w12[par][:, KC + h, :], start=(h == 0), stop=False, skip_group_check=True)
                    mm = pe.matmul(banks[4 + 2 * par + b // 2][:, cols(b % 2, D)], ones[0:1, :], b2r[:, k, :],
                                   start=False, stop=True, skip_group_check=True)
                    if b % 2:
                        mm.then_inc(fy_done, 1)
            pipelined(pe, E1, [(turn_rows, 0), (hidden, 0), (outputs, 0)])
            end_stage(pe, 7)


def kernel(**inputs):
    import numpy as np
    import concourse.bacc as bacc
    from concourse.bass_utils import run_bass_kernel_spmd

    def arr(name):
        return np.asarray(inputs[name])

    def kmaj(w):
        return w.reshape(-1, P, w.shape[1]).transpose(1, 0, 2)

    g0, f0, g1, f1 = "L0_gnn_", "L0_ffn_", "L1_gnn_", "L1_ffn_"
    x = np.pad(arr("x"), ((0, NP - N), (0, 0)))
    adj = np.pad(arr("adj"), ((0, NP - N), (0, NP - N)))
    gate, up, down = (arr(f0 + n).transpose(0, 2, 1) for n in ("w_gate", "w_up", "w_down"))
    sgate, sup, sdown = (arr(f0 + n).transpose(0, 2, 1) for n in ("shared_w_gate", "shared_w_up", "shared_w_down"))

    def two(w):
        return w.reshape(w.shape[0], -1, P, w.shape[2]).transpose(0, 2, 1, 3)

    arrays = {
        "x": x.reshape(T, P, D).transpose(1, 0, 2),
        "adj": adj.reshape(T, P, T, P).transpose(0, 3, 2, 1),
        "W_self_T": kmaj(arr(g0 + "W_self").T),
        "W_nb_T": kmaj(arr(g0 + "W_nb").T),
        "W_comb": kmaj(arr(g0 + "W_comb")),
        "b_self_nb": np.stack([arr(g0 + "b_self"), arr(g0 + "b_nb")]).reshape(2, KC, P).transpose(2, 0, 1),
        "b_comb": arr(g0 + "b_comb").reshape(1, D),
        "router_w": kmaj(arr(f0 + "router_w").T),
        "router_b": arr(f0 + "bias").reshape(1, E0),
        "shared_gate_up": np.stack([two(sgate), two(sup)], 1).transpose(2, 0, 1, 3, 4),
        "shared_down": sdown.transpose(1, 0, 2),
        "gate_up0": np.concatenate([two(gate), two(up)], 2),
        "down0": down,
        "W_T": kmaj(arr(g1 + "W").T),
        "W": kmaj(arr(g1 + "W")),
        "a12": kmaj(np.stack([arr(g1 + "a1"), arr(g1 + "a2")], 1)),
        "gate_w": kmaj(arr(f1 + "gate_weight")),
        "experts1": np.concatenate([two(arr(f1 + "w1")), two(arr(f1 + "w2"))], 2),
        "b1": arr(f1 + "b1").reshape(E1, KC, P).transpose(2, 0, 1),
        "b2": arr(f1 + "b2").reshape(1, E1, D),
    }
    nc = bacc.Bacc("TRN2", target_bir_lowering=False, num_devices=1)
    feeds, aps = {}, {}
    for name, a in arrays.items():
        a = np.ascontiguousarray(a)
        feeds[f"in_{name}"] = a
        aps[name] = nc.dram_tensor(f"in_{name}", a.shape, mybir.dt.from_np(a.dtype), kind="ExternalInput").ap()
    out = nc.dram_tensor("out", (N, D), F32, kind="ExternalOutput").ap()
    ids = nc.dram_tensor("ids", (E0 * S0, 1), U32, kind="Internal").ap()
    nbuf = nc.dram_tensor("nbuf", (NP, D), F32, kind="Internal").ap()
    ybuf = nc.dram_tensor("ybuf", (E0 * S0 + 1, D), F32, kind="Internal").ap()
    rbuf = nc.dram_tensor("rbuf", (NP, XW), F32, kind="Internal").ap()
    build(nc, aps, out, ids, nbuf, ybuf, rbuf)
    return run_bass_kernel_spmd(nc, [feeds], core_ids=[0]).results[0]["out"]
```

```python
from contextlib import ExitStack

import concourse.bass as bass
from concourse import mybir

P = 128
N = 3327
D = 256
KC = D // P
T = (N + P - 1) // P
NP = T * P
PAD = N - (T - 1) * P
GT = 2
G = T // GT
GW = GT * P
EPS = 1e-5

E0, K0, SH = 64, 6, 2
CAP0 = max(1, int(N * K0 * 2.0 / E0))
B0 = (CAP0 + P - 1) // P
S0 = B0 * P
ZROW = E0 * S0
SKIP = 65536.0

E1 = 16
CAP1 = N // E1 * 2
B1 = (CAP1 + P - 1) // P
S1 = B1 * P
XW = D + E1
ROUNDS = 5
DVE_E = 13
TOP_BIT = 29

XPARTS = [(T * i // 4, T * (i + 1) // 4) for i in range(4)]
HT = T // 2

AW = 512
ABLOCKS = [(o, min(AW, NP - o)) for o in range(0, NP, AW)]
ALPHA = 0.2
PEEL = 10

F32, F16, BF16 = mybir.dt.float32, mybir.dt.float16, mybir.dt.bfloat16
I32, U32, U8 = mybir.dt.int32, mybir.dt.uint32, mybir.dt.uint8
ALU, ACT = mybir.AluOpType, mybir.ActivationFunctionType
AX = mybir.AxisListType.X
MAXR = bass.bass_isa.ReduceOp.max

HI, ONE, LO, XSW = 0, D, D + 2, 2 * D + 2
HW = D + 4


class Chain:

    def __init__(self, eng, sem):
        self.eng, self.sem, self.n, self.loop = eng, sem, 0, None

    def inc(self, ins):
        ins.then_inc(self.sem, 1)
        self.n += 1

    def wait(self):
        if self.loop is None:
            self.eng.wait_ge(self.sem, self.n)
        else:
            i, per = self.loop
            self.eng.wait_ge(self.sem, i * per + self.n)


def pipelined(eng, n, parts, chain=None, peel=0):
    late = max(off for _, off in parts)
    early = min(off for _, off in parts)

    def step(s, base=None):
        for fn, off in parts:
            k = s - off
            if base is not None:
                fn(base + k, k % 2, False)
            elif 0 <= k < n:
                fn(k, k % 2, k < 2)

    lo, hi = late + 2 + peel, n + early
    pairs = max((hi - lo) // 2, 0)
    before = 0
    for s in range(early, lo):
        before = chain.n if chain else 0
        step(s)
    if pairs > 1:
        if chain:
            per, start = chain.n - before, chain.n
        with eng.Fori(0, pairs) as i:
            if chain:
                chain.loop = (i, 2 * per)
            step(lo, base=i * 2)
            step(lo + 1, base=i * 2)
        if chain:
            assert chain.n == start + 2 * per, (chain.n, start, per)
            chain.loop = None
            chain.n = start + 2 * per * pairs
        lo += 2 * pairs
    for s in range(lo, n + late):
        step(s)


def each(eng, n, fn, chain, per):
    start = chain.n
    with eng.Fori(0, n) as i:
        chain.loop = (i, per)
        fn(i)
    assert chain.n == start + per
    chain.loop = None
    chain.n = start + per * n


def cols(k, width):
    return bass.ds(k * width, width)


def bc(ap, shape, axis):
    return ap.unsqueeze(axis).broadcast_to(shape)


def build(nc, d, out, ids, nbuf, ybuf, rbuf):
    top = ExitStack()
    with top:
        def sem(name):
            return top.enter_context(nc.semaphore(name))

        def sems(name, n):
            return [sem(f"{name}{i}") for i in range(n)]

        def stage():
            ctx = ExitStack()
            return ctx, lambda name, shape, dt: ctx.enter_context(nc.sbuf_tensor(name, shape, dt))

        banks = [top.enter_context(nc.psum_tensor(f"bank{i}", [P, 512], F32)) for i in range(8)]

        _ctx, sb = stage()
        top.enter_context(_ctx)
        X = sb("X", [P, T, D], F32)
        ident = sb("ident", [P, P], F32)
        ones = sb("ones", [P, P], F32)
        ones16 = sb("ones16", [P, P], BF16)
        before = sb("before", [P, P], BF16)
        notbefore = sb("notbefore", [P, P], BF16)
        bn = sb("bn", [P, T, 6], F32)
        mean = sb("mean", [P, T], F32)
        rstd = sb("rstd", [P, T], F32)
        stat = sb("stat", [P, 3, T], F32)
        iota64 = sb("iota64", [P, E0], F32)
        slots16 = sb("slots16", [P, S1], F16)
        tokp = sb("tokp", [P, T, 2], F16)
        padm = sb("padm", [P, 1], F32)
        padn = sb("padn", [P, 1], F32)
        tail = sb("tail", [P, B1], F32)
        tokens = sb("tokens", [P, T], U32)
        MX8 = sb("MX8", [P, T, 8], F32)
        VAL = sb("VAL", [P, T, K0], F32)
        DS = sb("DS", [P, T, K0], U32)
        G6 = sb("G6", [P, T, K0], F32)
        DG = sb("DG", [P, T, K0], U32)
        SC = sb("SC", [P, 64], F32)

        m_ctx, sb = stage()
        M = sb("M", [P, T, NP], U8)

        lg_ctx, sb = stage()
        LG = sb("LG", [P, T, E0], F32)

        ctx, sb = stage()
        XS = sb("XS", [P, T, XSW], F16)
        adj = [sb(f"adj{i}", [P, HT, P], I32) for i in range(2)]
        mt = [sb(f"mt{i}", [P, T, P], F16) for i in range(2)]
        bsn = sb("bsn", [P, 2, KC], F32)
        bcomb = sb("bcomb", [1, D], F32)
        WF = sb("WF", [P, 2 * KC, D], F32)
        BF = sb("BF", [1, D], F32)
        BFb = sb("BFb", [P, D], F32)
        pre = sb("pre", [P, D], F32)
        dg = [sb(f"dg{i}", [P, 2], F32) for i in range(2)]
        sa = [sb(f"sa{i}", [P, 2 * KC, P], F32) for i in range(2)]
        saT = [sb(f"saT{i}", [P, 2 * KC, P], F32) for i in range(2)]
        WselfT, WnbT = (buf[:, :, :].rearrange("p (c x) b -> p c (x b)", c=KC) for buf in sa)
        Wc = [buf[:, :, :].rearrange("p (c x) b -> p c (x b)", c=KC) for buf in saT]
        xn0 = [sb(f"xn0{i}", [P, D], F32) for i in range(2)]
        bnb = [sb(f"bnb{i}", [P, 6], F32) for i in range(2)]
        mv = [sb(f"mv{i}", [P, 2], F32) for i in range(2)]
        sd = [sb(f"sd{i}", [P, 2], F32) for i in range(2)]
        xnb = [sb(f"xnb{i}", [P, KC, P], F32) for i in range(2)]
        xTb = [sb(f"xTb{i}", [P, KC, P], F32) for i in range(2)]
        lgb = [sb(f"lgb{i}", [P, E0], F32) for i in range(2)]
        mx8b = [sb(f"mx8b{i}", [P, 8], F32) for i in range(2)]
        ix8b = [sb(f"ix8b{i}", [P, 8], U32) for i in range(2)]
        OH = [sb(f"OH{i}", [P, K0, E0], BF16) for i in range(2)]
        OHP = sb("OHP", [P, K0, E0], F32)
        r6 = sb("r6", [P, 4, K0], F32)
        rw = sb("rw", [P, KC, E0], F32)
        rb = sb("rb", [1, E0], F32)
        zero = sb("zero", [P, 320], U32)
        ctx.close()

        ctx, sb = stage()
        EI = sb("EI", [P, E0, B0], U32)
        EXs = sb("EXs", [P, T, E0], F32)
        EX6 = sb("EX6", [P, T, K0], F32)
        zrow = sb("zrow", [1, D], F32)
        ex_in = [sb(f"ex_in{i}", [P, B0, D], F32) for i in range(2)]
        ex_w = [sb(f"ex_w{i}", [P, 2 * KC, P], F32) for i in range(2)]
        ex_wd = [sb(f"ex_wd{i}", [P, D], F32) for i in range(2)]
        ex_T = [sb(f"ex_T{i}", [P, KC, S0], F32) for i in range(2)]
        ex_sg = [sb(f"ex_sg{i}", [P, S0], F32) for i in range(2)]
        ex_ac = [sb(f"ex_ac{i}", [P, S0], F32) for i in range(2)]
        ex_y = [sb(f"ex_y{i}", [P, B0, D], F32) for i in range(2)]
        ctx.close()
        lg_ctx.close()

        ctx, sb = stage()
        H = sb("H", [P, T, HW], F32)
        SD = sb("SD", [P, T, 2], F32)
        dcol = sb("dcol", [P, 3, T], F32)
        HS = sb("HS", [P, D + 2], F32)
        acc = sb("acc", [P, NP], F32)
        in1, sb = stage()
        W2 = sb("W2", [P, KC, D + 2], F32)
        Wn = sb("Wn", [P, KC, D], F32)
        a12 = sb("a12", [P, KC, 2], F32)
        Y6 = [sb(f"Y6{i}", [P, K0, D], F32) for i in range(2)]
        xg = [sb(f"xg{i}", [P, KC, P], F32) for i in range(2)]
        xT = [sb(f"xT{i}", [P, KC, P], F32) for i in range(2)]
        sgs = [sb(f"sgs{i}", [P, SH, P], F32) for i in range(2)]
        acs = [sb(f"acs{i}", [P, SH, P], F32) for i in range(2)]
        sgu = sb("sgu", [P, SH, 2, KC, P], F32)
        sdn = sb("sdn", [P, SH, D], F32)
        dgc = [sb(f"dgc{i}", [P, K0, P], F32) for i in range(2)]
        bnc = [sb(f"bnc{i}", [P, 6], F32) for i in range(2)]
        mvc = [sb(f"mvc{i}", [P, 2], F32) for i in range(2)]
        sdc = [sb(f"sdc{i}", [P, 2], F32) for i in range(2)]
        gx = [sb(f"gx{i}", [P, KC, P], F32) for i in range(2)]
        gxT = [sb(f"gxT{i}", [P, KC, P], F32) for i in range(2)]
        in1.close()
        in1, sb = stage()
        PB = sb("PB", [P, NP], F32)
        QB = sb("QB", [P, NP], F32)
        MM = sb("MM", [P, 6, T], F32)
        dgn = [sb(f"dgn{i}", [P, AW // P, P], F32) for i in range(2)]
        HA = sb("HA", [P, D + 2], F32)
        in2, sb = stage()
        at1 = [sb(f"at1{i}", [P, AW], F32) for i in range(2)]
        at2 = [sb(f"at2{i}", [P, AW], F32) for i in range(2)]
        atp = [sb(f"atp{i}", [P, AW], F32) for i in range(2)]
        num = [sb(f"num{i}", [P, D + 2], F32) for i in range(2)]
        in2.close()
        in1.close()
        ctx.close()
        m_ctx.close()

        ctx, sb = stage()
        XR = sb("XR", [P, T, XW], F32)
        AF = sb("AF", [P, T, E1], F32)
        fxg = [sb(f"fxg{i}", [P, GT * KC, P], F32) for i in range(2)]
        fxT = [sb(f"fxT{i}", [P, KC, GW], F32) for i in range(2)]
        gw = sb("gw", [P, KC, E1], F32)
        SL = sb("SL", [P, T, E1], F32)
        SLI = sb("SLI", [P, T, E1], I32)
        LOW = sb("LOW", [P, T, E1], F32)
        LO16 = sb("LO16", [P, T, E1], F16)
        HB = sb("HB", [P, T, E1], F32)
        A16 = sb("A16", [P, T, E1], BF16)
        S16 = sb("S16", [P, T, E1], BF16)
        cmp3 = sb("cmp3", [P, T, 3, E1], BF16)
        thr = sb("thr", [P, E1], I32)
        cand = sb("cand", [P, 3, E1], I32)
        digit = sb("digit", [P, 3, E1], I32)
        bitf = sb("bitf", [P, 3, E1], F32)
        stepf = sb("stepf", [P, 3, E1], F32)
        stepi = sb("stepi", [P, E1], I32)
        oh1 = [sb(f"oh1{i}", [P, E1, P], F16) for i in range(2)]
        inblock = sb("inblock", [P, T, E1, B1], F16)
        R8 = sb("R8", [P, T, E1, B1, 2], F16)
        LI = sb("LI", [P, E1, B1], F32)
        GI = sb("GI", [P, E1, B1], U32)
        SI = sb("SI", [P, E1, B1], U32)
        in1, sb = stage()
        w12 = [sb(f"w12{i}", [P, 2 * KC, D], F32) for i in range(2)]
        b1c = sb("b1c", [P, E1, KC], F32)
        b2b = sb("b2b", [P, E1, D], F32)
        gcol = [sb(f"gcol{i}", [P, B1], F32) for i in range(2)]
        fx = [sb(f"fx{i}", [P, B1, XW], F32) for i in range(2)]
        fT = [sb(f"fT{i}", [P, KC, S1], F32) for i in range(2)]
        fh = [sb(f"fh{i}", [P, KC, S1], F32) for i in range(2)]
        fy = [sb(f"fy{i}", [P, B1, D], F32) for i in range(2)]
        in1.close()
        ctx.close()

        stage_end = sem("stage_end")
        dve_done, pool_done = sem("dve_done"), sem("pool_done")
        x_in, w0_in, adj_in = sems("x_in", len(XPARTS)), sem("w0_in"), sems("adj_in", 2)
        consts = sem("consts")
        bias_done, comb_read = sem("bias_done"), sem("comb_read")
        xn0_ready, hi_copied, lo_ready = sem("xn0_ready"), sem("hi_copied"), sem("lo_ready")
        var_ready, std_ready = sem("var_ready"), sem("std_ready")
        fold_done, fold_copied = sem("fold_done"), sem("fold_copied")
        xs_ready, mask_ready, agg_done = sem("xs_ready"), sem("mask_ready"), sem("agg_done")
        sa_ready, saT_done, saT_copied, comb_done, x1_ready = (
            sem("sa_ready"), sem("saT_done"), sem("saT_copied"), sem("comb_done"), sem("x1_ready"))
        m_kept, vr_ready, sd_ready, xn_ready, xn_out = (
            sem("m_kept"), sem("vr_ready"), sem("sd_ready"), sem("xn_ready"), sems("xn_out", 2))
        x1T_done, x1T_copied, lg_done, lg_copied, oh_made, pos_done, pos_read, rows_ready = (
            sem("x1T_done"), sem("x1T_copied"), sem("lg_done"), sem("lg_copied"), sem("oh_made"), sem("pos_done"),
            sem("pos_read"), sem("rows_ready"))
        zero_ready, zero_out, ids_out, ids_in, zrow_ready = (
            sem("zero_ready"), sem("zero_out"), sem("ids_out"), sem("ids_in"), sem("zrow_ready"))
        exp_in, exp_out = sem("exp_in"), sem("exp_out")
        w1_in, xg_in, xT_done, xT_copied = sem("w1_in"), sems("xg_in", 2), sem("xT_done"), sem("xT_copied")
        hgu_done, sg_ready, acs_ready, sd_done, sd_read = (
            sem("hgu_done"), sem("sg_ready"), sem("acs_ready"), sem("sd_done"), sem("sd_read"))
        exin, exw, exwd = sems("exin", 2), sems("exw", 2), sems("exwd", 2)
        exT_done, exT_copied, exT_mid, exgu_done, exsg_ready, exac_ready, exy_done, exy_copied = (
            sem("exT_done"), sem("exT_copied"), sem("exT_mid"), sem("exgu_done"), sem("exsg_ready"), sem("exac_ready"),
            sem("exy_done"), sem("exy_copied"))
        exy_out = sems("exy_out", 2)
        y6_in, dgc_ready = sems("y6_in", 2), sem("dgc_ready")
        w2_in, va_done, va_copied, sq_sum, bound_done, bound_ready = (
            sem("w2_in"), sem("va_done"), sem("va_copied"), sem("sq_sum"), sem("bound_done"), sem("bound_ready"))
        vc_ready, sc_ready, gx_ready, gxT_done, gxT_copied, h_done, h_copied = (
            sem("vc_ready"), sem("sc_ready"), sem("gx_ready"), sem("gxT_done"), sem("gxT_copied"), sem("h_done"),
            sem("h_copied"))
        h_ones = sem("h_ones")
        low_ready, ohp_ready = sem("low_ready"), sem("ohp_ready")
        ha_ready, hs_read = sem("ha_ready"), sem("hs_read")
        hs_done, accT_done, accT_read = sem("hs_done"), sem("accT_done"), sem("accT_read")
        dgn_ready, pb_done, pb_copied = sem("dgn_ready"), sem("pb_done"), sem("pb_copied")
        at1_ready, at2_ready, ate_ready, atp_ready, atp_used, blk_done, blk_read = (
            sem("at1_ready"), sem("at2_ready"), sem("ate_ready"), sem("atp_ready"), sem("atp_used"),
            sem("blk_done"), sem("blk_read"))
        w3_in, fxg_ready, fxT_done, fxT_copied, fl_done, fl_read = (
            sem("w3_in"), sem("fxg_ready"), sem("fxT_done"), sem("fxT_copied"), sem("fl_done"), sem("fl_read"))
        fx_kept = sem("fx_kept")
        aff_in, aff_out, xr_ready, xr_out, x3_out = (
            sem("aff_in"), sem("aff_out"), sem("xr_ready"), sem("xr_out"), sem("x3_out"))
        cmp_ready, cnt_done, sel1_ready, sel1_done = (
            sem("cmp_ready"), sem("cnt_done"), sem("sel1_ready"), sem("sel1_done"))
        oh_ready, oh_used, lt_done = sem("oh_ready"), sem("oh_used"), sem("lt_done")
        fw_in, fv_in, fx_in, g_kept = sems("fw_in", 2), sems("fv_in", 2), sems("fx_in", 2), sem("g_kept")
        fT_done, fT_read, fh_done, fh_ready, fy_done, fy_ready = (
            sem("fT_done"), sem("fT_read"), sem("fh_done"), sem("fh_ready"), sem("fy_done"), sem("fy_ready"))
        y_out = sem("y_out")

        block = top.enter_context(nc.Block())

        def end_stage(eng, k):
            eng.drain().then_inc(stage_end, 1)
            eng.wait_ge(stage_end, 5 * k)

        out_rows = out[0:(T - 1) * P, :].rearrange("(t p) d -> p t d", p=P)

        @block.sync
        def _(sp):
            for (a, z), s in zip(XPARTS, x_in):
                sp.dma_start(X[:, a:z, :], d["x"][:, a:z, :]).then_inc(s, 16)
            for dst, name in ((WselfT, "W_self_T"), (WnbT, "W_nb_T"), (bsn, "b_self_nb"),
                              (bcomb, "b_comb"), (rw, "router_w"), (rb, "router_b")):
                sp.dma_start(dst[tuple(slice(None) for _ in dst.shape)], d[name]).then_inc(w0_in, 16)
            for half in range(2):
                sp.dma_start(Wc[half], d["W_comb"][:, half * KC:(half + 1) * KC, :]).then_inc(w0_in, 16)

            def load_adj(k, par, first):
                for h in range(2):
                    if not (isinstance(k, int) and k < 1):
                        sp.wait_ge(mask_ready, 2 * k - 1 + h)
                    sp.dma_start(adj[h][:, :, :], d["adj"][k, :, h * HT:(h + 1) * HT, :]).then_inc(adj_in[h], 16)

            def store_xn(k, par, first):
                sp.wait_ge(xn_ready, k + 1)
                sp.dma_start(nbuf[cols(k, P), :], xnb[par][:, :, :].rearrange("p a b -> p (a b)")
                             ).then_inc(xn_out[par], 16)
            sp.wait_ge(zero_ready, 1)
            sp.dma_start(ids.rearrange("(p n) o -> p (n o)", p=P), zero[:, :]).then_inc(zero_out, 16)
            pipelined(sp, T, [(load_adj, -2), (store_xn, 2)])
            for s in xn_out:
                sp.wait_ge(s, 16 * T // 2)
            end_stage(sp, 1)

            sp.dma_start(EI[:, :, :], ids.rearrange("(e p b) o -> p e (b o)", p=P, b=B0)).then_inc(ids_in, 16)
            sp.wait_ge(zrow_ready, 1)
            sp.dma_start(ybuf[ZROW:ZROW + 1, :], zrow[:, :]).then_inc(zero_out, 16)

            def load_up(k, par, first):
                if not first:
                    sp.wait_ge(exgu_done, 2 * k - 2)
                sp.dma_start(ex_w[par][:, :, :], d["gate_up0"][k, :, :, :]).then_inc(exw[par], 16)

            def load_down(k, par, first):
                if not first:
                    sp.wait_ge(exy_done, 3 * k - 3)
                sp.dma_start(ex_wd[par][:, :], d["down0"][k, :, :]).then_inc(exwd[par], 16)

            def store_expert(k, par, first):
                sp.wait_ge(exy_copied, 3 * k + 3)
                sp.dma_start(ybuf[bass.ds(k * S0, S0), :].rearrange("(p b) d -> p (b d)", p=P),
                             ex_y[par][:, :, :].rearrange("p b d -> p (b d)")).then_inc(exy_out[par], 16)
            pipelined(sp, E0, [(load_up, -1), (store_expert, 1), (load_down, -1)])
            for s in exy_out:
                sp.wait_ge(s, 16 * E0 // 2)
            sp.wait_ge(zero_out, 32)
            end_stage(sp, 2)

            for dst, name in ((sgu, "shared_gate_up"), (sdn, "shared_down")):
                sp.dma_start(dst[tuple(slice(None) for _ in dst.shape)], d[name]).then_inc(w1_in, 16)

            sp.dma_start(W2[:, :, 0:D], d["W_T"]).then_inc(w2_in, 16)
            sp.dma_start(Wn[:, :, :], d["W"]).then_inc(w2_in, 16)
            sp.dma_start(a12[:, :, :], d["a12"]).then_inc(w2_in, 16)

            def load_xn(k, par, first):
                if not first:
                    sp.wait_ge(xT_done, k - 1)
                sp.dma_start(xg[par][:, :, :].rearrange("p c b -> p (c b)"), nbuf[cols(k, P), :]
                             ).then_inc(xg_in[par], 16)
            pipelined(sp, T, [(load_xn, 0)])
            end_stage(sp, 3)
            end_stage(sp, 4)

            sp.dma_start(gw[:, :, :], d["gate_w"]).then_inc(w3_in, 16)
            sp.dma_start(out_rows, X[:, 0:T - 1, :]).then_inc(x3_out, 16)
            sp.dma_start(out[(T - 1) * P:N, :], X[0:PAD, T - 1, :]).then_inc(x3_out, 16)
            sp.dma_start(b1c[:, :, :], d["b1"]).then_inc(w3_in, 16)
            sp.dma_start(b2b[:, :, :], d["b2"].broadcast_to([P, E1, D])).then_inc(w3_in, 16)
            sp.wait_ge(fx_kept, G)
            sp.wait_ge(xr_ready, 1)
            sp.dma_start(rbuf.rearrange("(t p) d -> p t d", p=P), XR[:, :, :]).then_inc(xr_out, 16)
            sp.wait_ge(x3_out, 32)
            sp.wait_ge(xr_out, 16)
            end_stage(sp, 5)

            def load_hidden(k, par, first):
                if not first:
                    sp.wait_ge(fh_done, 2 * k - 2)
                sp.dma_start(w12[par][:, 0:KC, :], d["experts1"][k, :, 0:KC, :]).then_inc(fw_in[par], 16)

            def load_outputs(k, par, first):
                if not first:
                    sp.wait_ge(fy_done, 2 * k - 2)
                sp.dma_start(w12[par][:, KC:2 * KC, :], d["experts1"][k, :, KC:2 * KC, :]).then_inc(fv_in[par], 16)
            pipelined(sp, E1, [(load_hidden, -1), (load_outputs, -1)])
            end_stage(sp, 6)

        @block.gpsimd
        def _(pool):
            c = Chain(pool, pool_done)
            c.inc(pool.memset(ident[:, :], 0.0))
            pool.memset(zero[:, :], 0).then_inc(zero_ready, 1)
            c.inc(pool.memset(before[:, :], 0.0))
            c.inc(pool.memset(notbefore[:, :], 1.0))
            pool.memset(ones[:, :], 1.0).then_inc(consts, 1)
            pool.memset(ones16[:, :], 1.0).then_inc(consts, 1)
            pool.memset(XS[:, :, ONE:LO], 1.0).then_inc(consts, 1)
            pool.iota(iota64[:, :], [[1, E0]], base=0, channel_multiplier=0,
                      allow_small_or_imprecise_dtypes=True).then_inc(consts, 1)
            pool.iota(slots16[:, :], [[1, S1]], base=0, channel_multiplier=0,
                      allow_small_or_imprecise_dtypes=True).then_inc(consts, 1)
            pool.iota(tokens[:, :], [[P, T]], base=0, channel_multiplier=1).then_inc(consts, 1)
            pool.iota(tokp[:, :, 0], [[1, T]], base=0, channel_multiplier=0,
                      allow_small_or_imprecise_dtypes=True).then_inc(consts, 1)
            pool.iota(tokp[:, :, 1], [[0, T]], base=0, channel_multiplier=1,
                      allow_small_or_imprecise_dtypes=True).then_inc(consts, 1)
            c.inc(pool.memset(padm[:, :], 1.0))
            c.inc(pool.memset(padn[:, :], 0.0))
            c.inc(pool.memset(tail[:, :], 0.0))
            c.wait()
            pool.affine_select(out=ident[:, :], in_=ident[:, :], compare_op=ALU.not_equal, fill=1.0, base=0,
                               pattern=[[-1, P]], channel_multiplier=1).then_inc(consts, 1)
            pool.affine_select(out=before[:, :], in_=before[:, :], compare_op=ALU.is_ge, fill=1.0, base=0,
                               pattern=[[-1, P]], channel_multiplier=1).then_inc(consts, 1)
            pool.affine_select(out=notbefore[:, :], in_=notbefore[:, :], compare_op=ALU.is_ge, fill=0.0, base=0,
                               pattern=[[-1, P]], channel_multiplier=1).then_inc(consts, 1)
            pool.affine_select(out=padm[:, :], in_=padm[:, :], compare_op=ALU.not_equal, fill=0.0, base=-PAD,
                               pattern=[[0, 1]], channel_multiplier=1).then_inc(consts, 1)
            pool.affine_select(out=padn[:, :], in_=padn[:, :], compare_op=ALU.not_equal, fill=-1.0, base=-PAD,
                               pattern=[[0, 1]], channel_multiplier=1).then_inc(consts, 1)
            pool.affine_select(out=tail[:, :], in_=tail[:, :], compare_op=ALU.is_ge, fill=SKIP, base=CAP1 - 1,
                               pattern=[[-P, B1]], channel_multiplier=-1).then_inc(consts, 1)
            pool.wait_ge(consts, 14)
            pool.wait_ge(zero_out, 16)
            for t in range(T):
                pool.wait_ge(rows_ready, t + 1)
                for k in range(K0):
                    pool.indirect_dma_start(
                        ids[:, :], bass.IndirectOffsetOnAxis(ap=DS[:, t, k:k + 1], axis=0), tokens[:, t:t + 1], None,
                        bounds_check=E0 * S0 - 1, oob_is_err=False).then_inc(ids_out, 16)
            pool.wait_ge(ids_out, 16 * T * K0)
            end_stage(pool, 1)
            pool.memset(zrow[:, :], 0.0).then_inc(zrow_ready, 1)
            pool.wait_ge(ids_in, 16)
            for e in range(E0):
                if e >= 2:
                    pool.wait_ge(exT_done, 3 * e - 3)
                for b in range(B0):
                    pool.indirect_dma_start(
                        ex_in[e % 2][:, b, :], None, nbuf[:, :], bass.IndirectOffsetOnAxis(ap=EI[:, e, b:b + 1], axis=0),
                        bounds_check=NP - 1, oob_is_err=False).then_inc(exin[e % 2], 16)
            end_stage(pool, 2)
            for t in range(T):
                if t >= 2:
                    pool.wait_ge(sd_done, t - 1)
                for k in range(K0):
                    pool.indirect_dma_start(
                        Y6[t % 2][:, k, :], None, ybuf[:, :], bass.IndirectOffsetOnAxis(ap=DG[:, t, k:k + 1], axis=0),
                        bounds_check=ZROW, oob_is_err=False).then_inc(y6_in[t % 2], 16)
            end_stage(pool, 3)
            c.inc(pool.tensor_tensor(HA[:, :], H[:, 0, 0:D + 2], H[:, 1, 0:D + 2], ALU.add))
            for t in range(2, T):
                c.wait()
                ins = pool.tensor_tensor(HA[:, :], HA[:, :], H[:, t, 0:D + 2], ALU.add)
                if t < T - 1:
                    c.inc(ins)
            ins.then_inc(ha_ready, 1)
            end_stage(pool, 4)
            pool.wait_ge(low_ready, 1)
            for t in range(T):
                if t >= 2:
                    pool.wait_ge(oh_used, t - 1)
                for e in range(DVE_E, E1):
                    ins = pool.tensor_scalar(oh1[t % 2][:, e, :], slots16[:, 0:P], LO16[:, t, e:e + 1], None,
                                             ALU.is_equal)
                ins.then_inc(ohp_ready, 1)
            end_stage(pool, 5)

            def gather(e):
                if e >= 2:
                    pool.wait_ge(fT_done, 2 * e - 2)
                    pool.wait_ge(g_kept, e - 1)
                for b in range(B1):
                    pool.indirect_dma_start(
                        fx[e % 2][:, b, :], None, rbuf[:, :], bass.IndirectOffsetOnAxis(ap=GI[:, e, b:b + 1], axis=0),
                        bounds_check=NP - 1, oob_is_err=False).then_inc(fx_in[e % 2], 16)
            gather(0)
            gather(1)
            for e in range(E1):
                if e + 2 < E1:
                    gather(e + 2)
                pool.wait_ge(fy_ready, e + 1)
                if e:
                    pool.wait_ge(y_out, 16 * B1 * e)
                for b in range(B1):
                    pool.indirect_dma_start(
                        out[:, :], bass.IndirectOffsetOnAxis(ap=SI[:, e, b:b + 1], axis=0), fy[e % 2][:, b, :], None,
                        bounds_check=N - 1, oob_is_err=False, compute_op=ALU.add).then_inc(y_out, 16)
            pool.wait_ge(y_out, 16 * B1 * E1)
            end_stage(pool, 6)

        @block.scalar
        def _(act):
            def norm_root(n):
                act.wait_ge(var_ready, n)
                act.activation(stat[:, 1, :], stat[:, 0, :], ACT.Sqrt).then_inc(std_ready, 1)

            norm_root(1)

            def high_halves(k, par, first):
                act.wait_ge(xn0_ready, k + 1)
                act.copy(XS[:, k, HI:HI + D], xn0[par][:, :]).then_inc(hi_copied, 1)
            pipelined(act, T, [(high_halves, 0)])
            act.wait_ge(fold_done, 2)
            act.copy(WF[:, 0:KC, :].rearrange("p c n -> p (c n)"), banks[6][:, :]).then_inc(fold_copied, 1)
            act.copy(WF[:, KC:2 * KC, :].rearrange("p c n -> p (c n)"), banks[7][:, :]).then_inc(fold_copied, 1)

            def copy_saT(k, par, first):
                act.wait_ge(saT_done, k + 1)
                if not first:
                    act.wait_ge(comb_done, k - 1)
                act.copy(saT[par][:, :, :].rearrange("p a b -> p (a b)"), banks[2][:, :]).then_inc(saT_copied, 1)

            def keep_mask(k, par, first):
                act.wait_ge(mask_ready, 2 * k + 2)
                act.copy(M[:, :, cols(k, P)], mt[par][:, :, :]).then_inc(m_kept, 1)

            def root(k, par, first):
                act.wait_ge(vr_ready, k + 1)
                act.activation(sd[par][:, 0:1], mv[par][:, 1:2], ACT.Sqrt).then_inc(sd_ready, 1)

            def copy_x1T(k, par, first):
                act.wait_ge(x1T_done, k + 1)
                if not first:
                    act.wait_ge(lg_done, k - 1)
                act.copy(xTb[par][:, :, :].rearrange("p a b -> p (a b)"), banks[4][:, 0:D]).then_inc(x1T_copied, 1)

            def copy_logits(k, par, first):
                act.wait_ge(lg_done, k + 1)
                if not first:
                    act.wait_ge(oh_made, k - 1)
                act.copy(lgb[par][:, :], banks[5][:, 0:E0]).then_inc(lg_copied, 1)
                act.wait_ge(lg_copied, 2 * k + 1)
                act.copy(LG[:, k, :], lgb[par][:, :]).then_inc(lg_copied, 1)
            pipelined(act, T, [(root, 2), (copy_saT, 1), (copy_logits, 3), (keep_mask, -1), (copy_x1T, 2)])
            end_stage(act, 1)

            act.wait_ge(exp_in, 2)
            act.activation(EXs[:, :, :], EXs[:, :, :], ACT.Exp).then_inc(exp_out, 1)
            act.activation(EX6[:, :, :], EX6[:, :, :], ACT.Exp).then_inc(exp_out, 1)

            def copy_exT(k, par, first, j):
                if j == 0 and not first:
                    act.wait_ge(exgu_done, 2 * k - 2)
                nb = min(2, B0 - 2 * j)
                act.wait_ge(exT_done, 3 * k + j + 1)
                act.copy(ex_T[par][:, :, 2 * j * P:(2 * j + nb) * P],
                         banks[(par + j) % 2][:, 0:KC * nb * P].rearrange("p (c n) -> p c n", c=KC)
                         ).then_inc(exT_copied, 1)

            def silu_expert(k, par, first):
                if not first:
                    act.wait_ge(exac_ready, 2 * k - 2)
                for h in range(2):
                    act.wait_ge(exgu_done, 2 * k + h + 1)
                    act.activation(ex_sg[par][:, cols(h, S0 // 2)], banks[2 + 2 * h][:, 0:S0 // 2],
                                   ACT.Silu).then_inc(exsg_ready, 1)

            def copy_exy(k, par, first):
                if not first:
                    act.wait_ge(exy_out[par], (k - par) * 8)
                for j in range(3):
                    nb = min(2, B0 - 2 * j)
                    act.wait_ge(exy_done, 3 * k + j + 1)
                    act.copy(ex_y[par][:, 2 * j:2 * j + nb, :].rearrange("p b d -> p (b d)"),
                             banks[6 + (par + j) % 2][:, 0:nb * D]).then_inc(exy_copied, 1)
            pipelined(act, E0, [(lambda k, par, first: copy_exT(k, par, first, 0), -1), (silu_expert, 0),
                                (lambda k, par, first: copy_exT(k, par, first, 2), -1), (copy_exy, 1)])
            end_stage(act, 2)

            act.wait_ge(va_done, 1)
            act.copy(W2[:, :, D:D + 2], banks[7][:, 0:2 * KC].rearrange("p (c n) -> p c n", c=KC)).then_inc(va_copied, 1)
            act.wait_ge(bound_done, 1)
            act.activation(SC[:, 1:2], banks[5][:, 0:1], ACT.Sqrt, scale=1.02 * D).then_inc(bound_ready, 1)

            def copy_xT(k, par, first):
                act.wait_ge(xT_done, k + 1)
                if not first:
                    act.wait_ge(hgu_done, 2 * k - 2)
                act.copy(xT[par][:, :, :].rearrange("p a b -> p (a b)"), banks[0][:, 0:D]).then_inc(xT_copied, 1)

            def silu_shared(k, par, first):
                if not first:
                    act.wait_ge(acs_ready, 2 * k - 2)
                for s in range(SH):
                    act.wait_ge(hgu_done, 2 * k + s + 1)
                    act.activation(sgs[par][:, s, :], banks[2 + s][:, 0:P], ACT.Silu).then_inc(sg_ready, 1)

            def root_c(k, par, first):
                act.wait_ge(vc_ready, k + 1)
                act.activation(sdc[par][:, 0:1], mvc[par][:, 1:2], ACT.Sqrt).then_inc(sc_ready, 1)

            def copy_gxT(k, par, first):
                act.wait_ge(gxT_done, k + 1)
                if not first:
                    act.wait_ge(h_done, k - 1)
                act.copy(gxT[par][:, :, :].rearrange("p a b -> p (a b)"), banks[1][:, 0:D]).then_inc(gxT_copied, 1)

            def copy_h(k, par, first):
                act.wait_ge(h_done, k + 1)
                act.copy(H[:, k, 0:D], banks[6 + par][:, 0:D]).then_inc(h_copied, 1)
                act.copy(SD[:, k, :], banks[6 + par][:, D:D + 2]).then_inc(h_copied, 1)
            pipelined(act, T, [(root_c, 2), (copy_xT, -1), (silu_shared, 0), (copy_h, 3), (copy_gxT, 2)])
            end_stage(act, 3)

            def copy_rows(b):
                o, w = ABLOCKS[b]
                for i in range(2):
                    act.wait_ge(pb_done, 2 * b + i + 1)
                    act.copy((PB, QB)[i][:, o:o + w], banks[4 * (b % 2) + i][:, 0:w]).then_inc(pb_copied, 1)
            copy_rows(0)
            for bi, (o, w) in enumerate(ABLOCKS):
                base = T * bi
                act.wait_ge(pb_copied, 2 * bi + 2)

                def attend_sum(k, par, first):
                    if not first or bi:
                        act.wait_ge(at2_ready, k + base - 1)
                    act.activation(at1[par][:, 0:w], PB[:, o:o + w], ACT.Identity,
                                   bias=dcol[:, 0, k:k + 1] if isinstance(k, int) else dcol[:, 0, bass.ds(k, 1)]
                                   ).then_inc(at1_ready, 1)

                def attend_exp(k, par, first):
                    act.wait_ge(at2_ready, k + base + 1)
                    act.activation(at2[par][:, 0:w], at2[par][:, 0:w], ACT.Exp).then_inc(ate_ready, 1)

                def rows_beside(k, par, first):
                    if isinstance(k, int) and k == PEEL + 4 and bi + 1 < len(ABLOCKS):
                        copy_rows(bi + 1)
                pipelined(act, T, [(attend_sum, 0), (attend_exp, 1), (rows_beside, 0)], peel=PEEL + 2)
            end_stage(act, 4)

            norm_root(2)

            def copy_fxT(k, par, first):
                act.wait_ge(fxT_done, k + 1)
                if not first:
                    act.wait_ge(fl_done, k - 1)
                act.copy(fxT[par][:, :, :].rearrange("p a b -> p (a b)"), banks[par][:, :]).then_inc(fxT_copied, 1)

            def keep_fx(k, par, first):
                act.wait_ge(fxg_ready, k + 1)
                act.copy(XR[:, cols(k, GT), 0:D],
                         fxg[par][:, :, :].rearrange("p (t c) b -> p t (c b)", t=GT)).then_inc(fx_kept, 1)
            pipelined(act, G, [(keep_fx, 0), (copy_fxT, 0)])
            act.wait_ge(aff_in, 1)
            act.activation(AF[:, :, :], AF[:, :, :], ACT.Exp).then_inc(aff_out, 1)
            end_stage(act, 5)

            act.wait_ge(w3_in, 48)

            def gelu(k, par, first):
                if not first:
                    act.wait_ge(fy_done, 2 * k - 2)
                for h in range(KC):
                    act.wait_ge(fh_done, 2 * k + h + 1)
                    act.activation(fh[par][:, h, :], banks[2 + h][:, :], ACT.Gelu_apprx_tanh,
                                   bias=b1c[:, k, h:h + 1]).then_inc(fh_ready, 1)
            pipelined(act, E1, [(gelu, 0)])
            end_stage(act, 6)

        @block.vector
        def _(dve):
            c = Chain(dve, dve_done)
            norms = [0]

            def layer_norm():
                norms[0] += 1
                c.inc(dve.tensor_tensor(stat[:, 0, :], bn[:, :, 1], bn[:, :, 4], ALU.add))
                c.inc(dve.tensor_tensor(stat[:, 1, :], bn[:, :, 1], bn[:, :, 4], ALU.subtract))
                c.inc(dve.tensor_tensor(stat[:, 2, :], bn[:, :, 2], bn[:, :, 5], ALU.add))
                c.wait()
                c.inc(dve.tensor_scalar(mean[:, :], stat[:, 0, :], 0.5, None, ALU.mult))
                c.inc(dve.scalar_tensor_tensor(stat[:, 1, :], stat[:, 1, :], 0.25, stat[:, 1, :], ALU.mult, ALU.mult))
                c.wait()
                c.inc(dve.scalar_tensor_tensor(stat[:, 0, :], stat[:, 2, :], 1.0 / D, stat[:, 1, :], ALU.mult, ALU.add))
                c.wait()
                dve.tensor_scalar(stat[:, 0, :], stat[:, 0, :], EPS, None, ALU.add).then_inc(var_ready, 1)
                dve.wait_ge(std_ready, norms[0])
                c.inc(dve.reciprocal(rstd[:, :], stat[:, 1, :]))
                c.wait()

            def normalise(dst, t):
                return dve.tensor_scalar(dst, X[:, t, :], mean[:, bass.ds(t, 1)], rstd[:, bass.ds(t, 1)],
                                         ALU.subtract, ALU.mult)

            def normalise_group(dst, k):
                for u in range(GT - 1):
                    c.inc(normalise(dst[:, cols(u, KC), :].rearrange("p a b -> p (a b)"), k * GT + u))
                return normalise(dst[:, (GT - 1) * KC:GT * KC, :].rearrange("p a b -> p (a b)"), k * GT + GT - 1)

            def stand_alone():
                dve.memset(SC[0:1, 8:9], 0.0)

            for (a, z), s in zip(XPARTS, x_in):
                dve.wait_ge(s, 16)
                for t in range(a, z):
                    c.inc(dve.bn_stats(bn[:, t, :], X[:, t, :]))
            c.wait()
            layer_norm()

            def rows0(k, par, first):
                if not first:
                    dve.wait_ge(hi_copied, k - 1)
                    dve.wait_ge(lo_ready, k - 1)
                normalise(xn0[par][:, :], k).then_inc(xn0_ready, 1)

            def low_halves(k, par, first):
                dve.wait_ge(hi_copied, k + 1)
                dve.tensor_tensor(XS[:, k, LO:LO + D], xn0[par][:, :], XS[:, k, HI:HI + D],
                                  ALU.subtract).then_inc(lo_ready, 1)
            pipelined(dve, T, [(rows0, 0), (low_halves, 1)])
            dve.wait_ge(lo_ready, T)
            c.wait()
            dve.tensor_copy(dg[0][:, :], XS[:, 0, 0:2]).then_inc(xs_ready, 1)
            dve.wait_ge(fold_done, 3)
            dve.wait_ge(w0_in, 128)
            dve.tensor_tensor(BF[:, :], banks[5][0:1, 0:D], bcomb[:, :], ALU.add).then_inc(fold_copied, 1)

            dve.wait_ge(bias_done, 1)
            c.inc(dve.tensor_copy(BFb[:, :], banks[5][:, 0:D]))
            c.wait()

            def masks(k, par, first):
                if not first:
                    dve.wait_ge(agg_done, k - 1)
                    dve.wait_ge(m_kept, k - 1)
                for h in range(2):
                    dve.wait_ge(adj_in[h], 16 * k + 16)
                    dve.tensor_scalar(mt[par][:, h * HT:(h + 1) * HT, :], adj[h][:, :, :], 0, None,
                                      ALU.is_gt).then_inc(mask_ready, 1)

            def mean_of_neighbours(k, par, first):
                dve.wait_ge(agg_done, k + 1)
                if not first:
                    dve.wait_ge(saT_done, k - 1)
                c.inc(normalise(sa[par][:, 0:KC, :].rearrange("p a b -> p (a b)"), k))
                c.inc(dve.tensor_scalar(dg[par][:, 0:1], banks[par][:, D:D + 1], 1.0, None, ALU.max))
                c.wait()
                c.inc(dve.reciprocal(dg[par][:, 1:2], dg[par][:, 0:1]))
                c.wait()
                dve.tensor_scalar(sa[par][:, KC:2 * KC, :].rearrange("p a b -> p (a b)"), banks[par][:, 0:D],
                                  dg[par][:, 1:2], None, ALU.mult).then_inc(sa_ready, 1)

            def residual0(k, par, first):
                dve.wait_ge(comb_done, k + 1)
                dve.tensor_tensor(pre[:, :], banks[3][:, 0:D], BFb[:, :], ALU.add).then_inc(comb_read, 1)
                dve.wait_ge(comb_read, k + 1)
                dve.scalar_tensor_tensor(X[:, k, :], pre[:, :], 0.0, X[:, k, :], ALU.max,
                                         ALU.add).then_inc(x1_ready, 1)
                dve.wait_ge(x1_ready, k + 1)
                stand_alone()
                c.inc(dve.bn_stats(bnb[par][:, :], X[:, k, :]))
                c.wait()
                stand_alone()
                c.inc(dve.bn_aggr(mv[par][:, :], bnb[par][:, :]))
                c.wait()
                dve.tensor_scalar(mv[par][:, 1:2], mv[par][:, 1:2], EPS, None, ALU.add).then_inc(vr_ready, 1)

            def norm1(k, par, first):
                dve.wait_ge(sd_ready, k + 1)
                c.inc(dve.reciprocal(sd[par][:, 1:2], sd[par][:, 0:1]))
                c.wait()
                if not first:
                    dve.wait_ge(x1T_done, k - 1)
                    dve.wait_ge(xn_out[par], (k - par) * 8)
                dve.tensor_scalar(xnb[par][:, :, :].rearrange("p a b -> p (a b)"), X[:, k, :], mv[par][:, 0:1],
                                  sd[par][:, 1:2], ALU.subtract, ALU.mult).then_inc(xn_ready, 1)

            def choose(k, par, first):
                dve.wait_ge(lg_copied, 2 * k + 1)
                stand_alone()
                c.inc(dve.max(mx8b[par][:, :], lgb[par][:, :]))
                c.wait()
                stand_alone()
                c.inc(dve.max_index(ix8b[par][:, :], mx8b[par][:, :], lgb[par][:, :]))
                c.inc(dve.tensor_copy(MX8[:, k, :], mx8b[par][:, :]))
                c.wait()
                if not first:
                    dve.wait_ge(pos_done, k)
                dve.tensor_tensor(OH[par][:, :, :], iota64[:, :].unsqueeze(1).broadcast_to([P, K0, E0]),
                                  ix8b[par][:, 0:K0].unsqueeze(2).broadcast_to([P, K0, E0]),
                                  ALU.is_equal).then_inc(oh_made, 1)

            def assign(k, par, first):
                dve.wait_ge(pos_done, k + 1)
                dve.tensor_tensor(OHP[:, :, :], OH[par][:, :, :],
                                  banks[6][:, 0:E0].unsqueeze(1).broadcast_to([P, K0, E0]), ALU.mult).then_inc(pos_read, 1)
                dve.wait_ge(pos_read, k + 1)
                c.inc(dve.tensor_reduce(r6[:, 0, :], OHP[:, :, :], AX, ALU.add))
                c.wait()
                c.inc(dve.tensor_scalar(VAL[:, k, :], r6[:, 0, :], float(CAP0), None, ALU.is_lt))
                c.inc(dve.scalar_tensor_tensor(r6[:, 1, :], ix8b[par][:, 0:K0], float(S0), r6[:, 0, :], ALU.mult, ALU.add))
                c.wait()
                c.inc(dve.tensor_scalar(r6[:, 2, :], VAL[:, k, :], -SKIP, SKIP, ALU.mult, ALU.add))
                c.inc(dve.scalar_tensor_tensor(r6[:, 3, :], r6[:, 1, :], -float(ZROW), VAL[:, k, :], ALU.add, ALU.mult))
                c.wait()
                dve.tensor_tensor(DS[:, k, :], r6[:, 1, :], r6[:, 2, :], ALU.add).then_inc(rows_ready, 1)
                c.inc(dve.tensor_scalar(DG[:, k, :], r6[:, 3, :], float(ZROW), None, ALU.add))
            pipelined(dve, T, [(mean_of_neighbours, 1), (residual0, 2), (masks, -1), (norm1, 2), (choose, 4),
                               (assign, 5)], c)
            end_stage(dve, 1)

            dve.tensor_tensor(EXs[:, :, :], LG[:, :, :], MX8[:, :, 0:1].broadcast_to([P, T, E0]),
                              ALU.subtract).then_inc(exp_in, 1)
            dve.tensor_tensor(EX6[:, :, :], MX8[:, :, 0:K0], MX8[:, :, 0:1].broadcast_to([P, T, K0]),
                              ALU.subtract).then_inc(exp_in, 1)
            dve.wait_ge(exp_out, 2)
            c.inc(dve.tensor_reduce(stat[:, 0, :], EXs[:, :, :], AX, ALU.add))
            c.inc(dve.tensor_reduce(stat[:, 1, :], EX6[:, :, :], AX, ALU.add))
            c.wait()
            c.inc(dve.scalar_tensor_tensor(stat[:, 0, :], stat[:, 0, :], 1e-9, stat[:, 1, :], ALU.mult, ALU.add))
            c.wait()
            c.inc(dve.reciprocal(stat[:, 1, :], stat[:, 0, :]))
            c.wait()
            c.inc(dve.tensor_tensor(G6[:, :, :], EX6[:, :, :], bc(stat[:, 1, :], [P, T, K0], 2), ALU.mult))

            def copy_exT1(k, par, first):
                if not first:
                    dve.wait_ge(exgu_done, 2 * k - 2)
                dve.wait_ge(exT_done, 3 * k + 2)
                dve.tensor_copy(ex_T[par][:, :, 2 * P:4 * P],
                                banks[(par + 1) % 2][:, :].rearrange("p (c n) -> p c n", c=KC)).then_inc(exT_mid, 1)

            def gate_expert(k, par, first):
                if not first:
                    dve.wait_ge(exy_done, 3 * k - 3)
                for h in range(2):
                    dve.wait_ge(exsg_ready, 2 * k + h + 1)
                    dve.tensor_tensor(ex_ac[par][:, cols(h, S0 // 2)], banks[3 + 2 * h][:, 0:S0 // 2],
                                      ex_sg[par][:, cols(h, S0 // 2)], ALU.mult).then_inc(exac_ready, 1)
            pipelined(dve, E0, [(copy_exT1, -1), (gate_expert, 0)])
            end_stage(dve, 2)

            dve.memset(H[:, :, D:HW], 1.0).then_inc(h_ones, 1)
            c.inc(dve.memset(acc[:, :], 0.0))
            dve.wait_ge(va_copied, 1)
            dve.wait_ge(h_ones, 1)
            c.inc(dve.tensor_tensor(SC[:, 4:6], W2[:, :, D + 1], W2[:, :, D + 1], ALU.mult))
            c.inc(dve.tensor_scalar(H[:, T - 1, D:HW], H[:, T - 1, D:HW], padm[:, 0:1], None, ALU.mult))
            c.wait()
            dve.tensor_tensor(SC[:, 6:7], SC[:, 4:5], SC[:, 5:6], ALU.add).then_inc(sq_sum, 1)
            dve.wait_ge(bound_ready, 1)

            def gate_shared(k, par, first):
                if not first:
                    dve.wait_ge(sd_done, k - 1)
                for s in range(SH):
                    dve.wait_ge(sg_ready, 2 * k + s + 1)
                    dve.scalar_tensor_tensor(acs[par][:, s, :], banks[2 + s][:, P:2 * P], 1.0 / SH, sgs[par][:, s, :],
                                             ALU.mult, ALU.mult).then_inc(acs_ready, 1)

            def diagonal(k, par, first):
                if not first:
                    dve.wait_ge(sd_done, k - 1)
                dve.tensor_tensor(dgc[par][:, :, :], bc(ident[:, :], [P, K0, P], 1), bc(G6[:, k, :], [P, K0, P], 2),
                                  ALU.mult).then_inc(dgc_ready, 1)

            def add_ffn(k, par, first):
                dve.wait_ge(sd_done, k + 1)
                dve.tensor_tensor(X[:, k, :], banks[4 + par][:, 0:D], X[:, k, :], ALU.add).then_inc(sd_read, 1)
                dve.wait_ge(sd_read, k + 1)
                stand_alone()
                c.inc(dve.bn_stats(bnc[par][:, :], X[:, k, :]))
                c.wait()
                stand_alone()
                c.inc(dve.bn_aggr(mvc[par][:, :], bnc[par][:, :]))
                c.wait()
                dve.tensor_scalar(mvc[par][:, 1:2], mvc[par][:, 1:2], EPS, None, ALU.add).then_inc(vc_ready, 1)

            def norm2(k, par, first):
                dve.wait_ge(sc_ready, k + 1)
                c.inc(dve.reciprocal(sdc[par][:, 1:2], sdc[par][:, 0:1]))
                c.wait()
                if not first:
                    dve.wait_ge(gxT_done, k - 1)
                dve.tensor_scalar(gx[par][:, :, :].rearrange("p a b -> p (a b)"), X[:, k, :], mvc[par][:, 0:1],
                                  sdc[par][:, 1:2], ALU.subtract, ALU.mult).then_inc(gx_ready, 1)

            def best(k, par, first):
                dve.wait_ge(h_copied, 2 * k + 2)
                c.inc(dve.tensor_scalar(dcol[:, 2, bass.ds(k, 1)], SD[:, k, 1:2], SC[:, 1:2], 1.0, ALU.add, ALU.add))
                c.wait()
                c.inc(dve.scalar_tensor_tensor(acc[:, :], M[:, k, :], dcol[:, 2, bass.ds(k, 1)], acc[:, :], ALU.mult,
                                               ALU.max))
            pipelined(dve, T, [(best, 4), (gate_shared, 0), (diagonal, 0), (norm2, 2), (add_ffn, 1)], c)
            c.inc(dve.tensor_copy(dcol[:, 0, :], SD[:, :, 1]))
            c.inc(dve.tensor_scalar(dcol[:, 1, :], SD[:, :, 1], ALPHA, None, ALU.mult))
            end_stage(dve, 3)

            for j, (o, w) in enumerate(ABLOCKS):
                dve.wait_ge(accT_done, j + 1)
                ins = dve.tensor_reduce(MM[:, 0, o // P:(o + w) // P],
                                        banks[4 + j % 4][:, 0:w].rearrange("p (a b) -> p a b", b=P), AX, ALU.max)
                ins.then_inc(accT_read, 1)
            dve.wait_ge(accT_read, len(ABLOCKS))
            c.inc(dve.tensor_scalar(MM[:, 1, :], MM[:, 0, :], SC[:, 1:2], -1.0, ALU.subtract, ALU.add))
            c.wait()
            c.inc(dve.tensor_tensor(MM[:, 1, :], MM[:, 1, :], SD[:, :, 0], ALU.add))
            c.wait()
            c.inc(dve.scalar_tensor_tensor(MM[:, 2, :], MM[:, 1, :], ALPHA, MM[:, 1, :], ALU.mult, ALU.max))
            c.wait()
            c.inc(dve.tensor_tensor(MM[:, 3, :], SD[:, :, 0], MM[:, 2, :], ALU.subtract))
            c.inc(dve.scalar_tensor_tensor(MM[:, 4, :], SD[:, :, 0], ALPHA, MM[:, 2, :], ALU.mult, ALU.subtract))
            c.wait()

            def diagonal_of(b, i):
                o, w = ABLOCKS[b]
                n = w // P
                if b:
                    dve.wait_ge(pb_done, 2 * b)
                dve.tensor_tensor(dgn[i][:, 0:n, :], bc(ident[:, :], [P, n, P], 1),
                                  bc(MM[:, 3 + i, o // P:o // P + n], [P, n, P], 2), ALU.mult
                                  ).then_inc(dgn_ready, 1)

            def weigh_sums(b, q):
                src = banks[4 * (b % 2) + q]
                if q == 0:
                    dve.wait_ge(blk_done, b + 1)
                c.inc(dve.tensor_scalar(SC[:, 2:3], src[:, D:D + 1], 0.5, None, ALU.is_lt))
                c.wait()
                ins = dve.scalar_tensor_tensor(num[q % 2][:, 0:D + 1], HS[:, 0:D + 1], SC[:, 2:3], src[:, 0:D + 1],
                                               ALU.mult, ALU.add)
                if q == ABLOCKS[b][1] // P - 1:
                    ins.then_inc(blk_read, 1)
                    dve.wait_ge(blk_read, b + 1)
                else:
                    c.inc(ins)

            def add_sums(b, q):
                t = ABLOCKS[b][0] // P + q
                c.wait()
                c.inc(dve.reciprocal(SC[:, 3:4], num[q % 2][:, D:D + 1]))
                c.wait()
                c.inc(dve.scalar_tensor_tensor(X[:, t, :], num[q % 2][:, 0:D], SC[:, 3:4], X[:, t, :], ALU.mult,
                                               ALU.add))

            def spread(b, tiles):
                c.wait()
                for q in range(*tiles):
                    t = ABLOCKS[b][0] // P + q
                    c.inc(dve.bn_stats(bn[:, t, :], X[:, t, :]))
            diagonal_of(0, 0)
            diagonal_of(0, 1)

            for bi, (o, w) in enumerate(ABLOCKS):
                base = T * bi
                dve.wait_ge(pb_copied, 2 * bi + 2)

                def attend_max(k, par, first):
                    dve.wait_ge(at1_ready, k + base + 1)
                    if not first or bi:
                        dve.wait_ge(atp_ready, k + base - 1)
                    dve.scalar_tensor_tensor(at2[par][:, 0:w], QB[:, o:o + w],
                                             dcol[:, 1, bass.ds(k, 1)], at1[par][:, 0:w], ALU.add,
                                             ALU.max).then_inc(at2_ready, 1)

                def attend_mask(k, par, first):
                    dve.wait_ge(ate_ready, k + base + 1)
                    if not first or bi:
                        dve.wait_ge(atp_used, k + base - 1)
                    dve.scalar_tensor_tensor(atp[par][:, 0:w], at2[par][:, 0:w], 1.0, M[:, k, o:o + w], ALU.min,
                                             ALU.mult).then_inc(atp_ready, 1)

                def beside(k, par, first):
                    if not isinstance(k, int):
                        return
                    if bi and 1 <= k <= 2 * AW // P:
                        (weigh_sums, add_sums)[(k - 1) % 2](bi - 1, (k - 1) // 2)
                    if k in (PEEL - 1, PEEL) and bi + 1 < len(ABLOCKS):
                        diagonal_of(bi + 1, k - (PEEL - 1))
                    if bi and k > PEEL:
                        spread(bi - 1, (0, 2) if k == PEEL + 1 else (2, 4))
                    if k == PEEL + 2 and bi == 0:
                        dve.wait_ge(hs_done, 1)
                        dve.tensor_copy(HS[:, 0:D + 1], banks[7][:, 0:D + 1]).then_inc(hs_read, 1)
                        dve.wait_ge(hs_read, 1)
                pipelined(dve, T, [(attend_max, 0), (attend_mask, 1), (beside, 0)], peel=PEEL)
            last = len(ABLOCKS) - 1
            for q in range(ABLOCKS[last][1] // P):
                weigh_sums(last, q)
                add_sums(last, q)
            spread(last, (0, ABLOCKS[last][1] // P))
            c.wait()
            end_stage(dve, 4)

            layer_norm()

            def xn_group2(k, par, first):
                if not first:
                    dve.wait_ge(fxT_done, k - 1)
                    dve.wait_ge(fx_kept, k - 1)
                normalise_group(fxg[par], k).then_inc(fxg_ready, 1)

            def read_gates(k, par, first):
                dve.wait_ge(fl_done, k + 1)
                dve.tensor_copy(AF[:, cols(k, GT), :].rearrange("p t e -> p (t e)"),
                                banks[2 + par][:, 0:GT * E1]).then_inc(fl_read, 1)
            pipelined(dve, G, [(xn_group2, -2), (read_gates, 0)], c)
            dve.wait_ge(fl_read, G)
            c.inc(dve.tensor_reduce(stat[:, 0, :], AF[:, :, :], AX, ALU.max))
            c.wait()
            dve.tensor_tensor(AF[:, :, :], AF[:, :, :], bc(stat[:, 0, :], [P, T, E1], 2),
                              ALU.subtract).then_inc(aff_in, 1)
            dve.wait_ge(aff_out, 1)
            c.inc(dve.tensor_reduce(stat[:, 0, :], AF[:, :, :], AX, ALU.add))
            c.wait()
            c.inc(dve.reciprocal(stat[:, 1, :], stat[:, 0, :]))
            c.wait()
            c.inc(dve.tensor_tensor(AF[:, :, :], AF[:, :, :], bc(stat[:, 1, :], [P, T, E1], 2), ALU.mult))
            c.wait()
            c.inc(dve.tensor_scalar(AF[:, T - 1, :], AF[:, T - 1, :], padm[:, 0:1], padn[:, 0:1], ALU.mult, ALU.add))
            c.wait()
            dve.tensor_copy(XR[:, :, D:XW], AF[:, :, :]).then_inc(xr_ready, 1)

            c.inc(dve.memset(thr[:, :], 0))
            for j in range(3):
                c.inc(dve.memset(digit[:, j, :], (j + 1) << (TOP_BIT - 1)))
            c.inc(dve.memset(bitf[:, :, :], float(1 << (TOP_BIT - 1))))
            c.wait()

            def two_bits(i):
                c.inc(dve.tensor_tensor(cand[:, :, :], bc(thr[:, :], [P, 3, E1], 1), digit[:, :, :], ALU.bitwise_or))
                c.wait()
                for h in range(2):
                    ts = slice(h * HT, (h + 1) * HT)
                    dve.tensor_tensor(cmp3[:, ts, :, :],
                                      bc(AF[:, ts, :], [P, HT, 3, E1], 2),
                                      bc(cand[:, :, :].bitcast(F32), [P, HT, 3, E1], 1),
                                      ALU.is_ge).then_inc(cmp_ready, 1)
                c.inc(dve.tensor_scalar(digit[:, :, :], digit[:, :, :], 2, None, ALU.logical_shift_right))
                dve.wait_ge(cnt_done, i + 1)
                c.inc(dve.scalar_tensor_tensor(stepf[:, :, :].rearrange("p j e -> p (j e)"), banks[4][:, 0:3 * E1],
                                               float(CAP1), bitf[:, :, :].rearrange("p j e -> p (j e)"), ALU.is_ge,
                                               ALU.mult))
                c.wait()
                c.inc(dve.tensor_scalar(bitf[:, :, :], bitf[:, :, :], 0.25, None, ALU.mult))
                c.inc(dve.tensor_tensor(stepf[:, 0, :], stepf[:, 0, :], stepf[:, 1, :], ALU.add))
                c.wait()
                c.inc(dve.tensor_tensor(stepi[:, :], stepf[:, 0, :], stepf[:, 2, :], ALU.add))
                c.wait()
                c.inc(dve.tensor_tensor(thr[:, :], thr[:, :], stepi[:, :], ALU.bitwise_or))
                c.wait()
            def rounds(i):
                for n in range(ROUNDS):
                    two_bits(i * ROUNDS + n)
            each(dve, (TOP_BIT + 1) // 2 // ROUNDS, rounds, c, 7 * ROUNDS)

            tb = bc(thr[:, :].bitcast(F32), [P, T, E1], 1)
            c.inc(dve.tensor_tensor(A16[:, :, :], AF[:, :, :], tb, ALU.is_gt))
            c.wait()
            dve.tensor_tensor(S16[:, :, :], AF[:, :, :], tb, ALU.is_equal).then_inc(sel1_ready, 1)
            dve.wait_ge(sel1_done, 1)
            w = T * E1
            c.inc(dve.tensor_copy(SL[:, :, :].rearrange("p t e -> p (t e)"), banks[5][:, 0:w]))
            c.wait()
            c.inc(dve.tensor_tensor(SL[:, :, :], SL[:, :, :], bc(banks[7][:, 0:E1], [P, T, E1], 1), ALU.add))
            c.wait()
            c.inc(dve.scalar_tensor_tensor(SL[:, :, :], SL[:, :, :], float(CAP1), S16[:, :, :], ALU.is_lt, ALU.mult))
            c.wait()
            dve.tensor_tensor(S16[:, :, :], A16[:, :, :], SL[:, :, :], ALU.add).then_inc(sel1_ready, 1)
            dve.wait_ge(sel1_done, 2)
            c.inc(dve.scalar_tensor_tensor(SL[:, :, :].rearrange("p t e -> p (t e)"), banks[6][:, 0:w], 1.0,
                                           S16[:, :, :].rearrange("p t e -> p (t e)"), ALU.add, ALU.mult))
            c.wait()
            c.inc(dve.tensor_scalar(SLI[:, :, :], SL[:, :, :], -1.0, None, ALU.add))
            c.wait()
            c.inc(dve.tensor_scalar(HB[:, :, :].bitcast(I32), SLI[:, :, :], 7, None,
                                    ALU.arith_shift_right))
            c.inc(dve.tensor_scalar(LOW[:, :, :].bitcast(I32), SLI[:, :, :], P - 1, None, ALU.bitwise_and))
            c.wait()
            c.inc(dve.tensor_copy(HB[:, :, :], HB[:, :, :].bitcast(I32)))
            c.inc(dve.tensor_copy(LO16[:, :, :], LOW[:, :, :].bitcast(I32)))
            c.wait()

            dve.drain().then_inc(low_ready, 1)
            c.inc(dve.tensor_tensor(inblock[:, :, :, :].rearrange("p t e b -> p (t e) b"),
                                    bc(HB[:, :, :].rearrange("p t e -> p (t e)"), [P, w, B1], 2),
                                    bc(slots16[:, 0:B1], [P, w, B1], 1), ALU.is_equal))
            c.wait()
            c.inc(dve.tensor_tensor(R8[:, :, :, :, 0].rearrange("p t e b -> p t (e b)"),
                                    inblock[:, :, :, :].rearrange("p t e b -> p t (e b)"),
                                    bc(tokp[:, :, 0], [P, T, E1 * B1], 2), ALU.mult))
            c.inc(dve.tensor_tensor(R8[:, :, :, :, 1].rearrange("p t e b -> p t (e b)"),
                                    inblock[:, :, :, :].rearrange("p t e b -> p t (e b)"),
                                    bc(tokp[:, :, 1], [P, T, E1 * B1], 2), ALU.mult))
            c.wait()

            def one_hot(t, par, first):
                if not first:
                    dve.wait_ge(oh_used, t - 1)
                dve.tensor_tensor(oh1[par][:, 0:DVE_E, :], bc(slots16[:, 0:P], [P, DVE_E, P], 1),
                                  bc(LO16[:, t, 0:DVE_E], [P, DVE_E, P], 2), ALU.is_equal).then_inc(oh_ready, 1)
            pipelined(dve, T, [(one_hot, 0)])
            dve.wait_ge(lt_done, 1)
            LT = banks[4][:, 0:E1 * B1 * 2].rearrange("p (e b n) -> p e b n", e=E1, b=B1)
            c.inc(dve.tensor_scalar(LI[:, :, :], LT[:, :, :, 0], float(P), None, ALU.mult))
            c.wait()
            c.inc(dve.tensor_tensor(LI[:, :, :], LI[:, :, :], LT[:, :, :, 1], ALU.add))
            c.wait()
            c.inc(dve.tensor_copy(GI[:, :, :], LI[:, :, :]))
            c.inc(dve.tensor_tensor(SI[:, :, :], LI[:, :, :], bc(tail[:, :], [P, E1, B1], 1), ALU.add))
            end_stage(dve, 5)

            def copy_fT(k, par, first):
                if not first:
                    dve.wait_ge(fh_done, 2 * k - 2)
                for j in range(2):
                    dve.wait_ge(fT_done, 2 * k + j + 1)
                    dve.tensor_copy(fT[par][:, :, cols(j, 2 * P)],
                                    banks[j][:, :].rearrange("p (c n) -> p c n", c=KC)).then_inc(fT_read, 1)

            def keep_gates(k, par, first):
                dve.wait_ge(fx_in[par], (k - par) * (8 * B1) + 16 * B1)
                if not first:
                    dve.wait_ge(fy_ready, k - 1)
                dve.tensor_scalar(gcol[par][:, :], fx[par][:, :, bass.ds(k + D, 1)].rearrange("p b o -> p (b o)"), 1.0,
                                  None, ALU.mult).then_inc(g_kept, 1)

            def weigh(k, par, first):
                if not first:
                    dve.wait_ge(y_out, (k - 1) * (16 * B1))
                for j in range(B1 // 2):
                    dve.wait_ge(fy_done, 2 * k + j + 1)
                    c.inc(dve.tensor_tensor(fy[par][:, 2 * j:2 * j + 2, :],
                                            banks[4 + 2 * par + j][:, :].rearrange("p (b d) -> p b d", b=2),
                                            b2b[:, bass.ds(k, 1), :].broadcast_to([P, 2, D]), ALU.add))
                c.wait()
                dve.wait_ge(g_kept, k + 1)
                for b in range(B1):
                    ins = dve.tensor_scalar(fy[par][:, b, :], fy[par][:, b, :], gcol[par][:, b:b + 1], None, ALU.mult)
                    if b < B1 - 1:
                        c.inc(ins)
                ins.then_inc(fy_ready, 1)
            pipelined(dve, E1, [(weigh, 1), (copy_fT, -1), (keep_gates, -1)], c)
            end_stage(dve, 6)

        @block.tensor
        def _(pe):
            pe.wait_ge(consts, 14)
            pe.wait_ge(w0_in, 128)
            for which, (wT, bank) in enumerate(((WselfT, banks[6]), (WnbT, banks[7]))):
                for dc in range(KC):
                    for mc in range(KC):
                        mm = pe.matmul(bank[:, cols(dc, D)], wT[:, mc, cols(dc, P)], Wc[which][:, mc, :],
                                       start=(mc == 0), stop=(mc == KC - 1))
                mm.then_inc(fold_done, 1)
            for which in range(2):
                for mc in range(KC):
                    mm = pe.matmul(banks[5][0:1, 0:D], bsn[:, which, mc:mc + 1], Wc[which][:, mc, :],
                                   start=(which + mc == 0), stop=(which + mc == KC))
            mm.then_inc(fold_done, 1)
            pe.wait_ge(fold_copied, 3)
            pe.matmul(banks[5][:, 0:D], ones[0:1, :], BF[:, :], start=True, stop=True).then_inc(bias_done, 1)
            pe.wait_ge(xs_ready, 1)

            def aggregate(k, par, first, half):
                if half == 0:
                    if not first:
                        pe.wait_ge(sa_ready, k - 1)
                pe.wait_ge(mask_ready, 2 * k + 1 + half)
                for j in range(half * HT, (half + 1) * HT):
                    halves = ((D + 1, HI), (D, LO)) if j == 0 else ((D, LO), (D + 1, HI))
                    for n, (w, o) in enumerate(halves):
                        mm = pe.matmul(banks[par][:, 0:w], mt[par][:, j, :], XS[:, j, o:o + w],
                                       start=(j == 0 and n == 0), stop=(j == T - 1 and n == 1), skip_group_check=True)
                if half == 1:
                    mm.then_inc(agg_done, 1)

            def turn0(k, par, first):
                pe.wait_ge(sa_ready, k + 1)
                if not (isinstance(k, int) and k < 1):
                    pe.wait_ge(saT_copied, k)
                for j in range(2 * KC):
                    mm = pe.transpose(banks[2][:, cols(j, P)], sa[par][:, j, :], ident[:, :])
                mm.then_inc(saT_done, 1)

            def combine(k, par, first):
                pe.wait_ge(saT_copied, k + 1)
                if not (isinstance(k, int) and k < 1):
                    pe.wait_ge(comb_read, k)
                for j in range(2 * KC):
                    mm = pe.matmul(banks[3][:, 0:D], saT[par][:, j, :], WF[:, j, :], start=(j == 0),
                                   stop=(j == 2 * KC - 1))
                mm.then_inc(comb_done, 1)

            def turn1(k, par, first):
                pe.wait_ge(xn_ready, k + 1)
                if not (isinstance(k, int) and k < 1):
                    pe.wait_ge(x1T_copied, k)
                for ch in range(KC):
                    mm = pe.transpose(banks[4][:, cols(ch, P)], xnb[par][:, ch, :], ident[:, :])
                mm.then_inc(x1T_done, 1)

            def logits(k, par, first):
                pe.wait_ge(x1T_copied, k + 1)
                if not (isinstance(k, int) and k < 1):
                    pe.wait_ge(lg_copied, 2 * k - 1)
                for ch in range(KC):
                    pe.matmul(banks[5][:, 0:E0], xTb[par][:, ch, :], rw[:, ch, :], start=(ch == 0), stop=False)
                pe.matmul(banks[5][:, 0:E0], ones[0:1, :], rb[:, :], start=False, stop=True).then_inc(lg_done, 1)

            def count(k, par, first):
                pe.wait_ge(oh_made, k + 1)
                start = isinstance(k, int) and k == 0
                if not start:
                    pe.wait_ge(pos_read, k)
                    for j in range(K0):
                        pe.matmul(banks[6][:, 0:E0], notbefore[:, :], OH[1 - par][:, j, :], start=False, stop=False,
                                  skip_group_check=True)
                for j in range(K0):
                    mm = pe.matmul(banks[6][:, 0:E0], before[:, :], OH[par][:, j, :], start=(start and j == 0),
                                   stop=(j == K0 - 1), skip_group_check=True)
                mm.then_inc(pos_done, 1)
            pipelined(pe, T, [(lambda k, par, first: aggregate(k, par, first, 0), 0), (turn0, 1), (logits, 3),
                              (lambda k, par, first: aggregate(k, par, first, 1), 0), (combine, 1), (count, 4),
                              (turn1, 2)])
            end_stage(pe, 1)

            def turn_tiles(src, bank):
                for ch in range(KC):
                    for u in range(GT):
                        mm = pe.transpose(banks[bank][:, cols(ch * GT + u, P)], src[:, u * KC + ch, :], ident[:, :])
                return mm

            def turn_group(src, ready, done, read, k, par, first):
                pe.wait_ge(ready, k + 1)
                if not first:
                    pe.wait_ge(read, k - 1)
                turn_tiles(src[par], par).then_inc(done, 1)

            def turn_expert(k, par, first, parts):
                if parts[0] == 0:
                    pe.wait_ge(exin[par], (k - par) * (8 * B0) + 16 * B0)
                for j in parts:
                    nb = min(2, B0 - 2 * j)
                    if j == 2:
                        pe.wait_ge(exT_copied, 2 * k + 1)
                    elif not (isinstance(k, int) and k == 0):
                        pe.wait_ge((exT_mid, exT_copied)[j], k if j == 0 else 2 * k)
                    for ch in range(KC):
                        for u in range(nb):
                            mm = pe.transpose(banks[(par + j) % 2][:, cols(ch * nb + u, P)],
                                              ex_in[par][:, 2 * j + u, cols(ch, P)], ident[:, :])
                    mm.then_inc(exT_done, 1)

            def up_expert(k, par, first):
                pe.wait_ge(exw[par], (k - par) * 8 + 16)
                pe.wait_ge(exT_copied, 2 * k + 2)
                pe.wait_ge(exT_mid, k + 1)
                for h in range(2):
                    if not (isinstance(k, int) and k < 1):
                        pe.wait_ge(exac_ready, 2 * k - 1 + h)
                    for gu in range(2):
                        for ch in range(KC):
                            mm = pe.matmul(banks[2 + 2 * h + gu][:, 0:S0 // 2], ex_w[par][:, gu * KC + ch, :],
                                           ex_T[par][:, ch, cols(h, S0 // 2)], start=(ch == 0), stop=(ch == KC - 1))
                    mm.then_inc(exgu_done, 1)

            def down_expert(k, par, first):
                pe.wait_ge(exwd[par], (k - par) * 8 + 16)
                pe.wait_ge(exac_ready, 2 * k + 2)
                for j in range(3):
                    if not (isinstance(k, int) and k == 0 and j < 2):
                        pe.wait_ge(exy_copied, 3 * k + j - 1)
                    for u in range(min(2, B0 - 2 * j)):
                        mm = pe.matmul(banks[6 + (par + j) % 2][:, cols(u, D)],
                                       ex_ac[par][:, cols(2 * j + u, P)], ex_wd[par][:, :],
                                       start=True, stop=True)
                    mm.then_inc(exy_done, 1)
            pipelined(pe, E0, [(lambda k, par, first: turn_expert(k, par, first, (0, 1)), -1), (up_expert, 0),
                               (lambda k, par, first: turn_expert(k, par, first, (2,)), -1), (down_expert, 1)])
            end_stage(pe, 2)

            pe.wait_ge(w2_in, 48)
            for dc in range(KC):
                for oc in range(KC):
                    mm = pe.matmul(banks[7][:, cols(dc, 2)], Wn[:, oc, cols(dc, P)], a12[:, oc, :],
                                   start=(oc == 0), stop=(oc == KC - 1))
            mm.then_inc(va_done, 1)
            pe.wait_ge(sq_sum, 1)
            pe.matmul(banks[5][:, 0:1], ones[:, :], SC[:, 6:7], start=True, stop=True).then_inc(bound_done, 1)
            pe.wait_ge(bound_ready, 1)
            pe.wait_ge(w1_in, 32)

            def turn_shared(k, par, first):
                pe.wait_ge(xg_in[par], (k - par) * 8 + 16)
                if not (isinstance(k, int) and k < 1):
                    pe.wait_ge(xT_copied, k)
                for ch in range(KC):
                    mm = pe.transpose(banks[0][:, cols(ch, P)], xg[par][:, ch, :], ident[:, :])
                mm.then_inc(xT_done, 1)

            def shared(k, par, first):
                pe.wait_ge(xT_copied, k + 1)
                for s in range(SH):
                    if not (isinstance(k, int) and k < 1):
                        pe.wait_ge(acs_ready, 2 * k - 1 + s)
                    for gu in range(2):
                        for ch in range(KC):
                            mm = pe.matmul(banks[2 + s][:, cols(gu, P)], sgu[:, s, gu, ch, :], xT[par][:, ch, :],
                                           start=(ch == 0), stop=(ch == KC - 1), skip_group_check=True)
                    mm.then_inc(hgu_done, 1)

            def sum_up(k, par, first):
                pe.wait_ge(acs_ready, 2 * k + 2)
                if not first:
                    pe.wait_ge(sd_read, k - 1)
                for s in range(SH):
                    pe.matmul(banks[4 + par][:, 0:D], acs[par][:, s, :], sdn[:, s, :], start=(s == 0), stop=False)
                pe.wait_ge(dgc_ready, k + 1)
                pe.wait_ge(y6_in[par], (k - par) * (8 * K0) + 16 * K0)
                for j in range(K0):
                    mm = pe.matmul(banks[4 + par][:, 0:D], dgc[par][:, j, :], Y6[par][:, j, :], start=False,
                                   stop=(j == K0 - 1))
                mm.then_inc(sd_done, 1)

            def turn2(k, par, first):
                pe.wait_ge(gx_ready, k + 1)
                if not (isinstance(k, int) and k < 1):
                    pe.wait_ge(gxT_copied, k)
                for ch in range(KC):
                    mm = pe.transpose(banks[1][:, cols(ch, P)], gx[par][:, ch, :], ident[:, :])
                mm.then_inc(gxT_done, 1)

            def features(k, par, first):
                pe.wait_ge(gxT_copied, k + 1)
                if not first:
                    pe.wait_ge(h_copied, 2 * k - 2)
                for ch in range(KC):
                    mm = pe.matmul(banks[6 + par][:, 0:D + 2], gxT[par][:, ch, :], W2[:, ch, :],
                                   start=(ch == 0), stop=(ch == KC - 1))
                mm.then_inc(h_done, 1)
            pipelined(pe, T, [(turn_shared, -1), (shared, 0), (features, 3), (sum_up, 1), (turn2, 2)])
            end_stage(pe, 3)

            for j, (o, w) in enumerate(ABLOCKS):
                if j >= 4:
                    pe.wait_ge(accT_read, j - 3)
                for q in range(w // P):
                    mm = pe.transpose(banks[4 + j % 4][:, cols(q, P)], acc[:, o + q * P:o + (q + 1) * P], ident[:, :])
                mm.then_inc(accT_done, 1)

            def rows(b):
                o, w = ABLOCKS[b]
                for i in range(2):
                    pe.wait_ge(dgn_ready, 2 * b + i + 1)
                    pe.matmul(banks[4 * (b % 2) + i][:, 0:w], ones[:, :],
                              dgn[i][:, 0:w // P, :].rearrange("p q t -> p (q t)"), start=True, stop=True
                              ).then_inc(pb_done, 1)
            rows(0)
            for bi, (o, w) in enumerate(ABLOCKS):
                pe.wait_ge(pb_copied, 2 * bi + 2)
                if bi == 1:
                    pe.wait_ge(hs_read, 1)

                def attend(k, par, first):
                    pe.wait_ge(atp_ready, k + T * bi + 1)
                    for q in range(w // P):
                        mm = pe.matmul(banks[4 * (bi % 2) + q][:, 0:D + 1], atp[par][:, cols(q, P)], H[:, k, 0:D + 1],
                                       start=(isinstance(k, int) and k == 0), stop=(isinstance(k, int) and k == T - 1),
                                       skip_group_check=True)
                    mm.then_inc(atp_used, 1)

                def rows_beside(k, par, first):
                    if isinstance(k, int) and k == PEEL + 1:
                        if bi + 1 < len(ABLOCKS):
                            if bi:
                                pe.wait_ge(blk_read, bi)
                            rows(bi + 1)
                        if bi == 0:
                            pe.wait_ge(ha_ready, 1)
                            pe.matmul(banks[7][:, 0:D + 2], ones[:, :], HA[:, :], start=True, stop=True
                                      ).then_inc(hs_done, 1)
                pipelined(pe, T, [(attend, 0), (rows_beside, 0)], peel=PEEL)
                pe.wait_ge(atp_used, T * (bi + 1))
                pe.drain().then_inc(blk_done, 1)
            end_stage(pe, 4)

            pe.wait_ge(w3_in, 48)

            def turn3(k, par, first):
                turn_group(fxg, fxg_ready, fxT_done, fxT_copied, k, par, first)

            def gates(k, par, first):
                pe.wait_ge(fxT_copied, k + 1)
                if not first:
                    pe.wait_ge(fl_read, k - 1)
                for u in range(GT):
                    for ch in range(KC):
                        mm = pe.matmul(banks[2 + par][:, cols(u, E1)], fxT[par][:, ch, cols(u, P)], gw[:, ch, :],
                                       start=(ch == 0), stop=(ch == KC - 1), skip_group_check=True)
                mm.then_inc(fl_done, 1)
            pipelined(pe, G, [(turn3, -1), (gates, 0)])
            with pe.Fori(0, (TOP_BIT + 1) // 2 // ROUNDS) as i:
                for n in range(ROUNDS):
                    for t in range(T):
                        if t % HT == 0:
                            pe.wait_ge(cmp_ready, i * (2 * ROUNDS) + (2 * n + t // HT + 1))
                        mm = pe.matmul(banks[4][:, 0:3 * E1], ones16[:, :],
                                       cmp3[:, t, :, :].rearrange("p j e -> p (j e)"),
                                       start=(t == 0), stop=(t == T - 1))
                    mm.then_inc(cnt_done, 1)

            def prefix(bank):
                pe.matmul(bank[:, 0:E1], before[:, :], S16[:, 0, :], start=True, stop=True, skip_group_check=True)
                pe.matmul(bank[:, E1:T * E1], before[:, :], S16[:, 1:T, :].rearrange("p t e -> p (t e)"),
                          start=True, stop=False, skip_group_check=True)
                for t in range(T - 2, -1, -1):
                    mm = pe.matmul(bank[:, (t + 1) * E1:T * E1].rearrange("p (t e) -> p t e", e=E1), ones16[:, :],
                                   bc(S16[:, t, :], [P, T - 1 - t, E1], 1), start=False, stop=(t == 0),
                                   skip_group_check=True)
                return mm
            pe.wait_ge(sel1_ready, 1)
            for t in range(T):
                pe.matmul(banks[7][:, 0:E1], ones16[:, :], A16[:, t, :], start=(t == 0), stop=(t == T - 1))
            prefix(banks[5]).then_inc(sel1_done, 1)
            pe.wait_ge(sel1_ready, 2)
            prefix(banks[6]).then_inc(sel1_done, 1)

            def place(t, par, first):
                pe.wait_ge(oh_ready, t + 1)
                pe.wait_ge(ohp_ready, t + 1)
                for e in range(E1):
                    mm = pe.matmul(banks[4][:, cols(e, 2 * B1)], oh1[par][:, e, :],
                                   R8[:, t, e, :, :].rearrange("p b n -> p (b n)"),
                                   start=(isinstance(t, int) and t == 0 and e == 0), stop=False,
                                   skip_group_check=True)
                mm.then_inc(oh_used, 1)
            pipelined(pe, T, [(place, 0)])
            pe.drain().then_inc(lt_done, 1)
            end_stage(pe, 5)

            pe.wait_ge(w3_in, 48)

            def turn_rows(k, par, first):
                pe.wait_ge(fx_in[par], (k - par) * (8 * B1) + 16 * B1)
                for j in range(2):
                    if not (isinstance(k, int) and k < 1):
                        pe.wait_ge(fT_read, 2 * k + j - 1)
                    for ch in range(KC):
                        for u in range(2):
                            mm = pe.transpose(banks[j][:, cols(ch * 2 + u, P)], fx[par][:, 2 * j + u, cols(ch, P)],
                                              ident[:, :])
                    mm.then_inc(fT_done, 1)

            def hidden(k, par, first):
                pe.wait_ge(fw_in[par], (k - par) * 8 + 16)
                pe.wait_ge(fT_read, 2 * k + 2)
                for h in range(KC):
                    if not (isinstance(k, int) and k < 1):
                        pe.wait_ge(fh_ready, 2 * k - 1 + h)
                    for ch in range(KC):
                        mm = pe.matmul(banks[2 + h][:, :], w12[par][:, ch, cols(h, P)], fT[par][:, ch, :],
                                       start=(ch == 0), stop=(ch == KC - 1))
                    mm.then_inc(fh_done, 1)

            def outputs(k, par, first):
                pe.wait_ge(fh_ready, 2 * k + 2)
                if not first:
                    pe.wait_ge(fy_ready, k - 1)
                pe.wait_ge(fv_in[par], (k - par) * 8 + 16)
                for b in range(B1):
                    for h in range(KC):
                        mm = pe.matmul(banks[4 + 2 * par + b // 2][:, cols(b % 2, D)], fh[par][:, h, cols(b, P)],
                                       w12[par][:, KC + h, :], start=(h == 0), stop=(h == KC - 1),
                                       skip_group_check=True)
                    if b % 2:
                        mm.then_inc(fy_done, 1)
            pipelined(pe, E1, [(outputs, 1), (hidden, 0), (turn_rows, -1)])
            end_stage(pe, 6)


def kernel(**inputs):
    import numpy as np
    import concourse.bacc as bacc
    from concourse.bass_utils import run_bass_kernel_spmd

    def arr(name):
        return np.asarray(inputs[name])

    def kmaj(w):
        return w.reshape(-1, P, w.shape[1]).transpose(1, 0, 2)

    g0, f0, g1, f1 = "L0_gnn_", "L0_ffn_", "L1_gnn_", "L1_ffn_"
    x = np.pad(arr("x"), ((0, NP - N), (0, 0)))
    adj = np.pad(arr("adj"), ((0, NP - N), (0, NP - N)))
    gate, up, down = (arr(f0 + n).transpose(0, 2, 1) for n in ("w_gate", "w_up", "w_down"))
    sgate, sup, sdown = (arr(f0 + n).transpose(0, 2, 1) for n in ("shared_w_gate", "shared_w_up", "shared_w_down"))

    def two(w):
        return w.reshape(w.shape[0], -1, P, w.shape[2]).transpose(0, 2, 1, 3)

    arrays = {
        "x": x.reshape(T, P, D).transpose(1, 0, 2),
        "adj": adj.reshape(T, P, T, P).transpose(0, 3, 2, 1),
        "W_self_T": kmaj(arr(g0 + "W_self").T),
        "W_nb_T": kmaj(arr(g0 + "W_nb").T),
        "W_comb": kmaj(arr(g0 + "W_comb")),
        "b_self_nb": np.stack([arr(g0 + "b_self"), arr(g0 + "b_nb")]).reshape(2, KC, P).transpose(2, 0, 1),
        "b_comb": arr(g0 + "b_comb").reshape(1, D),
        "router_w": kmaj(arr(f0 + "router_w").T),
        "router_b": arr(f0 + "bias").reshape(1, E0),
        "shared_gate_up": np.stack([two(sgate), two(sup)], 1).transpose(2, 0, 1, 3, 4),
        "shared_down": sdown.transpose(1, 0, 2),
        "gate_up0": np.concatenate([two(gate), two(up)], 2),
        "down0": down,
        "W_T": kmaj(arr(g1 + "W").T),
        "W": kmaj(arr(g1 + "W")),
        "a12": kmaj(np.stack([arr(g1 + "a1"), arr(g1 + "a2")], 1)),
        "gate_w": kmaj(arr(f1 + "gate_weight")),
        "experts1": np.concatenate([two(arr(f1 + "w1")), two(arr(f1 + "w2"))], 2),
        "b1": arr(f1 + "b1").reshape(E1, KC, P).transpose(2, 0, 1),
        "b2": arr(f1 + "b2").reshape(1, E1, D),
    }
    nc = bacc.Bacc("TRN2", target_bir_lowering=False, num_devices=1)
    feeds, aps = {}, {}
    for name, a in arrays.items():
        a = np.ascontiguousarray(a)
        feeds[f"in_{name}"] = a
        aps[name] = nc.dram_tensor(f"in_{name}", a.shape, mybir.dt.from_np(a.dtype), kind="ExternalInput").ap()
    out = nc.dram_tensor("out", (N, D), F32, kind="ExternalOutput").ap()
    ids = nc.dram_tensor("ids", (E0 * S0, 1), U32, kind="Internal").ap()
    nbuf = nc.dram_tensor("nbuf", (NP, D), F32, kind="Internal").ap()
    ybuf = nc.dram_tensor("ybuf", (E0 * S0 + 1, D), F32, kind="Internal").ap()
    rbuf = nc.dram_tensor("rbuf", (NP, XW), F32, kind="Internal").ap()
    build(nc, aps, out, ids, nbuf, ybuf, rbuf)
    return run_bass_kernel_spmd(nc, [feeds], core_ids=[0]).results[0]["out"]
```
